# Optimizing a Trainium2 kernel written in Bass

```python
import numpy as np
import jax
import jax.numpy as jnp

def _softmax(x, axis=-1):
    return jax.nn.softmax(x, axis=axis)

def _gelu(x):
    return jax.nn.gelu(x, approximate=True)

def _silu(x):
    return jax.nn.silu(x)

def _sigmoid(x):
    return jax.nn.sigmoid(x)

def _layernorm(x, axis=-1, eps=1e-05):
    m = jnp.mean(x, axis=axis, keepdims=True)
    v = jnp.var(x, axis=axis, keepdims=True)
    return (x - m) / jnp.sqrt(v + eps)

def _scatter_add(tgt, idx, src, axis=0):
    return tgt.at[idx].add(src)

def _segment_sum(src, seg, n):
    return jax.ops.segment_sum(src, seg, n)
kernel_name = 'mk_gnn_resnorm_d4_gnn_r8_439c59'

def setup_inputs(seed: int=0):
    np.random.seed(seed)
    _w = jnp.asarray

    def _rec_inputs():
        import jax
        import jax.numpy as jnp
        _gk = jax.random.key(seed)
        x = -0.0009044 + 1 * jax.random.normal(jax.random.fold_in(_gk, 1), (12500, 32), jnp.float32)
        src = jax.random.randint(jax.random.fold_in(_gk, 2), (400000,), 0, 12500, jnp.int32)
        dst = jnp.minimum((12500 * jax.random.uniform(jax.random.fold_in(_gk, 3), (400000,)) ** 2.0).astype(jnp.int32), 99999)
        _o = jnp.argsort(dst, stable=True)
        src = src[_o]
        dst = dst[_o]
        edge_attr_3 = 0.000844983 + 0.999762 * jax.random.normal(jax.random.fold_in(_gk, 11), (400000, 3), jnp.float32)
        edge_weight = jax.random.uniform(jax.random.fold_in(_gk, 13), (400000,), jnp.float32, 0.0, 1)
        node_vec1 = jax.random.uniform(jax.random.fold_in(_gk, 14), (12500, 1), jnp.float32, 0.0, 1)
        return (x, src, dst, edge_attr_3, edge_weight, node_vec1)
    x, src, dst, edge_attr_3, edge_weight, node_vec1 = _rec_inputs()

    def _L0_gnn_setup():
        import jax, jax.numpy as jnp
        import numpy as np
        N_NODES = 6250
        DEG = 16
        N_HEAD = 4
        F_IN = 32
        F_OUT = 32
        key = jax.random.key(seed)
        k_h, k_w, k_fw, k_fb = jax.random.split(key, 4)
        h = jax.random.normal(k_h, (N_NODES, F_IN), dtype=jnp.float32)
        src = jnp.repeat(jnp.arange(N_NODES, dtype=jnp.int64), DEG)
        offs = (jnp.arange(DEG, dtype=jnp.int64) + 1) * 97
        dst = (src.reshape(N_NODES, DEG) + offs[None, :]).reshape(-1) % N_NODES
        edge_index = jnp.stack([src, dst], axis=0)
        gain = 1.414
        bound_w = gain * np.sqrt(6.0 / (F_IN + F_OUT))
        w = jax.random.uniform(k_w, (N_HEAD, F_IN, F_OUT), jnp.float32, -bound_w, bound_w)
        bound_fc = np.sqrt(1.0 / (2 * F_OUT))
        fc_w = jax.random.uniform(k_fw, (1, 2 * F_OUT), jnp.float32, -bound_fc, bound_fc)
        fc_b = jax.random.uniform(k_fb, (1,), jnp.float32, -bound_fc, bound_fc)
        bias = jnp.zeros((F_OUT,), jnp.float32)
        return {'h': h, 'edge_index': edge_index, 'w': w, 'fc_w': fc_w, 'fc_b': fc_b, 'bias': bias}
    _L0_gnn_all = _L0_gnn_setup()
    _L0_gnn_in = {k: v for k, v in _L0_gnn_all.items() if k in ('w', 'fc_w', 'fc_b', 'bias')}
    del _L0_gnn_all

    def _L1_gnn_setup():
        import jax, jax.numpy as jnp
        import numpy as np
        N = 12500
        E = 200000
        D_IN = 32
        D_OUT = 32
        key = jax.random.key(seed)
        k0, k1, k2, k3 = jax.random.split(key, 4)
        x = jax.random.normal(k0, (N, D_IN), dtype=jnp.float32)
        mask = jax.random.randint(k1, (N, 1), 0, 2).astype(jnp.float32)
        edge_index = jax.random.randint(k2, (2, E), 0, N, dtype=jnp.int32)
        W = jax.random.normal(k3, (D_OUT, D_IN), dtype=jnp.float32) / np.sqrt(D_IN)
        b = jnp.zeros((D_OUT,), dtype=jnp.float32)
        return {'x': x, 'mask': mask, 'W': W, 'b': b, 'edge_index': edge_index}
    _L1_gnn_all = _L1_gnn_setup()
    _L1_gnn_in = {k: v for k, v in _L1_gnn_all.items() if k in ('W', 'b')}
    del _L1_gnn_all

    def _L2_gnn_setup():
        import jax, jax.numpy as jnp
        import numpy as np
        from math import factorial, pi, sqrt
        MUL = 8
        RS = [(MUL, 0), (MUL, 1)]
        N_NODES = 2500
        N_EDGES = 80000
        FEAT_DIM = sum((m * (2 * l + 1) for m, l in RS))
        R_DIM = sum((mo * mi * (2 * min(lo, li) + 1) for mo, lo in RS for mi, li in RS))
        HIDDEN = 64

        def _cg(j1, j2, j3, m1, m2, m3):
            if m1 + m2 != m3:
                return 0.0
            f = factorial
            pre = sqrt((2 * j3 + 1) * f(j3 + j1 - j2) * f(j3 - j1 + j2) * f(j1 + j2 - j3) / f(j1 + j2 + j3 + 1))
            pre *= sqrt(f(j3 + m3) * f(j3 - m3) * f(j1 - m1) * f(j1 + m1) * f(j2 - m2) * f(j2 + m2))
            kmin = max(0, j2 - j3 - m1, j1 - j3 + m2)
            kmax = min(j1 + j2 - j3, j1 - m1, j2 + m2)
            s = 0.0
            for k in range(kmin, kmax + 1):
                s += (-1) ** k / (f(k) * f(j1 + j2 - j3 - k) * f(j1 - m1 - k) * f(j2 + m2 - k) * f(j3 - j2 + m1 + k) * f(j3 - j1 - m2 + k))
            return pre * s

        def _w3j_complex(l1, l2, l3):
            w = np.zeros((2 * l1 + 1, 2 * l2 + 1, 2 * l3 + 1))
            for m1 in range(-l1, l1 + 1):
                for m2 in range(-l2, l2 + 1):
                    m3 = -(m1 + m2)
                    if abs(m3) <= l3:
                        w[m1 + l1, m2 + l2, m3 + l3] = (-1) ** (l1 - l2 - m3) / sqrt(2 * l3 + 1) * _cg(l1, l2, l3, m1, m2, -m3)
            return w

        def _A(l):
            A = np.zeros((2 * l + 1, 2 * l + 1), dtype=complex)
            A[l, l] = 1.0
            for m in range(1, l + 1):
                A[l + m, l + m] = (-1) ** m / sqrt(2)
                A[l + m, l - m] = 1.0 / sqrt(2)
                A[l - m, l - m] = 1j / sqrt(2)
                A[l - m, l + m] = -1j * (-1) ** m / sqrt(2)
            return A

        def real_w3j(l1, l2, l3):
            wc = _w3j_complex(l1, l2, l3).astype(complex)
            wr = np.einsum('abc,ma,nb,oc->mno', wc, _A(l1).conj(), _A(l2).conj(), _A(l3).conj())
            i = int(np.argmax(np.abs(wr)))
            ph = wr.flat[i] / abs(wr.flat[i])
            wr = wr / ph
            assert np.abs(wr.imag).max() < 1e-10
            return np.real(wr).astype(np.float32)
        _W3J = {}
        for _mo, _lo in RS:
            for _mi, _li in RS:
                for _lf in range(abs(_lo - _li), _lo + _li + 1):
                    if (_lo, _lf, _li) not in _W3J:
                        _W3J[_lo, _lf, _li] = jnp.asarray(real_w3j(_lo, _lf, _li))
        _NORM = []
        for _mo, _lo in RS:
            _num = sum((mi * (2 * min(_lo, li) + 1) for mi, li in RS))
            _NORM.append(sqrt(4.0 * pi) * sqrt(2.0 * _lo + 1.0) / sqrt(_num))
        _F_OFFS = [0] + list(np.cumsum([mi * (2 * li + 1) for mi, li in RS]))

        def spherical_harmonics(rel_vec):
            r = rel_vec / jnp.linalg.norm(rel_vec, axis=-1, keepdims=True)
            x, y, z = (r[:, 0], r[:, 1], r[:, 2])
            y0 = jnp.full_like(x, 0.5 / sqrt(pi))[:, None]
            c1 = sqrt(3.0 / (4.0 * pi))
            y1 = c1 * jnp.stack([y, z, x], axis=-1)
            c2a = 0.5 * sqrt(15.0 / pi)
            c2b = 0.25 * sqrt(5.0 / pi)
            c2c = 0.25 * sqrt(15.0 / pi)
            y2 = jnp.stack([c2a * x * y, c2a * y * z, c2b * (3.0 * z * z - 1.0), c2a * x * z, c2c * (x * x - y * y)], axis=-1)
            return jnp.concatenate([y0, y1, y2], axis=-1)
        key = jax.random.key(seed)
        ks = jax.random.split(key, 6)
        features = jax.random.normal(ks[0], (N_NODES, FEAT_DIM), dtype=jnp.float32)
        abs_distances = jax.random.uniform(ks[1], (N_EDGES,), dtype=jnp.float32, minval=0.1, maxval=1.0)
        rel_vec = jax.random.normal(ks[2], (N_EDGES, 3), dtype=jnp.float32)
        edge_index = jax.random.randint(ks[3], (2, N_EDGES), 0, N_NODES, dtype=jnp.int32)
        w1 = jax.random.normal(ks[4], (1, HIDDEN), dtype=jnp.float32)
        b1 = jnp.zeros((HIDDEN,), jnp.float32)
        w2 = jax.random.normal(ks[5], (HIDDEN, R_DIM), dtype=jnp.float32) / sqrt(HIDDEN)
        b2 = jnp.zeros((R_DIM,), jnp.float32)
        return {'features': features, 'abs_distances': abs_distances, 'rel_vec': rel_vec, 'edge_index': edge_index, 'w1': w1, 'b1': b1, 'w2': w2, 'b2': b2}
    _L2_gnn_all = _L2_gnn_setup()
    _L2_gnn_in = {k: v for k, v in _L2_gnn_all.items() if k in ('w1', 'b1', 'w2', 'b2')}
    del _L2_gnn_all

    def _L3_gnn_setup():
        import jax, jax.numpy as jnp
        import numpy as np
        N_NODES = 12500
        N_EDGES = 200000
        EMB = 32
        HID = 64

        def gcn_conv(x, W, b, row, col, n_nodes):
            xw = x @ W
            ones = jnp.ones(row.shape[0], dtype=x.dtype)
            deg = jax.ops.segment_sum(ones, col, num_segments=n_nodes)
            dinv = jnp.where(deg > 0, jax.lax.rsqrt(deg), 0.0)
            norm = dinv[row] * dinv[col]
            msgs = norm[:, None] * xw[row]
            out = jax.ops.segment_sum(msgs, col, num_segments=n_nodes)
            return out + b
        key = jax.random.key(seed)
        k1, k2, k3, k4, k5, k6 = jax.random.split(key, 6)
        x = jax.random.normal(k1, (N_NODES, EMB), dtype=jnp.float32)
        edge_index = jax.random.randint(k2, (2, N_EDGES), 0, N_NODES, dtype=jnp.int64)
        W1 = jax.random.normal(k3, (EMB, HID), dtype=jnp.float32) / np.sqrt(EMB)
        b1 = jnp.zeros((HID,), dtype=jnp.float32)
        W2 = jax.random.normal(k4, (HID, EMB), dtype=jnp.float32) / np.sqrt(HID)
        b2 = jnp.zeros((EMB,), dtype=jnp.float32)
        return {'x': x, 'edge_index': edge_index, 'W1': W1, 'b1': b1, 'W2': W2, 'b2': b2}
    _L3_gnn_all = _L3_gnn_setup()
    _L3_gnn_in = {k: v for k, v in _L3_gnn_all.items() if k in ('W1', 'b1', 'W2', 'b2')}
    del _L3_gnn_all
    return {'x': x, 'src': src, 'dst': dst, 'edge_attr_3': edge_attr_3, 'edge_weight': edge_weight, 'node_vec1': node_vec1, 'L0_gnn_w': _L0_gnn_in['w'], 'L0_gnn_fc_w': _L0_gnn_in['fc_w'], 'L0_gnn_fc_b': _L0_gnn_in['fc_b'], 'L0_gnn_bias': _L0_gnn_in['bias'], 'L1_gnn_W': _L1_gnn_in['W'], 'L1_gnn_b': _L1_gnn_in['b'], 'L2_gnn_w1': _L2_gnn_in['w1'], 'L2_gnn_b1': _L2_gnn_in['b1'], 'L2_gnn_w2': _L2_gnn_in['w2'], 'L2_gnn_b2': _L2_gnn_in['b2'], 'L3_gnn_W1': _L3_gnn_in['W1'], 'L3_gnn_b1': _L3_gnn_in['b1'], 'L3_gnn_W2': _L3_gnn_in['W2'], 'L3_gnn_b2': _L3_gnn_in['b2']}

def reference(x, src, dst, edge_attr_3, edge_weight, node_vec1, L0_gnn_w, L0_gnn_fc_w, L0_gnn_fc_b, L0_gnn_bias, L1_gnn_W, L1_gnn_b, L2_gnn_w1, L2_gnn_b1, L2_gnn_w2, L2_gnn_b2, L3_gnn_W1, L3_gnn_b1, L3_gnn_W2, L3_gnn_b2):
    import jax
    import jax.numpy as jnp

    def _L0_gnn_ref(h, edge_index, w, fc_w, fc_b, bias):
        import jax, jax.numpy as jnp
        import numpy as np
        N_NODES = 6250
        DEG = 16
        N_HEAD = 4
        F_IN = 32
        F_OUT = 32
        n_head, f_in, f_out = w.shape
        n = h.shape[0]
        src, dst = (edge_index[0], edge_index[1])
        hp = jnp.einsum('nf,hfo->hno', h, w)
        w_src = fc_w[0, :f_out]
        w_dst = fc_w[0, f_out:]
        a_src = jnp.einsum('hnf,f->hn', hp, w_src)
        a_dst = jnp.einsum('hnf,f->hn', hp, w_dst)
        e = a_src[:, src] + a_dst[:, dst] + fc_b[0]
        e = jax.nn.leaky_relu(e, negative_slope=0.2)
        seg_max = jax.ops.segment_max(e.T, src, num_segments=n)
        e = jnp.exp(e - seg_max.T[:, src])
        seg_sum = jax.ops.segment_sum(e.T, src, num_segments=n)
        att = e / seg_sum.T[:, src]
        msg = att[:, :, None] * hp[:, dst, :]
        agg = jax.vmap(lambda m: jax.ops.segment_sum(m, src, num_segments=n))(msg)
        out = agg.mean(axis=0) + bias
        return out

    def _L1_gnn_ref(x, mask, W, b, edge_index):
        import jax, jax.numpy as jnp
        import numpy as np
        N = 12500
        E = 200000
        D_IN = 32
        D_OUT = 32
        row, col = (edge_index[0], edge_index[1])
        n = x.shape[0]
        x = jnp.nan_to_num(x)
        deg = jax.ops.segment_sum(jnp.ones(row.shape[0], x.dtype), row, num_segments=n)
        dis = jnp.where(deg > 0, jax.lax.rsqrt(deg), 0.0)
        w = dis[row] * dis[col]

        def spmm(v):
            return jax.ops.segment_sum(w[:, None] * v[col], row, num_segments=n)
        numerator = spmm(jnp.ones_like(x)) * spmm(mask * x)
        denominator = spmm(mask)
        den_safe = jnp.where(denominator == 0, 1.0, denominator)
        ratio = jnp.where(denominator == 0, 0.0, numerator / den_safe)
        return ratio @ W.T + b

    def _L2_gnn_ref(features, abs_distances, rel_vec, edge_index, w1, b1, w2, b2):
        import jax, jax.numpy as jnp
        import numpy as np
        from math import factorial, pi, sqrt
        MUL = 8
        RS = [(MUL, 0), (MUL, 1)]
        N_NODES = 2500
        N_EDGES = 80000
        FEAT_DIM = sum((m * (2 * l + 1) for m, l in RS))
        R_DIM = sum((mo * mi * (2 * min(lo, li) + 1) for mo, lo in RS for mi, li in RS))
        HIDDEN = 64

        def _cg(j1, j2, j3, m1, m2, m3):
            if m1 + m2 != m3:
                return 0.0
            f = factorial
            pre = sqrt((2 * j3 + 1) * f(j3 + j1 - j2) * f(j3 - j1 + j2) * f(j1 + j2 - j3) / f(j1 + j2 + j3 + 1))
            pre *= sqrt(f(j3 + m3) * f(j3 - m3) * f(j1 - m1) * f(j1 + m1) * f(j2 - m2) * f(j2 + m2))
            kmin = max(0, j2 - j3 - m1, j1 - j3 + m2)
            kmax = min(j1 + j2 - j3, j1 - m1, j2 + m2)
            s = 0.0
            for k in range(kmin, kmax + 1):
                s += (-1) ** k / (f(k) * f(j1 + j2 - j3 - k) * f(j1 - m1 - k) * f(j2 + m2 - k) * f(j3 - j2 + m1 + k) * f(j3 - j1 - m2 + k))
            return pre * s

        def _w3j_complex(l1, l2, l3):
            w = np.zeros((2 * l1 + 1, 2 * l2 + 1, 2 * l3 + 1))
            for m1 in range(-l1, l1 + 1):
                for m2 in range(-l2, l2 + 1):
                    m3 = -(m1 + m2)
                    if abs(m3) <= l3:
                        w[m1 + l1, m2 + l2, m3 + l3] = (-1) ** (l1 - l2 - m3) / sqrt(2 * l3 + 1) * _cg(l1, l2, l3, m1, m2, -m3)
            return w

        def _A(l):
            A = np.zeros((2 * l + 1, 2 * l + 1), dtype=complex)
            A[l, l] = 1.0
            for m in range(1, l + 1):
                A[l + m, l + m] = (-1) ** m / sqrt(2)
                A[l + m, l - m] = 1.0 / sqrt(2)
                A[l - m, l - m] = 1j / sqrt(2)
                A[l - m, l + m] = -1j * (-1) ** m / sqrt(2)
            return A

        def real_w3j(l1, l2, l3):
            wc = _w3j_complex(l1, l2, l3).astype(complex)
            wr = np.einsum('abc,ma,nb,oc->mno', wc, _A(l1).conj(), _A(l2).conj(), _A(l3).conj())
            i = int(np.argmax(np.abs(wr)))
            ph = wr.flat[i] / abs(wr.flat[i])
            wr = wr / ph
            assert np.abs(wr.imag).max() < 1e-10
            return np.real(wr).astype(np.float32)
        _W3J = {}
        for _mo, _lo in RS:
            for _mi, _li in RS:
                for _lf in range(abs(_lo - _li), _lo + _li + 1):
                    if (_lo, _lf, _li) not in _W3J:
                        _W3J[_lo, _lf, _li] = jnp.asarray(real_w3j(_lo, _lf, _li))
        _NORM = []
        for _mo, _lo in RS:
            _num = sum((mi * (2 * min(_lo, li) + 1) for mi, li in RS))
            _NORM.append(sqrt(4.0 * pi) * sqrt(2.0 * _lo + 1.0) / sqrt(_num))
        _F_OFFS = [0] + list(np.cumsum([mi * (2 * li + 1) for mi, li in RS]))

        def spherical_harmonics(rel_vec):
            r = rel_vec / jnp.linalg.norm(rel_vec, axis=-1, keepdims=True)
            x, y, z = (r[:, 0], r[:, 1], r[:, 2])
            y0 = jnp.full_like(x, 0.5 / sqrt(pi))[:, None]
            c1 = sqrt(3.0 / (4.0 * pi))
            y1 = c1 * jnp.stack([y, z, x], axis=-1)
            c2a = 0.5 * sqrt(15.0 / pi)
            c2b = 0.25 * sqrt(5.0 / pi)
            c2c = 0.25 * sqrt(15.0 / pi)
            y2 = jnp.stack([c2a * x * y, c2a * y * z, c2b * (3.0 * z * z - 1.0), c2a * x * z, c2c * (x * x - y * y)], axis=-1)
            return jnp.concatenate([y0, y1, y2], axis=-1)
        src, dst = (edge_index[0], edge_index[1])
        R = jax.nn.relu(abs_distances[:, None] @ w1 + b1) @ w2 + b2
        Y = spherical_harmonics(rel_vec)
        Fj = features[src]
        E = Fj.shape[0]
        msg_blocks = []
        r_off = 0
        for i, (mo, lo) in enumerate(RS):
            acc = jnp.zeros((E, mo, 2 * lo + 1), dtype=features.dtype)
            for j, (mi, li) in enumerate(RS):
                n_lf = 2 * min(lo, li) + 1
                sz = mo * mi * n_lf
                Rb = R[:, r_off:r_off + sz].reshape(E, mo, mi, n_lf)
                r_off += sz
                Fb = Fj[:, _F_OFFS[j]:_F_OFFS[j + 1]].reshape(E, mi, 2 * li + 1)
                for k, lf in enumerate(range(abs(lo - li), lo + li + 1)):
                    C = _W3J[lo, lf, li]
                    Yf = Y[:, lf * lf:(lf + 1) * (lf + 1)]
                    acc = acc + _NORM[i] * jnp.einsum('euv,ef,evi,ofi->euo', Rb[..., k], Yf, Fb, C)
            msg_blocks.append(acc.reshape(E, -1))
        msg = jnp.concatenate(msg_blocks, axis=-1)
        out = jnp.zeros((features.shape[0], msg.shape[1]), dtype=features.dtype)
        out = out.at[dst].add(msg)
        return out

    def _L3_gnn_ref(x, edge_index, W1, b1, W2, b2):
        import jax, jax.numpy as jnp
        import numpy as np
        N_NODES = 12500
        N_EDGES = 200000
        EMB = 32
        HID = 64

        def gcn_conv(x, W, b, row, col, n_nodes):
            xw = x @ W
            ones = jnp.ones(row.shape[0], dtype=x.dtype)
            deg = jax.ops.segment_sum(ones, col, num_segments=n_nodes)
            dinv = jnp.where(deg > 0, jax.lax.rsqrt(deg), 0.0)
            norm = dinv[row] * dinv[col]
            msgs = norm[:, None] * xw[row]
            out = jax.ops.segment_sum(msgs, col, num_segments=n_nodes)
            return out + b
        n = x.shape[0]
        loops = jnp.arange(n, dtype=edge_index.dtype)
        row = jnp.concatenate([edge_index[0], loops])
        col = jnp.concatenate([edge_index[1], loops])
        h = jax.nn.relu(gcn_conv(x, W1, b1, row, col, n))
        h = jax.nn.relu(gcn_conv(h, W2, b2, row, col, n))
        return h
    edge_index = jnp.stack([src, dst])
    x = _layernorm(x + _L0_gnn_ref(x, edge_index, L0_gnn_w, L0_gnn_fc_w, L0_gnn_fc_b, L0_gnn_bias), axis=-1)
    x = _layernorm(x + _L1_gnn_ref(x, node_vec1, L1_gnn_W, L1_gnn_b, edge_index), axis=-1)
    x = _layernorm(x + _L2_gnn_ref(x, edge_weight, edge_attr_3, edge_index, L2_gnn_w1, L2_gnn_b1, L2_gnn_w2, L2_gnn_b2), axis=-1)
    x = _layernorm(x + _L3_gnn_ref(x, edge_index, L3_gnn_W1, L3_gnn_b1, L3_gnn_W2, L3_gnn_b2), axis=-1)
    return x

_drawn_inputs = setup_inputs


def setup_inputs(seed=0):
    import zlib

    import numpy as np

    out = dict(_drawn_inputs(seed))
    spreads = {'L0_gnn_bias': (0.0, 0.1),
     'L1_gnn_b': (0.0, 0.1),
     'L2_gnn_b1': (0.0, 0.1),
     'L2_gnn_b2': (0.0, 0.1),
     'L3_gnn_b1': (0.0, 0.1),
     'L3_gnn_b2': (0.0, 0.1)}
    factors = {}
    for name, (base, spread) in spreads.items():
        noise = np.random.default_rng([zlib.crc32(name.encode()), seed]).standard_normal(out[name].shape)
        drawn = base * np.exp(spread * noise) if base else spread * noise
        out[name] = jnp.asarray(drawn.astype(out[name].dtype))
    for name, factor in factors.items():
        out[name] = (out[name] * factor).astype(out[name].dtype)
    return out
```

```python
import concourse.bass as bass
import concourse.mybir as mybir
import numpy as np
from contextlib import ExitStack
from math import factorial, pi, sqrt

F32 = mybir.dt.float32
BF16 = mybir.dt.bfloat16
I32 = mybir.dt.int32
U8 = mybir.dt.uint8
ALU = mybir.AluOpType
ACT = mybir.ActivationFunctionType
AX = mybir.AxisListType

P = 128
N = 12500
F = 32
W = -(-N // P)
NW = W * P
LAST = N - (W - 1) * P
E = 400000
TE = E // P
HEADS = 4
HID = 64
H2 = 64

TILES_PER_GROUP = 2
GROUP = TILES_PER_GROUP * P
SLOTS = 4
GPS = 4
TPS = GPS * TILES_PER_GROUP
MAX_GROUPS = (E + W * (GROUP - 1)) // GROUP
ITERS = -(-MAX_GROUPS // (SLOTS * GPS))
STEPS = ITERS * SLOTS
NG = STEPS * GPS
NT = NG * TILES_PER_GROUP
ROWS = P * NT

RING = 5
RSLOTS = 5
RITERS = TE // (RING * RSLOTS)

PAD_KEY = 1 << 20
KEY_MASK = PAD_KEY | (P - 1)
BIG = float(2.0 ** 100)
FMAX = 3.4028234663852886e38
EPS = 1e-05

C0 = F + 1 + HEADS
CM = HEADS * (F + 1) + 1
C1 = F + 2
C2 = 41
CF = F


def _coupling():
    def cg(j1, j2, j3, m1, m2, m3):
        if m1 + m2 != m3:
            return 0.0
        f = factorial
        pre = sqrt((2 * j3 + 1) * f(j3 + j1 - j2) * f(j3 - j1 + j2) * f(j1 + j2 - j3) / f(j1 + j2 + j3 + 1))
        pre *= sqrt(f(j3 + m3) * f(j3 - m3) * f(j1 - m1) * f(j1 + m1) * f(j2 - m2) * f(j2 + m2))
        s = 0.0
        for k in range(max(0, j2 - j3 - m1, j1 - j3 + m2), min(j1 + j2 - j3, j1 - m1, j2 + m2) + 1):
            s += (-1) ** k / (f(k) * f(j1 + j2 - j3 - k) * f(j1 - m1 - k) * f(j2 + m2 - k)
                              * f(j3 - j2 + m1 + k) * f(j3 - j1 - m2 + k))
        return pre * s

    def basis(l):
        a = np.zeros((2 * l + 1, 2 * l + 1), dtype=complex)
        a[l, l] = 1.0
        for m in range(1, l + 1):
            a[l + m, l + m] = (-1) ** m / sqrt(2)
            a[l + m, l - m] = 1.0 / sqrt(2)
            a[l - m, l - m] = 1j / sqrt(2)
            a[l - m, l + m] = -1j * (-1) ** m / sqrt(2)
        return a

    def w3j(l1, l2, l3):
        w = np.zeros((2 * l1 + 1, 2 * l2 + 1, 2 * l3 + 1))
        for m1 in range(-l1, l1 + 1):
            for m2 in range(-l2, l2 + 1):
                m3 = -(m1 + m2)
                if abs(m3) <= l3:
                    w[m1 + l1, m2 + l2, m3 + l3] = (-1) ** (l1 - l2 - m3) / sqrt(2 * l3 + 1) * cg(l1, l2, l3, m1, m2, -m3)
        wr = np.einsum('abc,ma,nb,oc->mno', w.astype(complex), basis(l1).conj(), basis(l2).conj(), basis(l3).conj())
        i = int(np.argmax(np.abs(wr)))
        return np.real(wr / (wr.flat[i] / abs(wr.flat[i])))

    norm0 = sqrt(4 * pi) / sqrt(8 * 1 + 8 * 1)
    norm1 = sqrt(4 * pi) * sqrt(3.0) / sqrt(8 * 1 + 8 * 3)
    y0 = 0.5 / sqrt(pi)
    c1 = sqrt(3.0 / (4.0 * pi))
    c2b, c2c = 0.25 * sqrt(5.0 / pi), 0.25 * sqrt(15.0 / pi)
    y2 = np.array([0, 0, -c2b, 0, -c2c])
    k2 = 0.5 * float(w3j(1, 2, 1)[0, :, 0] @ y2)
    return {
        "s_f0": norm0 * y0 * float(w3j(0, 0, 0)[0, 0, 0]),
        "s_dot": norm0 * c1 * float(w3j(0, 1, 1)[0, 0, 0]),
        "v_f0": norm1 * c1 * float(w3j(1, 1, 0)[0, 0, 0]),
        "v_same": norm1 * y0 * float(w3j(1, 0, 1)[0, 0, 0]),
        "v_cross": norm1 * c1 * float(w3j(1, 1, 1)[0, 1, 2]),
        "v_quad": norm1 * k2,
    }


def resnorm_gnn_kernel(nc, a, out):
    ctx = ExitStack()
    with ctx:
        def sb(name, shape, dt=F32):
            return ctx.enter_context(nc.sbuf_tensor(name, shape, dt))

        def sem(name):
            return ctx.enter_context(nc.semaphore(name))

        def dram(name, shape):
            return nc.dram_tensor(name, shape, F32, kind="Internal").ap()

        edges_src = dram("edges_src", (E, 2))
        edges_dst = dram("edges_dst", (E, 6))
        rows_src = nc.dram_tensor("rows_src", (E, 1), I32, kind="Internal").ap()
        rows_dst = nc.dram_tensor("rows_dst", (E, 1), I32, kind="Internal").ap()
        by_src = dram("by_src", (ROWS, 2))
        by_dst = dram("by_dst", (ROWS, 6))
        staged = dram("staged", (ROWS, C0))
        tab0 = dram("tab0", (NW, C0))
        tab1 = dram("tab1", (NW, C1))
        tab2 = dram("tab2", (NW, F))
        tab3 = dram("tab3", (NW, F))
        tab4 = dram("tab4", (NW, F))
        by_src_v = by_src.rearrange("(p t) c -> p t c", p=P)
        by_dst_v = by_dst.rearrange("(p t) c -> p t c", p=P)
        staged_v = staged.rearrange("(p t) c -> p t c", p=P)

        x = sb("x", [P, W, F])
        tabx = sb("tabx", [P, W, C0])
        acc = sb("acc", [P, W * CM])
        srcs = sb("srcs", [P, TE], I32)
        dsts = sb("dsts", [P, TE], I32)
        pos = sb("pos", [P, TE])
        hot = sb("hot", [P, TPS, P])
        winb = acc[:, 0:TE]
        eqm = acc[:, TE:TE + (TE + 3) // 4 + 1].bitcast(U8)[:, 0:TE]
        cum = acc[:, 4096:4096 + TE]
        fill = acc[:, 8192:8192 + 416 * 6].rearrange("p (t c) -> p t c", c=6)
        fill2 = hot[:, :, :].rearrange("p t n -> p (t n)")[:, 0:416 * 2].rearrange("p (t c) -> p t c", c=2)
        FILL_T = 416
        assert NT % FILL_T == 0

        iota = sb("iota", [P, P])
        iotaw = iota[:, 0:W]
        iotap = sb("iotap", [P, 1])
        ident = sb("ident", [P, P])
        identb = sb("identb", [P, P], BF16)
        ones = sb("ones", [P, P])
        before = sb("before", [P, P])
        far = sb("far", [P, P], BF16)
        pick = sb("pick", [96, 32, P], BF16)
        hist = sb("hist", [P, W])
        start_ = sb("start_", [P, W])
        ends = sb("ends", [P, W])
        gcnt = sb("gcnt", [P, W], I32)
        endT = sb("endT", [P, 1])
        giota = acc[:, 10752:10752 + NG]
        gge = cum[:, 0:NG]
        CHUNK = TE // 5
        ch_attr = acc[:, 0:3 * CHUNK].rearrange("p (t c) -> p t c", c=3)
        ch_w = acc[:, 1875:1875 + CHUNK]
        ch_len = acc[:, 2500:2500 + CHUNK]
        ch_sq = acc[:, 3125:3125 + CHUNK]
        ch_pay = acc[:, 3750:3750 + 6 * CHUNK].rearrange("p (t c) -> p t c", c=6)
        pair = acc[:, 0:2 * TE].rearrange("p (t c) -> p t c", c=2)
        whb = tabx[:, :, :].rearrange("p w c -> p (w c)")
        win_src = sb("win_src", [1, NG], I32)
        win_dst = sb("win_dst", [1, NG], I32)
        posr = sb("posr", [P, RSLOTS, RING], I32)
        payr = sb("payr", [P, RSLOTS, RING, 6])

        pay = sb("pay", [P, SLOTS, TPS, 6])
        gat = sb("gat", [P, SLOTS, TPS, C0])
        keyi = sb("keyi", [P, TPS], I32)
        keyf = sb("keyf", [P, TPS])
        hotb = hot[:, :, :].rearrange("p t n -> p (t n)").bitcast(BF16)[:, 0:TPS * P].rearrange("p (t n) -> p t n", n=P)
        hotT = sb("hotT", [P, TPS, P], BF16)
        mmax = sb("mmax", [P, W, HEADS])
        asrc = sb("asrc", [P, W, HEADS])
        nodeam = sb("nodeam", [P, W, 2 * HEADS])
        nodesp = sb("nodesp", [P, W, 3, 2 * HEADS], BF16)
        padf = sb("padf", [P, TPS])
        adm = sb("adm", [P, TPS, HEADS])
        adsp = sb("adsp", [P, 3, TPS * HEADS], BF16)
        adT = sb("adT", [96, P], BF16)
        red = sb("red", [P, TPS, C2])
        am = sb("am", [P, TPS, 2 * HEADS])
        logit = sb("logit", [P, TPS, HEADS])
        prob = sb("prob", [P, TPS, HEADS])
        msg = sb("msg", [P, TPS, CM])
        msgf = msg[:, :, :].rearrange("p t c -> p (t c)")
        fT = msgf[:, 0:TPS * 40].rearrange("p (t i v) -> p t i v", i=5, v=8)
        g_s = msgf[:, 320:320 + TPS * 16].rearrange("p (t k) -> p t k", k=16)
        g_v = msgf[:, 448:448 + TPS * 48].rearrange("p (t o k) -> p t o k", o=3, k=16)
        tmpA = sb("tmpA", [P, TPS, 24])
        tmpB = sb("tmpB", [P, TPS, 24])
        rx = sb("rx", [P, TPS, 5])
        prod = sb("prod", [P, 2, 40, 16])
        dT = sb("dT", [TPS, P])
        hid = sb("hid", [HID + 1, TPS, P])
        w1row = sb("w1row", [TPS, HID + 1])
        w1sel = sb("w1sel", [TPS, TPS, HID + 1])
        b1col = sb("b1col", [HID + 1, 1])
        w2raw = sb("w2raw", [HID + 1, 384])
        w2p = sb("w2p", [HID + 1, 384])
        w2t = sb("w2t", [HID + 1, 64])
        wh = sb("wh", [P, F])
        whr = tabx[:, :, :].rearrange("p w c -> p (w c)")[:, 0:F * F].rearrange("p (f o) -> p f o", o=F)
        vtmp = tabx[:, :, :].rearrange("p w c -> p (w c)")[:, F * F:2 * F * F].rearrange("p (f o) -> p f o", o=F)
        fcw = sb("fcw", [P, 2 * F])
        vrow = sb("vrow", [P, 2, HEADS, F])
        gm = sb("gm", [P, 2, 2, HEADS])
        fcb = sb("fcb", [P, 1])
        bias0 = sb("bias0", [P, F])
        w1T = sb("w1T", [F, F])
        bias1 = sb("bias1", [P, F])
        g3w1 = sb("g3w1", [F, H2])
        g3b1 = sb("g3b1", [P, H2])
        g3w2 = sb("g3w2", [H2, F])
        g3b2 = sb("g3b2", [P, F])
        mask = sb("mask", [P, W])
        st1 = sb("st1", [P, W])
        st2 = sb("st2", [P, W])
        dis = sb("dis", [P, W])
        dinv = sb("dinv", [P, W])
        yb = sb("yb", [P, 2, P])
        yT = sb("yT", [P, 2, P])
        hb = sb("hb", [P, 2, H2])
        hT = sb("hT", [H2, 2, P])

        bank = [ctx.enter_context(nc.psum_tensor(f"bank{b}", [P, 512], F32)) for b in range(8)]

        loaded = sem("loaded")
        consts = sem("consts")
        vready = sem("vready")
        histed = sem("histed")
        hsum = sem("hsum")
        ended = sem("ended")
        endedT = sem("endedT")
        bucketed = sem("bucketed")
        compared = sem("compared")
        counted = sem("counted")
        filled = sem("filled")
        fill_set = sem("fill_set")
        ranked = sem("ranked")
        normed = sem("normed")
        sq_in = sem("sq_in")
        sq_out = sem("sq_out")
        ring_full = [sem(f"ring_full{s}") for s in range(RSLOTS)]
        whr_in = sem("whr_in")
        whr_used = sem("whr_used")
        chunk_in = sem("chunk_in")
        chunk_made = sem("chunk_made")
        chunk_sent = sem("chunk_sent")
        rows_sent = sem("rows_sent")
        ring_sent = [sem(f"ring_sent{s}") for s in range(RSLOTS)]
        tab_ready = sem("tab_ready")
        tab_sent = sem("tab_sent")
        pay_in = [sem(f"pay_in{s}") for s in range(SLOTS)]
        gat_in = {p_: [sem(f"gat_in{p_}_{s}") for s in range(SLOTS)] for p_ in (0, 2, 3, 4, 5)}
        att_in = [sem(f"att_in{s}") for s in range(SLOTS)]
        staged_out = [sem(f"staged_out{s}") for s in range(SLOTS)]
        step_done = sem("step_done")
        hot_ready = sem("hot_ready")
        sums_ready = sem("sums_ready")
        tp_done = sem("tp_done")
        hotT_ready = sem("hotT_ready")
        split_ready = sem("split_ready")
        mask_ready = sem("mask_ready")
        mask_used = sem("mask_used")
        am_ready = sem("am_ready")
        logit_ready = sem("logit_ready")
        prob_ready = sem("prob_ready")
        msg_ready = sem("msg_ready")
        dT_raw = sem("dT_raw")
        dT_ready = sem("dT_ready")
        hid_raw = sem("hid_raw")
        hid_ready = sem("hid_ready")
        geo_ready = sem("geo_ready")
        r_ready = sem("r_ready")
        r_used = sem("r_used")
        y_ready = sem("y_ready")
        yT_raw = sem("yT_raw")
        yT_ready = sem("yT_ready")
        z_ready = sem("z_ready")
        z_used = sem("z_used")
        h_ready = sem("h_ready")
        hT_raw = sem("hT_raw")
        hT_ready = sem("hT_ready")
        written = sem("written")

        block = ctx.enter_context(nc.Block())

        def node_rows(t):
            return t.rearrange("(w p) c -> p w c", p=P)

        def window_tail(name):
            return a[name][(W - 1) * P:N, :]

        PASS_MAX, PASS_ATT, PASS_L1, PASS_L2, PASS_L3A, PASS_L3B = range(6)
        KC = {PASS_MAX: 2, PASS_ATT: 2, PASS_L1: 2, PASS_L2: 6, PASS_L3A: 6, PASS_L3B: 6}
        GC = {PASS_MAX: C0, PASS_L1: C1, PASS_L2: F, PASS_L3A: F, PASS_L3B: F}
        TAB = {PASS_MAX: tab0, PASS_L1: tab1, PASS_L2: tab2, PASS_L3A: tab3, PASS_L3B: tab4}
        LIST = {PASS_MAX: by_src_v, PASS_ATT: by_src_v, PASS_L1: by_src_v,
                PASS_L2: by_dst_v, PASS_L3A: by_dst_v, PASS_L3B: by_dst_v}
        GATHERS = [PASS_MAX, PASS_L1, PASS_L2, PASS_L3A, PASS_L3B]

        def payv(s, pas):
            return pay[:, s, :, :].rearrange("p t c -> p (t c)")[:, 0:TPS * KC[pas]].rearrange(
                "p (t c) -> p t c", c=KC[pas])

        def gatv(s, c):
            return gat[:, s, :, :].rearrange("p t c -> p (t c)")[:, 0:TPS * c].rearrange("p (t c) -> p t c", c=c)

        def pay_count(pas, i):
            return (i + (pas * ITERS + 1)) * 16

        def gat_count(pas, i):
            return i * (16 * TPS) + 16 * TPS

        FILL_DMAS = 2 * (NT // FILL_T)
        sorted_dmas = 16 * RING

        @block.sync
        def _(sp):
            def load(dst, src):
                sp.dma_start(dst, src).then_inc(loaded, 16)

            load(srcs[:, :], a["src"].rearrange("(p t) -> p t", p=P))
            load(dsts[:, :], a["dst"].rearrange("(p t) -> p t", p=P))
            load(wh[:, :], a["L0_gnn_w"].rearrange("h f o -> (h f) o"))
            load(fcw[:, :], a["L0_gnn_fc_w"].to_broadcast([P, 2 * F]))
            load(fcb[:, :], a["L0_gnn_fc_b"].rearrange("(a b) -> a b", a=1).to_broadcast([P, 1]))
            load(bias0[:, :], a["L0_gnn_bias"].rearrange("(a b) -> a b", a=1).to_broadcast([P, F]))
            load(w1T[:, :], a["L1_WT"])
            load(bias1[:, :], a["L1_gnn_b"].rearrange("(a b) -> a b", a=1).to_broadcast([P, F]))
            load(g3w1[:, :], a["L3_gnn_W1"])
            load(g3b1[:, :], a["L3_gnn_b1"].rearrange("(a b) -> a b", a=1).to_broadcast([P, H2]))
            load(g3w2[:, :], a["L3_gnn_W2"])
            load(g3b2[:, :], a["L3_gnn_b2"].rearrange("(a b) -> a b", a=1).to_broadcast([P, F]))
            load(w1row[:, 0:HID], a["L2_gnn_w1"].to_broadcast([TPS, HID]))
            load(w2raw[0:HID, :], a["L2_gnn_w2"])
            load(w2raw[HID:HID + 1, :], a["L2_gnn_b2"].rearrange("(a b) -> a b", a=1))
            sp.wait_ge(fill_set, 1)
            load(x[:, 0:W - 1, :], a["x"][0:(W - 1) * P, :].rearrange("(w p) c -> p w c", p=P))
            load(x[0:LAST, W - 1, :], a["x"][(W - 1) * P:N, :])
            with nc.allow_non_contiguous_dma(reason="one value per node"):
                load(mask[:, 0:W - 1], a["node_vec1"][0:(W - 1) * P, :].rearrange("(w p) c -> p (w c)", p=P))
                load(mask[0:LAST, W - 1:W], a["node_vec1"][(W - 1) * P:N, :])
                load(b1col[0:HID, 0:1], a["L2_gnn_b1"].rearrange("(h c) -> h c", c=1))
            for f in range(NT // FILL_T):
                sp.dma_start(by_dst_v[:, f * FILL_T:(f + 1) * FILL_T, :], fill[:, :, :]).then_inc(filled, 16)
            for f in range(NT // FILL_T):
                sp.dma_start(by_src_v[:, f * FILL_T:(f + 1) * FILL_T, :], fill2[:, :, :]).then_inc(filled, 16)
            for h in range(HEADS):
                sp.wait_ge(whr_used, h + 1)
                sp.dma_start(whr, a["L0_gnn_w"][h:h + 1, :, :].to_broadcast([P, F, F])).then_inc(whr_in, 16)
            attr_v = a["edge_attr_3"].rearrange("(p t) c -> p t c", p=P)
            w_v = a["edge_weight"].rearrange("(p t) -> p t", p=P)
            for k in range(5):
                cols = slice(k * CHUNK, (k + 1) * CHUNK)
                if k:
                    sp.wait_ge(chunk_made, k)
                sp.dma_start(ch_attr, attr_v[:, cols, :]).then_inc(chunk_in, 16)
                sp.dma_start(ch_w, w_v[:, cols]).then_inc(chunk_in, 16)
                sp.wait_ge(chunk_made, k + 1)
                sp.dma_start(edges_dst.rearrange("(p t) c -> p t c", p=P)[:, cols, :], ch_pay).then_inc(chunk_sent, 16)
            sp.wait_ge(chunk_made, 6)
            sp.dma_start(edges_src.rearrange("(p t) c -> p t c", p=P), pair).then_inc(chunk_sent, 16)

            def ring_loads(k):
                rows, edges, c = ((rows_src, edges_src, 2), (rows_dst, edges_dst, 6))[k]
                sp.wait_ge(ranked, k + 1)
                sp.dma_start(rows.rearrange("(p t) c -> p (t c)", p=P), pos[:, :].bitcast(I32)).then_inc(rows_sent, 16)
                sp.wait_ge(rows_sent, 16 * (k + 1))
                sp.wait_ge(chunk_sent, 16 * 6)

                def ring_step(i):
                    for s in range(RSLOTS):
                        cols = bass.ds(i * (RSLOTS * RING) + s * RING, RING)
                        if not isinstance(i, int):
                            sp.wait_ge(ring_sent[s], i * sorted_dmas + sorted_dmas * RITERS * k)
                        sp.dma_start(posr[:, s, :], rows.rearrange("(p t) c -> p (t c)", p=P)[:, cols]).then_inc(ring_full[s], 16)
                        sp.dma_start(payr[:, s, :, :].rearrange("p t c -> p (t c)")[:, 0:RING * c].rearrange("p (t c) -> p t c", c=c),
                                     edges.rearrange("(p t) c -> p t c", p=P)[:, cols, :]).then_inc(ring_full[s], 16)

                if k:
                    for s in range(RSLOTS):
                        sp.wait_ge(ring_sent[s], sorted_dmas * RITERS * k)
                ring_step(0)
                with sp.Fori(1, RITERS) as i:
                    ring_step(i)

            def send_table(k, dst, c):
                sp.wait_ge(tab_ready, k + 1)
                view = tabx[:, :, :].rearrange("p w c -> p (w c)")[:, 0:W * c].rearrange("p (w c) -> p w c", c=c)
                sp.dma_start(node_rows(dst), view).then_inc(tab_sent, 16)

            def edge_loads(pas):
                with sp.Fori(0, ITERS) as i:
                    for s in range(SLOTS):
                        tiles = bass.ds(i * (SLOTS * TPS) + s * TPS, TPS)
                        sp.wait_ge(step_done, i * SLOTS + (pas * STEPS + s + 1))
                        sp.dma_start(payv(s, pas), LIST[pas][:, tiles, :]).then_inc(pay_in[s], 16)

            ring_loads(0)
            send_table(0, tab0, C0)
            sp.wait_ge(bucketed, 1)
            edge_loads(PASS_MAX)
            ring_loads(1)
            send_table(1, tab1, C1)
            edge_loads(PASS_L1)
            send_table(2, tab2, F)
            sp.wait_ge(bucketed, 2)
            edge_loads(PASS_L2)
            send_table(3, tab3, F)
            edge_loads(PASS_L3A)
            send_table(4, tab4, F)
            edge_loads(PASS_L3B)
            sp.wait_ge(tab_ready, 6)
            sp.dma_start(out[0:(W - 1) * P, :].rearrange("(w p) c -> p w c", p=P), x[:, 0:W - 1, :]).then_inc(written, 16)
            sp.dma_start(out[(W - 1) * P:N, :], x[0:LAST, W - 1, :]).then_inc(written, 16)
            sp.wait_ge(written, 32)
            sp.wait_ge(tab_sent, 16 * 5)
            sp.wait_ge(filled, 16 * FILL_DMAS)
            for s in range(SLOTS):
                sp.wait_ge(staged_out[s], 16 * ITERS)

        N_LOADS = 20

        @block.gpsimd
        def _(pool):
            g = nc.gpsimd
            g.iota(iota[:, :], pattern=[[1, P]], base=0, channel_multiplier=0,
                   allow_small_or_imprecise_dtypes=True)
            g.iota(giota, pattern=[[1, NG]], base=0, channel_multiplier=0,
                   allow_small_or_imprecise_dtypes=True)
            g.memset(ones[:, :], 1.0)
            g.memset(ident[:, :], 0.0)
            g.memset(before[:, :], 0.0)
            g.memset(far[:, :], -BIG)
            g.memset(pick[:, :, :], 0.0)
            pool.drain()
            g.affine_select(out=ident[:, :], in_=ident[:, :], compare_op=ALU.not_equal, fill=1.0,
                            base=0, pattern=[[-1, P]], channel_multiplier=1)
            g.affine_select(out=before[:, :], in_=before[:, :], compare_op=ALU.is_ge, fill=1.0,
                            base=0, pattern=[[-1, P]], channel_multiplier=1)
            g.affine_select(out=far[:, :], in_=far[:, :], compare_op=ALU.not_equal, fill=0.0,
                            base=0, pattern=[[-1, P]], channel_multiplier=1)
            for k in range(3):
                g.affine_select(out=pick[:, :, :], in_=pick[:, :, :], compare_op=ALU.not_equal, fill=1.0,
                                base=-32 * k, pattern=[[-1, 32], [0, P]], channel_multiplier=1)
                pool.drain()
            g.tensor_copy(identb[:, :], ident[:, :]).then_inc(consts, 1)
            pool.wait_ge(loaded, 16 * N_LOADS)
            g.memset(w1row[:, HID:HID + 1], 0.0)
            pool.drain()
            for t in range(TPS):
                g.tensor_copy(w1sel[:, t, :], w1row[:, :])
            pool.drain()
            g.affine_select(out=w1sel[:, :, :], in_=w1sel[:, :, :], compare_op=ALU.is_equal, fill=0.0,
                            base=0, pattern=[[-1, TPS], [0, HID + 1]], channel_multiplier=1).then_inc(consts, 1)

            def bucket(k, dst, c):
                pool.wait_ge(filled, 16 * FILL_DMAS)
                with pool.Fori(0, RITERS) as i:
                    for s in range(RSLOTS):
                        pool.wait_ge(ring_full[s], i * 32 + (32 * RITERS * k + 32))
                        pool.nop(nofuse=True)
                        pr = payr[:, s, :, :].rearrange("p t c -> p (t c)")
                        for j in range(RING):
                            pool.indirect_dma_start(
                                out=dst, out_offset=bass.IndirectOffsetOnAxis(ap=posr[:, s, j:j + 1], axis=0),
                                in_=pr[:, j * c:(j + 1) * c], in_offset=None).then_inc(ring_sent[s], 16)
                for s in range(RSLOTS):
                    pool.wait_ge(ring_sent[s], sorted_dmas * RITERS * (k + 1))
                pool.sem_inc(bucketed, 1)

            def gather(pas):
                def gather_step(i):
                    for s in range(SLOTS):
                        pool.wait_ge(pay_in[s], pay_count(pas, i))
                        if pas == PASS_MAX and not isinstance(i, int):
                            pool.wait_ge(staged_out[s], i * 16)
                        pool.nop(nofuse=True)
                        for t in range(TPS):
                            pool.indirect_dma_start(
                                out=gatv(s, GC[pas])[:, t, :], out_offset=None, in_=TAB[pas],
                                in_offset=bass.IndirectOffsetOnAxis(ap=payv(s, pas)[:, t, 1:2].bitcast(I32), axis=0),
                            ).then_inc(gat_in[pas][s], 16)

                gather_step(0)
                with pool.Fori(1, ITERS) as i:
                    gather_step(i)

            bucket(0, by_src, 2)
            pool.wait_ge(tab_sent, 16)
            gather(PASS_MAX)
            bucket(1, by_dst, 6)
            for k, pas in enumerate(GATHERS[1:]):
                pool.wait_ge(tab_sent, 16 * (k + 2))
                gather(pas)

        @block.scalar
        def _(act):
            s_ = nc.scalar
            roots = [0]

            def root(dst, src):
                roots[0] += 1
                act.wait_ge(sq_in, roots[0])
                s_.activation(dst, src, ACT.Sqrt).then_inc(sq_out, 1)

            act.sem_inc(step_done, SLOTS)
            for k in range(5):
                root(ch_len, ch_sq)

            with act.Fori(0, ITERS) as i:
                for s in range(SLOTS):
                    n = i * SLOTS + s
                    act.wait_ge(gat_in[PASS_MAX][s], gat_count(PASS_MAX, i))
                    act.dma_start(staged_v[:, bass.ds(i * (SLOTS * TPS) + s * TPS, TPS), :],
                                  gat[:, s, :, :]).then_inc(staged_out[s], 16)
                    act.wait_ge(tp_done, n + 1)
                    s_.copy(adT[:, :], bank[6][0:96, 0:64].bitcast(BF16))
                    s_.copy(hotT[:, :, :].rearrange("p t n -> p (t n)"),
                            bank[4][:, :].bitcast(BF16)).then_inc(hotT_ready, 1)
            for s in range(SLOTS):
                act.wait_ge(staged_out[s], 16 * ITERS)
            with act.Fori(0, ITERS) as i:
                for s in range(SLOTS):
                    n = i * SLOTS + s
                    tiles = bass.ds(i * (SLOTS * TPS) + s * TPS, TPS)
                    act.wait_ge(step_done, i * SLOTS + (PASS_ATT * STEPS + s + 1))
                    act.dma_start(payv(s, PASS_ATT), by_src_v[:, tiles, :]).then_inc(pay_in[s], 16)
                    act.dma_start(gat[:, s, :, :], staged_v[:, tiles, :]).then_inc(att_in[s], 16)
                    act.wait_ge(tp_done, n + (STEPS + 1))
                    for b in range(2):
                        last = s_.copy(hotT[:, 4 * b:4 * b + 4, :].rearrange("p t n -> p (t n)"), bank[4 + b][:, :])
                    last.then_inc(hotT_ready, 1)
                    act.wait_ge(logit_ready, n + 1)
                    s_.activation(prob[:, :, :], logit[:, :, :], ACT.Exp).then_inc(prob_ready, 1)

            def project(k, m, second):
                with act.Fori(0, W // 2) as j:
                    for b in range(2):
                        act.wait_ge(yT_raw, j * 2 + (k * W + b + 1))
                        s_.copy(yT[0:m, b, :], bank[b][0:m, 0:P]).then_inc(yT_ready, 1)
                        if second:
                            act.wait_ge(hT_raw, j * 2 + (b + 1))
                            s_.copy(hT[:, b, :], bank[4 + b][0:H2, 0:P]).then_inc(hT_ready, 1)

            project(0, P, False)
            root(st2[:, :], st2[:, :])
            root(st1[:, :], st1[:, :])
            project(1, F, False)
            root(st2[:, :], st2[:, :])
            with act.Fori(0, ITERS) as i:
                for s in range(SLOTS):
                    n = i * SLOTS + s
                    act.wait_ge(dT_raw, n + 1)
                    s_.copy(dT[:, :], bank[6][0:TPS, 0:P]).then_inc(dT_ready, 1)
                    act.wait_ge(gat_in[PASS_L2][s], gat_count(PASS_L2, i))
                    act.wait_ge(step_done, n + (PASS_L2 * STEPS + SLOTS))
                    fv = gatv(s, F)
                    fv1 = fv[:, :, 8:32].rearrange("p t (v i) -> p t i v", i=3)
                    s_.copy(fT[:, :, 0:3, :], fv1)
                    s_.copy(fT[:, :, 3:5, :], fv1[:, :, 0:2, :])
                    s_.copy(g_v[:, :, :, 0:8], fv1)
                    s_.copy(g_s[:, :, 0:8], fv[:, :, 0:8])
                    s_.copy(rx[:, :, 0:3], payv(s, PASS_L2)[:, :, 3:6])
                    s_.copy(rx[:, :, 3:5], payv(s, PASS_L2)[:, :, 3:5]).then_inc(geo_ready, 1)
                    act.wait_ge(hid_raw, n + 1)
                    for b in range(2):
                        last = s_.activation(hid[:, 4 * b:4 * b + 4, :].rearrange("p t n -> p (t n)"),
                                             bank[4 + b][0:HID + 1, :], ACT.Relu, bias=b1col[:, :])
                    last.then_inc(hid_ready, 1)
            root(st2[:, :], st2[:, :])
            root(st1[:, :], st1[:, :])
            project(2, F, True)
            root(st2[:, :], st2[:, :])

        @block.tensor
        def _(pe):
            t_ = nc.tensor
            pe.wait_ge(consts, 2)

            def bucket_sums(k):
                pe.wait_ge(histed, k + 1)
                t_.matmul(bank[0][:, 0:W], before[:, :], hist[:, :], start=True, stop=True)
                t_.matmul(bank[0][:, P:P + W], ones[:, :], hist[:, :], start=True, stop=True).then_inc(hsum, 1)
                pe.wait_ge(ended, k + 1)
                t_.transpose(bank[1][0:W, 0:P], ends[:, :], ident[:, :]).then_inc(endedT, 1)
                pe.wait_ge(compared, k + 1)
                q = NG // 4
                for b in range(4):
                    last = t_.matmul(bank[2 + b][0:1, 0:q], ones[0:W, 0:1], gge[0:W, b * q:(b + 1) * q],
                                     start=True, stop=True)
                last.then_inc(counted, 1)

            bucket_sums(0)
            bucket_sums(1)

            def group_sums(rows, c, where):
                for q in range(GPS):
                    for h in range(TILES_PER_GROUP):
                        t = q * TILES_PER_GROUP + h
                        last = t_.matmul(where(q), hot[:, t, :], rows(t), start=(h == 0), stop=(h == TILES_PER_GROUP - 1))
                last.then_inc(sums_ready, 1)

            with pe.Fori(0, ITERS) as i:
                for s in range(SLOTS):
                    n = i * SLOTS + s
                    pe.wait_ge(split_ready, n + 1)
                    t_.transpose(bank[6][0:96, 0:64].bitcast(BF16), adsp[:, :, :].rearrange("p k c -> p (k c)"), identb[:, :])
                    for t in range(TPS):
                        last = t_.transpose(bank[4][:, 64 * t:64 * t + 64].bitcast(BF16), hotb[:, t, :], identb[:, :])
                    last.then_inc(tp_done, 1)
                    pe.wait_ge(hotT_ready, n + 1)
                    for q in range(GPS):
                        pe.wait_ge(mask_used, n * GPS + (q + 1))
                        for h in range(TILES_PER_GROUP):
                            t = q * TILES_PER_GROUP + h
                            dst = bank[2 * (q % 2) + h]
                            hT_b = hotT[:, t:t + 1, :].to_broadcast([P, HEADS, P])
                            t_.matmul(dst[:, :].rearrange("p (h e) -> p h e", h=HEADS), far[:, :], hT_b,
                                      start=True, stop=False, skip_group_check=True)
                            for hd in range(HEADS):
                                last = t_.matmul(dst[:, hd * P:(hd + 1) * P], pick[:, t * HEADS + hd, :], adT[:, :],
                                                 start=False, stop=(hd == HEADS - 1), skip_group_check=True)
                        last.then_inc(mask_ready, 1)
            with pe.Fori(0, ITERS) as i:
                for s in range(SLOTS):
                    n = i * SLOTS + s
                    wins = [pe.value_load(win_src[0:1, bass.ds(n * GPS + q, 1)], min_val=0, max_val=W - 1)
                            for q in range(GPS)]
                    pe.wait_ge(hot_ready, n + 1)
                    for t in range(TPS):
                        last = t_.transpose(bank[4 + t // 4][:, (t % 4) * P:(t % 4 + 1) * P], hot[:, t, :], ident[:, :])
                    last.then_inc(tp_done, 1)
                    pe.wait_ge(hotT_ready, n + (STEPS + 1))
                    for t in range(TPS):
                        flat = nodesp[:, :, :, :].rearrange("p w k c -> p (w k c)")
                        last = t_.matmul(bank[6][:, 24 * t:24 * t + 24], hotT[:, t, :],
                                         flat[:, bass.ds(wins[t // TILES_PER_GROUP] * 24, 24)], start=True, stop=True)
                    last.then_inc(am_ready, 1)
                    pe.wait_ge(msg_ready, n + 1)
                    group_sums(lambda t: msg[:, t, :], CM, lambda q: bank[q // 2][:, (q % 2) * CM:(q % 2 + 1) * CM])

            def project(k, m, w_, mo, second):
                with pe.Fori(0, W // 2) as j:
                    for b in range(2):
                        n = j * 2 + b
                        pe.wait_ge(y_ready, n + (k * W + 1))
                        t_.transpose(bank[b][0:m, 0:P], yb[:, b, 0:m], ident[:, :]).then_inc(yT_raw, 1)
                        pe.wait_ge(yT_ready, n + (k * W + 1))
                        t_.matmul(bank[2 + b][:, 0:mo], yT[0:m, b, :], w_, start=True, stop=True).then_inc(z_ready, 1)
                        if second is not None:
                            pe.wait_ge(h_ready, n + 1)
                            pe.nop(nofuse=True)
                            t_.transpose(bank[4 + b][0:H2, 0:P], hb[:, b, :], ident[:, :]).then_inc(hT_raw, 1)
                            pe.wait_ge(hT_ready, n + 1)
                            t_.matmul(bank[6 + b][:, 0:F], hT[:, b, :], second, start=True, stop=True).then_inc(z_ready, 1)

            def spmm(pas, c, hot_base):
                with pe.Fori(0, ITERS) as i:
                    for s in range(SLOTS):
                        pe.wait_ge(hot_ready, i * SLOTS + (hot_base * STEPS + s + 1))
                        pe.wait_ge(gat_in[pas][s], gat_count(pas, i))
                        group_sums(lambda t: gatv(s, c)[:, t, :], c, lambda q: bank[0][:, q * c:(q + 1) * c])

            project(0, P, wh[:, :], F, None)
            spmm(PASS_L1, C1, 1)
            project(1, F, w1T[:, :], F, None)
            with pe.Fori(0, ITERS) as i:
                for s in range(SLOTS):
                    n = i * SLOTS + s
                    pe.wait_ge(pay_in[s], pay_count(PASS_L2, i))
                    pe.wait_ge(step_done, n + (PASS_L2 * STEPS + SLOTS))
                    t_.transpose(bank[6][0:TPS, 0:P], payv(s, PASS_L2)[:, :, 2], ident[:, :]).then_inc(dT_raw, 1)
                    pe.wait_ge(dT_ready, n + 1)
                    for t in range(TPS):
                        last = t_.matmul(bank[4 + t // 4][0:HID + 1, (t % 4) * P:(t % 4 + 1) * P],
                                         w1sel[:, t, :], dT[:, :], start=True, stop=True)
                    last.then_inc(hid_raw, 1)
                    pe.wait_ge(hid_ready, n + 1)
                    for t in range(TPS):
                        pe.wait_ge(r_used, n * TPS + (t + 1))
                        t_.matmul(bank[1 + t % 3][:, 0:384], hid[:, t, :], w2p[:, :],
                                  start=True, stop=True).then_inc(r_ready, 1)
                    pe.wait_ge(msg_ready, n + (STEPS + 1))
                    group_sums(lambda t: red[:, t, :], C2, lambda q: bank[0][:, q * C2:(q + 1) * C2])
            spmm(PASS_L3A, F, 3)
            project(2, F, g3w1[:, :], H2, g3w2[:, :])
            spmm(PASS_L3B, F, 4)

        @block.vector
        def _(dve):
            v = nc.vector
            tabf = tabx[:, :, :].rearrange("p w c -> p (w c)")

            def tab(c):
                return tabf[:, 0:W * c].rearrange("p (w c) -> p w c", c=c)

            def accv(c):
                return acc[:, 0:W * c].rearrange("p (w c) -> p w c", c=c)

            def each(col, c):
                return col.rearrange("p (w a) -> p w a", a=1).to_broadcast([P, W, c])

            def row(vec, c=F):
                return vec.rearrange("p (a c) -> p a c", a=1).to_broadcast([P, W, c])

            dve.sem_inc(mask_used, 2)
            dve.sem_inc(r_used, 3)
            v.memset(fill[:, :, 0:1].bitcast(I32), PAD_KEY)
            v.memset(fill[:, :, 1:3], 0.0)
            v.memset(fill[:, :, 3:6], 1.0)
            v.memset(fill2[:, :, 0:1].bitcast(I32), PAD_KEY)
            v.memset(fill2[:, :, 1:2], 0.0)
            v.memset(x[:, W - 1, :], 0.0)
            v.memset(mask[:, :], 0.0)
            v.memset(b1col[:, :], 1.0)
            v.memset(mmax[:, :, :], -BIG)
            v.memset(red[:, :, :], 1.0)
            v.memset(msg[:, :, CM - 1:CM], 1.0).then_inc(fill_set, 1)
            dve.wait_ge(loaded, 16 * N_LOADS)
            dve.wait_ge(consts, 1)

            dve.sem_inc(whr_used, 1)
            for h in range(HEADS):
                dve.wait_ge(whr_in, 16 * (h + 1))
                for k in range(2):
                    v.tensor_tensor(vtmp, whr, fcw[:, k * F:(k + 1) * F].rearrange("p (a c) -> p a c", a=1)
                                    .to_broadcast([P, F, F]), ALU.mult)
                    dve.drain()
                    last = v.tensor_reduce(vrow[:, k, h, :], vtmp, AX.X, ALU.add)
                    dve.drain()
                v.tensor_copy(gm[:, 0, 0, 0:1], iota[:, 0:1]).then_inc(whr_used, 1)

            for k in range(5):
                cols = slice(k * CHUNK, (k + 1) * CHUNK)
                dve.wait_ge(chunk_in, 32 * (k + 1))
                if k:
                    dve.wait_ge(chunk_sent, 16 * k)
                v.tensor_copy(ch_pay[:, :, 0].bitcast(I32), dsts[:, cols])
                v.tensor_copy(ch_pay[:, :, 1].bitcast(I32), srcs[:, cols])
                v.tensor_copy(ch_pay[:, :, 2], ch_w)
                v.tensor_tensor(ch_pay[:, :, 3:6], ch_attr, ch_attr, ALU.mult)
                dve.drain()
                v.tensor_reduce(ch_sq, ch_pay[:, :, 3:6], AX.X, ALU.add).then_inc(sq_in, 1)
                dve.wait_ge(sq_out, k + 1)
                v.reciprocal(ch_sq, ch_len)
                dve.drain()
                for c in range(3):
                    v.tensor_tensor(ch_pay[:, :, 3 + c], ch_attr[:, :, (c + 1) % 3], ch_sq, ALU.mult)
                dve.drain()
                v.tensor_copy(gm[:, 0, 0, 0:1], iota[:, 0:1]).then_inc(chunk_made, 1)
            dve.wait_ge(chunk_sent, 16 * 5)
            v.tensor_copy(pair[:, :, 0].bitcast(I32), srcs[:, :])
            v.tensor_copy(pair[:, :, 1].bitcast(I32), dsts[:, :]).then_inc(chunk_made, 1)
            dve.wait_ge(chunk_sent, 16 * 6)

            cp = _coupling()
            q_ = w2p[:, 0:256].rearrange("p (u k) -> p u k", k=16)
            ab = w2p[:, 256:384].rearrange("p (u k) -> p u k", k=16)
            blk = [w2raw[:, 64 * b:64 * b + 64].rearrange("p (u v) -> p u v", v=8) for b in range(3)]
            vec = w2raw[:, 192:384].rearrange("p (u v k) -> p u v k", v=8, k=3)
            w2tv = w2t[:, :].rearrange("p (u v) -> p u v", v=8)
            v.tensor_scalar(q_[:, 0:8, 0:8], blk[0], cp["s_f0"], None, ALU.mult)
            v.tensor_scalar(q_[:, 0:8, 8:16], blk[1], cp["s_dot"], None, ALU.mult)
            v.tensor_scalar(q_[:, 8:16, 0:8], blk[2], cp["v_f0"], None, ALU.mult)
            v.tensor_scalar(q_[:, 8:16, 8:16], vec[:, :, :, 2], 3.0 * cp["v_quad"], None, ALU.mult)
            v.tensor_scalar(ab[:, :, 8:16], vec[:, :, :, 1], cp["v_cross"], None, ALU.mult)
            v.tensor_scalar(w2tv, vec[:, :, :, 2], -cp["v_quad"], None, ALU.mult)
            v.tensor_scalar(ab[:, :, 0:8], vec[:, :, :, 0], cp["v_same"], None, ALU.mult)
            dve.drain()
            v.tensor_tensor(ab[:, :, 0:8], ab[:, :, 0:8], w2tv, ALU.add)
            dve.drain()

            def rank(k, key, win_tab):
                v.tensor_scalar(cum.bitcast(I32), key[:, :], 7, None, ALU.logical_shift_right)
                dve.drain()
                v.tensor_copy(winb, cum.bitcast(I32))
                dve.drain()
                with dve.Fori(0, W) as w:
                    v.tensor_scalar(cum, winb, iota[:, bass.ds(w, 1)], None, ALU.is_equal, ALU.add,
                                    accum_out=hist[:, bass.ds(w, 1)])
                    dve.drain()
                v.tensor_copy(start_[:, :], hist[:, :]).then_inc(histed, 1)
                dve.wait_ge(hsum, k + 1)
                v.tensor_scalar(gcnt[:, :], bank[0][:, P:P + W], float(GROUP - 1), None, ALU.add)
                dve.drain()
                v.tensor_scalar(gcnt[:, :], gcnt[:, :], GROUP.bit_length() - 1, None, ALU.logical_shift_right)
                dve.drain()
                v.tensor_copy(hist[:, :], gcnt[:, :])
                dve.drain()
                v.tensor_tensor_scan(ends[:, :], ones[:, 0:W], hist[:, :], 0.0, ALU.mult, ALU.add)
                dve.drain()
                v.tensor_tensor(start_[:, :], ends[:, :], hist[:, :], ALU.subtract).then_inc(ended, 1)
                dve.drain()
                v.tensor_scalar(start_[:, :], start_[:, :], float(GROUP), None, ALU.mult)
                dve.drain()
                v.tensor_tensor(start_[:, :], start_[:, :], bank[0][:, 0:W], ALU.add)
                dve.wait_ge(endedT, k + 1)
                v.tensor_copy(endT[0:W, :], bank[1][0:W, 0:1])
                dve.drain()
                v.tensor_scalar(gge[0:W, :], giota[0:W, :], endT[0:W, :], None, ALU.is_ge).then_inc(compared, 1)
                dve.wait_ge(counted, k + 1)
                q = NG // 4
                for b in range(4):
                    v.tensor_scalar(win_tab[:, b * q:(b + 1) * q], bank[2 + b][0:1, 0:q], float(W - 1), None, ALU.min)
                with dve.Fori(0, W) as w:
                    v.tensor_scalar(eqm, winb, iota[:, bass.ds(w, 1)], None, ALU.is_equal)
                    dve.drain()
                    v.tensor_tensor_scan(cum, eqm, eqm, start_[:, bass.ds(w, 1)], ALU.add, ALU.max)
                    dve.drain()
                    v.copy_predicated(pos[:, :], eqm, cum)
                    dve.drain()
                v.tensor_scalar(cum.bitcast(I32), pos[:, :], -1.0, None, ALU.add)
                dve.drain()
                v.tensor_scalar(winb.bitcast(I32), cum.bitcast(I32), 7, None, ALU.logical_shift_right)
                v.tensor_scalar(pos[:, :].bitcast(I32), cum.bitcast(I32), P - 1, None, ALU.bitwise_and)
                dve.drain()
                v.tensor_copy(cum, pos[:, :].bitcast(I32))
                dve.drain()
                v.scalar_tensor_tensor(pos[:, :].bitcast(I32), cum, float(NT), winb.bitcast(I32),
                                       ALU.mult, ALU.add).then_inc(ranked, 1)
                dve.drain()

            rank(0, srcs, win_src)

            t0 = tab(C0)
            sq = acc[:, 0:W * F].rearrange("p (w c) -> p w c", c=F)
            for k in range(2):
                for h in range(HEADS):
                    v.tensor_tensor(sq, x[:, :, :], row(vrow[:, k, h, :]), ALU.mult)
                    dve.drain()
                    dst = asrc[:, :, h] if k == 0 else t0[:, :, F + 1 + h]
                    v.tensor_reduce(dst, sq, AX.X, ALU.add)
                    dve.drain()
            v.tensor_copy(t0[:, :, 0:F], x[:, :, :])
            v.memset(t0[:, :, F:F + 1], 1.0).then_inc(tab_ready, 1)

            dve.wait_ge(rows_sent, 16)
            rank(1, dsts, win_dst)

            def windows(win_tab, n):
                return [dve.value_load(win_tab[0:1, bass.ds(n * GPS + q, 1)], min_val=0, max_val=W - 1)
                        for q in range(GPS)]

            def one_hot(s, pas, i, dst, pads=False):
                dve.wait_ge(pay_in[s], pay_count(pas, i))
                key = payv(s, pas)[:, :, 0].bitcast(I32)
                v.tensor_scalar(keyi[:, :], key, KEY_MASK, None, ALU.bitwise_and)
                if pads:
                    v.tensor_scalar(padf[:, :], key, float(PAD_KEY), -BIG, ALU.is_ge, ALU.mult)
                dve.drain()
                v.tensor_copy(keyf[:, :], keyi[:, :])
                dve.drain()
                return v.tensor_tensor(dst, iota[:, :].rearrange("p (a n) -> p a n", a=1).to_broadcast([P, TPS, P]),
                                       keyf[:, :].rearrange("p (t a) -> p t a", a=1).to_broadcast([P, TPS, P]),
                                       ALU.is_equal)

            def add_sums(wins, c, where, order, n, pas):
                dve.drain()
                dve.wait_ge(sums_ready, n + (order * STEPS + 1))
                for q in range(GPS):
                    if q:
                        dve.drain()
                    dst = acc[:, bass.ds(wins[q] * c, c)]
                    last = v.tensor_tensor(dst, dst, where(q), ALU.add)
                last.then_inc(step_done, 1)

            with dve.Fori(0, ITERS) as i:
                for s in range(SLOTS):
                    n = i * SLOTS + s
                    wins = windows(win_src, n)
                    one_hot(s, PASS_MAX, i, hotb, pads=True)
                    dve.wait_ge(gat_in[PASS_MAX][s], gat_count(PASS_MAX, i))
                    v.tensor_tensor(adm[:, :, :], gat[:, s, :, F + 1:C0],
                                    padf[:, :].rearrange("p (t a) -> p t a", a=1).to_broadcast([P, TPS, HEADS]), ALU.add)
                    dve.drain()
                    flat = adm[:, :, :].rearrange("p t h -> p (t h)")
                    v.tensor_copy(adsp[:, 0, :], flat)
                    dve.drain()
                    v.tensor_tensor(flat, flat, adsp[:, 0, :], ALU.subtract)
                    dve.drain()
                    v.tensor_copy(adsp[:, 1, :], flat)
                    dve.drain()
                    v.tensor_tensor(adsp[:, 2, :], flat, adsp[:, 1, :], ALU.subtract).then_inc(split_ready, 1)
                    for q in range(GPS):
                        dve.wait_ge(mask_ready, n * GPS + (q + 1))
                        for h in range(2):
                            last = v.tensor_reduce(gm[:, q % 2, h, :], bank[2 * (q % 2) + h][:, :].rearrange(
                                "p (h e) -> p h e", h=HEADS), AX.X, ALU.max)
                        last.then_inc(mask_used, 1)
                        dve.drain()
                        v.tensor_tensor(gm[:, q % 2, 0, :], gm[:, q % 2, 0, :], gm[:, q % 2, 1, :], ALU.max)
                        dve.drain()
                        dst = mmax[:, :, :].rearrange("p w h -> p (w h)")[:, bass.ds(wins[q] * HEADS, HEADS)]
                        last = v.tensor_tensor(dst, dst, gm[:, q % 2, 0, :], ALU.max)
                    last.then_inc(step_done, 1)
            dve.drain()
            v.tensor_scalar(nodeam[:, :, 0:HEADS], asrc[:, :, :], fcb[:, :], None, ALU.add)
            dve.drain()
            v.tensor_tensor(mmax[:, :, :], mmax[:, :, :], nodeam[:, :, 0:HEADS], ALU.add)
            dve.drain()
            v.scalar_tensor_tensor(nodeam[:, :, HEADS:2 * HEADS], mmax[:, :, :], 0.2, mmax[:, :, :], ALU.mult, ALU.max)
            dve.drain()
            v.tensor_copy(nodesp[:, :, 0, :], nodeam[:, :, :])
            dve.drain()
            v.tensor_tensor(nodeam[:, :, :], nodeam[:, :, :], nodesp[:, :, 0, :], ALU.subtract)
            dve.drain()
            v.tensor_copy(nodesp[:, :, 1, :], nodeam[:, :, :])
            dve.drain()
            v.tensor_tensor(nodesp[:, :, 2, :], nodeam[:, :, :], nodesp[:, :, 1, :], ALU.subtract)
            dve.wait_ge(filled, 16 * FILL_DMAS)
            v.memset(acc[:, :], 0.0)
            dve.drain()

            with dve.Fori(0, ITERS) as i:
                for s in range(SLOTS):
                    n = i * SLOTS + s
                    wins = windows(win_src, n)
                    one_hot(s, PASS_ATT, i, hot[:, :, :]).then_inc(hot_ready, 1)
                    dve.wait_ge(am_ready, n + 1)
                    v.tensor_reduce(am[:, :, :], bank[6][:, 0:24 * TPS].rearrange("p (t k c) -> p t c k", k=3, c=2 * HEADS),
                                    AX.X, ALU.add)
                    dve.drain()
                    dve.wait_ge(att_in[s], i * 16 + 16)
                    v.tensor_tensor(logit[:, :, :], am[:, :, 0:HEADS], gat[:, s, :, F + 1:C0], ALU.add)
                    dve.drain()
                    v.scalar_tensor_tensor(logit[:, :, :], logit[:, :, :], 0.2, logit[:, :, :], ALU.mult, ALU.max)
                    dve.drain()
                    v.tensor_tensor(logit[:, :, :], logit[:, :, :], am[:, :, HEADS:2 * HEADS], ALU.subtract)
                    dve.drain()
                    v.tensor_scalar(logit[:, :, :], logit[:, :, :], 0.0, None, ALU.min).then_inc(logit_ready, 1)
                    dve.wait_ge(prob_ready, n + 1)
                    v.tensor_tensor(msg[:, :, 0:CM - 1].rearrange("p t (h c) -> p t h c", h=HEADS),
                                    gat[:, s, :, 0:F + 1].rearrange("p t (a c) -> p t a c", a=1).to_broadcast([P, TPS, HEADS, F + 1]),
                                    prob[:, :, :].rearrange("p t (h a) -> p t h a", a=1).to_broadcast([P, TPS, HEADS, F + 1]),
                                    ALU.mult).then_inc(msg_ready, 1)
                    add_sums(wins, CM, lambda q: bank[q // 2][:, (q % 2) * CM:(q % 2 + 1) * CM], 0, n, PASS_ATT)
            dve.drain()

            def spmm(pas, c, order, win_tab):
                with dve.Fori(0, ITERS) as i:
                    for s in range(SLOTS):
                        n = i * SLOTS + s
                        wins = windows(win_tab, n)
                        one_hot(s, pas, i, hot[:, :, :]).then_inc(hot_ready, 1)
                        add_sums(wins, c, lambda q: bank[0][:, q * c:(q + 1) * c], order, n, pas)
                dve.drain()

            def project(k, make_y, take_z, take_h=None):
                zs = W * k
                per = 2 if take_h else 1
                with dve.Fori(0, W // 2) as j:
                    for b in range(2):
                        make_y(j * 2 + b, b).then_inc(y_ready, 1)
                    for b in range(2):
                        if take_h:
                            dve.wait_ge(z_ready, j * 4 + (zs + 2 * b + 1))
                            take_h(b).then_inc(h_ready, 1)
                        dve.wait_ge(z_ready, j * (2 * per) + (zs + per * b + per))
                        take_z(j * 2 + b, b)
                dve.drain()

            roots = [5]

            def root_of(last):
                last.then_inc(sq_in, 1)
                roots[0] += 1
                dve.wait_ge(sq_out, roots[0])

            def layernorm():
                t = tab(F)
                v.tensor_reduce(st1[:, :], x[:, :, :], AX.X, ALU.add)
                dve.drain()
                v.tensor_scalar(st1[:, :], st1[:, :], 1.0 / F, None, ALU.mult)
                dve.drain()
                v.tensor_tensor(x[:, :, :], x[:, :, :], each(st1[:, :], F), ALU.subtract)
                dve.drain()
                v.tensor_tensor(t, x[:, :, :], x[:, :, :], ALU.mult)
                dve.drain()
                v.tensor_reduce(st2[:, :], t, AX.X, ALU.add)
                dve.drain()
                root_of(v.tensor_scalar(st2[:, :], st2[:, :], 1.0 / F, EPS, ALU.mult, ALU.add))
                v.reciprocal(st2[:, :], st2[:, :])
                dve.drain()
                v.tensor_tensor(x[:, :, :], x[:, :, :], each(st2[:, :], F), ALU.mult)
                dve.drain()

            a0 = accv(CM)
            sums = a0[:, :, 0:CM - 1].rearrange("p w (h c) -> p w h c", h=HEADS)[:, :, :, F]
            v.tensor_scalar(asrc[:, :, :], sums, 0.0, None, ALU.is_equal)
            dve.drain()
            v.tensor_tensor(asrc[:, :, :], asrc[:, :, :], sums, ALU.add)
            dve.drain()
            v.reciprocal(asrc[:, :, :], asrc[:, :, :])
            v.tensor_copy(dis[:, :], a0[:, :, CM - 1])
            dve.drain()

            def y0(w, b):
                return v.tensor_tensor(
                    yb[:, b, :].rearrange("p (h c) -> p h c", h=HEADS),
                    acc[:, bass.ds(w * CM, CM)][:, 0:CM - 1].rearrange("p (h c) -> p h c", h=HEADS)[:, :, 0:F],
                    asrc[:, :, :].rearrange("p w h -> p (w h)")[:, bass.ds(w * HEADS, HEADS)]
                    .rearrange("p (h a) -> p h a", a=1).to_broadcast([P, HEADS, F]), ALU.mult)

            def xw(w):
                return x[:, :, :].rearrange("p w c -> p (w c)")[:, bass.ds(w * F, F)]

            def z0(w, b):
                return v.scalar_tensor_tensor(xw(w), bank[2 + b][:, 0:F], 1.0 / HEADS, xw(w), ALU.mult, ALU.add)

            project(0, y0, z0)
            v.tensor_tensor(x[:, :, :], x[:, :, :], row(bias0[:, :]), ALU.add)
            dve.wait_ge(tab_sent, 16)
            dve.drain()
            layernorm()

            v.tensor_scalar(dinv[:, :], dis[:, :], 0.0, None, ALU.is_gt)
            root_of(v.tensor_scalar(st1[:, :], dis[:, :], 1.0, None, ALU.max))
            v.reciprocal(st1[:, :], st1[:, :])
            dve.drain()
            v.tensor_tensor(dis[:, :], st1[:, :], dinv[:, :], ALU.mult)
            dve.drain()
            t1 = tab(C1)
            v.tensor_tensor(t1[:, :, F + 1], dis[:, :], mask[:, :], ALU.mult)
            v.tensor_copy(t1[:, :, F], dis[:, :])
            ok = acc[:, 0:W * F // 4].bitcast(U8).rearrange("p (w c) -> p w c", c=F)
            v.tensor_tensor(ok, x[:, :, :], x[:, :, :], ALU.is_equal)
            v.memset(t1[:, :, 0:F], 0.0)
            dve.drain()
            v.copy_predicated(t1[:, :, 0:F], ok, x[:, :, :])
            dve.drain()
            v.tensor_scalar(t1[:, :, 0:F], t1[:, :, 0:F], FMAX, -FMAX, ALU.min, ALU.max)
            dve.drain()
            v.tensor_tensor(t1[:, :, 0:F], t1[:, :, 0:F], t1[:, :, F + 1:F + 2].to_broadcast([P, W, F]),
                            ALU.mult).then_inc(tab_ready, 1)
            dve.drain()
            v.memset(acc[:, 0:W * C1], 0.0)
            dve.drain()
            spmm(PASS_L1, C1, 1, win_src)
            a1 = accv(C1)
            v.tensor_tensor(st2[:, :], dis[:, :], a1[:, :, F + 1], ALU.mult)
            v.tensor_tensor(st1[:, :], dis[:, :], a1[:, :, F], ALU.mult)
            dve.drain()
            v.tensor_scalar(dinv[:, :], st2[:, :], 0.0, None, ALU.is_equal)
            v.tensor_tensor(st1[:, :], st1[:, :], dis[:, :], ALU.mult)
            dve.drain()
            v.tensor_tensor(st2[:, :], st2[:, :], dinv[:, :], ALU.add)
            dve.drain()
            v.reciprocal(st2[:, :], st2[:, :])
            v.tensor_scalar(dinv[:, :], dinv[:, :], -1.0, 1.0, ALU.mult, ALU.add)
            dve.drain()
            v.tensor_tensor(st1[:, :], st1[:, :], st2[:, :], ALU.mult)
            dve.drain()
            v.tensor_tensor(st1[:, :], st1[:, :], dinv[:, :], ALU.mult)
            dve.drain()

            def y1(w, b):
                return v.tensor_scalar(yb[:, b, 0:F], acc[:, bass.ds(w * C1, C1)][:, 0:F], st1[:, bass.ds(w, 1)],
                                       None, ALU.mult)

            def z1(w, b):
                return v.tensor_tensor(xw(w), bank[2 + b][:, 0:F], xw(w), ALU.add)

            project(1, y1, z1)
            v.tensor_tensor(x[:, :, :], x[:, :, :], row(bias1[:, :]), ALU.add)
            dve.wait_ge(tab_sent, 32)
            dve.drain()
            layernorm()

            v.tensor_copy(tab(F), x[:, :, :]).then_inc(tab_ready, 1)
            v.memset(acc[:, 0:W * C2], 0.0)
            dve.drain()
            with dve.Fori(0, ITERS) as i:
                for s in range(SLOTS):
                    n = i * SLOTS + s
                    wins = windows(win_dst, n)
                    one_hot(s, PASS_L2, i, hot[:, :, :]).then_inc(hot_ready, 1)
                    dve.wait_ge(geo_ready, n + 1)

                    def r_(lo):
                        return rx[:, :, lo:lo + 3].rearrange("p t (o a) -> p t o a", a=1).to_broadcast([P, TPS, 3, 8])

                    tA = tmpA[:, :, :].rearrange("p t (o v) -> p t o v", o=3)
                    tB = tmpB[:, :, :].rearrange("p t (o v) -> p t o v", o=3)
                    v.tensor_tensor(tA, fT[:, :, 2:5, :], r_(1), ALU.mult)
                    v.tensor_tensor(tB, fT[:, :, 1:4, :], r_(2), ALU.mult)
                    dve.drain()
                    v.tensor_tensor(g_v[:, :, :, 8:16], tA, tB, ALU.subtract)
                    dve.drain()
                    v.tensor_tensor(tA, fT[:, :, 0:3, :], r_(0), ALU.mult)
                    dve.drain()
                    v.tensor_reduce(g_s[:, :, 8:16], tmpA[:, :, :].rearrange("p t (o v) -> p t v o", o=3), AX.X, ALU.add)
                    dve.drain()
                    for t in range(TPS):
                        dve.wait_ge(r_ready, n * TPS + (t + 1))
                        r = bank[1 + t % 3]
                        pb = t % 2
                        v.tensor_tensor(prod[:, pb, 0:16, :], r[:, 0:256].rearrange("p (u k) -> p u k", k=16),
                                        g_s[:, t:t + 1, :].to_broadcast([P, 16, 16]), ALU.mult)
                        v.tensor_tensor(prod[:, pb, 16:40, :].rearrange("p (u o) k -> p u o k", o=3),
                                        r[:, 256:384].rearrange("p (u a k) -> p u a k", a=1, k=16).to_broadcast([P, 8, 3, 16]),
                                        g_v[:, t:t + 1, :, :].to_broadcast([P, 8, 3, 16]), ALU.mult).then_inc(r_used, 1)
                        dve.drain()
                        v.tensor_reduce(red[:, t, 0:40], prod[:, pb, :, :], AX.X, ALU.add)
                    dve.drain()
                    v.tensor_tensor(tmpA[:, :, :].rearrange("p t (u o) -> p t u o", o=3),
                                    rx[:, :, 0:3].rearrange("p t (a o) -> p t a o", a=1).to_broadcast([P, TPS, 8, 3]),
                                    red[:, :, 8:16].rearrange("p t (u a) -> p t u a", a=1).to_broadcast([P, TPS, 8, 3]), ALU.mult)
                    dve.drain()
                    v.tensor_tensor(red[:, :, 16:40], red[:, :, 16:40], tmpA[:, :, :], ALU.add).then_inc(msg_ready, 1)
                    add_sums(wins, C2, lambda q: bank[0][:, q * C2:(q + 1) * C2], 2, n, PASS_L2)
            dve.drain()
            a2 = accv(C2)
            v.tensor_tensor(x[:, :, 0:8], x[:, :, 0:8], a2[:, :, 0:8], ALU.add)
            v.tensor_tensor(x[:, :, 8:F], x[:, :, 8:F], a2[:, :, 16:40], ALU.add)
            v.tensor_copy(dinv[:, :], a2[:, :, 40])
            dve.wait_ge(tab_sent, 48)
            dve.drain()
            layernorm()
            root_of(v.tensor_scalar(st1[:, :], dinv[:, :], 1.0, None, ALU.add))
            v.reciprocal(dinv[:, :], st1[:, :])
            dve.drain()
            v.tensor_tensor(tab(F), x[:, :, :], each(dinv[:, :], F), ALU.mult).then_inc(tab_ready, 1)
            v.memset(acc[:, 0:W * F], 0.0)
            dve.drain()
            spmm(PASS_L3A, F, 3, win_dst)

            def tw(w):
                return tabf[:, bass.ds(w * F, F)]

            v.tensor_tensor(acc[:, 0:W * F], acc[:, 0:W * F], tabf[:, 0:W * F], ALU.add)
            dve.wait_ge(tab_sent, 64)
            dve.drain()

            def y2(w, b):
                return v.tensor_scalar(yb[:, b, 0:F], acc[:, bass.ds(w * F, F)], dinv[:, bass.ds(w, 1)], None, ALU.mult)

            def h2(b):
                v.tensor_tensor(hb[:, b, :], bank[2 + b][:, 0:H2], g3b1[:, :], ALU.add)
                dve.drain()
                return v.tensor_scalar(hb[:, b, :], hb[:, b, :], 0.0, None, ALU.max)

            def z2(w, b):
                return v.tensor_scalar(tw(w), bank[6 + b][:, 0:F], dinv[:, bass.ds(w, 1)], None, ALU.mult)

            project(2, y2, z2, h2)
            v.memset(acc[:, 0:W * F], 0.0).then_inc(tab_ready, 1)
            dve.drain()
            spmm(PASS_L3B, F, 4, win_dst)
            v.tensor_tensor(acc[:, 0:W * F], acc[:, 0:W * F], tabf[:, 0:W * F], ALU.add)
            dve.drain()
            a3 = accv(F)
            v.tensor_tensor(a3, a3, each(dinv[:, :], F), ALU.mult)
            dve.drain()
            v.tensor_tensor(a3, a3, row(g3b2[:, :]), ALU.add)
            dve.drain()
            v.scalar_tensor_tensor(x[:, :, :], a3, 0.0, x[:, :, :], ALU.max, ALU.add)
            dve.wait_ge(tab_sent, 80)
            dve.drain()
            layernorm()
            v.tensor_copy(gm[:, 0, 0, 0:1], iota[:, 0:1]).then_inc(tab_ready, 1)


_INS = ['x', 'src', 'dst', 'edge_attr_3', 'edge_weight', 'node_vec1', 'L0_gnn_w', 'L0_gnn_fc_w', 'L0_gnn_fc_b',
        'L0_gnn_bias', 'L1_gnn_W', 'L1_gnn_b', 'L2_gnn_w1', 'L2_gnn_b1', 'L2_gnn_w2', 'L2_gnn_b2',
        'L3_gnn_W1', 'L3_gnn_b1', 'L3_gnn_W2', 'L3_gnn_b2']


def kernel(**inputs):
    import numpy as _np
    import concourse.bacc as _bacc
    from concourse import mybir as _mybir
    from concourse.bass_utils import run_bass_kernel_spmd as _run

    nc = _bacc.Bacc("TRN2", target_bir_lowering=False, num_devices=1)
    arrays, args = {}, {}
    for name in _INS:
        arr = _np.asarray(inputs[name])
        key = name
        if name == 'L1_gnn_W':
            arr, key = arr.T, 'L1_WT'
        arr = _np.ascontiguousarray(arr)
        arrays[f"in_{key}"] = arr
        args[key] = nc.dram_tensor(f"in_{key}", arr.shape, _mybir.dt.from_np(arr.dtype), kind="ExternalInput").ap()
    out = nc.dram_tensor("out", (N, F), _mybir.dt.float32, kind="ExternalOutput").ap()
    resnorm_gnn_kernel(nc, args, out)
    r = _run(nc, [arrays], core_ids=[0])
    return r.results[0]["out"]
```

```python
import concourse.bass as bass
import concourse.mybir as mybir
import numpy as np
from contextlib import ExitStack
from math import factorial, pi, sqrt

F32 = mybir.dt.float32
BF16 = mybir.dt.bfloat16
I32 = mybir.dt.int32
U8 = mybir.dt.uint8
ALU = mybir.AluOpType
ACT = mybir.ActivationFunctionType
AX = mybir.AxisListType

P = 128
N = 12500
F = 32
W = -(-N // P)
NW = W * P
LAST = N - (W - 1) * P
E = 400000
TE = E // P
HEADS = 4
HID = 64
H2 = 64

TILES_PER_GROUP = 2
GROUP = TILES_PER_GROUP * P
SLOTS = 4
GPS = 4
TPS = GPS * TILES_PER_GROUP
MAX_GROUPS = (E + W * (GROUP - 1)) // GROUP
ITERS = -(-MAX_GROUPS // (SLOTS * GPS))
STEPS = ITERS * SLOTS
NG = STEPS * GPS
NT = NG * TILES_PER_GROUP
ROWS = P * NT

RING = 5
RSLOTS = 5
RITERS = TE // (RING * RSLOTS)
PARTS = 5
PIT = RITERS // PARTS

PAD_KEY = 1 << 20
KEY_MASK = PAD_KEY | (P - 1)
BIG = float(2.0 ** 100)
FMAX = 3.4028234663852886e38
EPS = 1e-05

C0 = F + 1 + HEADS
CM = HEADS * (F + 1) + 1
C1 = F + 2
C2 = 41
CF = F


def _coupling():
    def cg(j1, j2, j3, m1, m2, m3):
        if m1 + m2 != m3:
            return 0.0
        f = factorial
        pre = sqrt((2 * j3 + 1) * f(j3 + j1 - j2) * f(j3 - j1 + j2) * f(j1 + j2 - j3) / f(j1 + j2 + j3 + 1))
        pre *= sqrt(f(j3 + m3) * f(j3 - m3) * f(j1 - m1) * f(j1 + m1) * f(j2 - m2) * f(j2 + m2))
        s = 0.0
        for k in range(max(0, j2 - j3 - m1, j1 - j3 + m2), min(j1 + j2 - j3, j1 - m1, j2 + m2) + 1):
            s += (-1) ** k / (f(k) * f(j1 + j2 - j3 - k) * f(j1 - m1 - k) * f(j2 + m2 - k)
                              * f(j3 - j2 + m1 + k) * f(j3 - j1 - m2 + k))
        return pre * s

    def basis(l):
        a = np.zeros((2 * l + 1, 2 * l + 1), dtype=complex)
        a[l, l] = 1.0
        for m in range(1, l + 1):
            a[l + m, l + m] = (-1) ** m / sqrt(2)
            a[l + m, l - m] = 1.0 / sqrt(2)
            a[l - m, l - m] = 1j / sqrt(2)
            a[l - m, l + m] = -1j * (-1) ** m / sqrt(2)
        return a

    def w3j(l1, l2, l3):
        w = np.zeros((2 * l1 + 1, 2 * l2 + 1, 2 * l3 + 1))
        for m1 in range(-l1, l1 + 1):
            for m2 in range(-l2, l2 + 1):
                m3 = -(m1 + m2)
                if abs(m3) <= l3:
                    w[m1 + l1, m2 + l2, m3 + l3] = (-1) ** (l1 - l2 - m3) / sqrt(2 * l3 + 1) * cg(l1, l2, l3, m1, m2, -m3)
        wr = np.einsum('abc,ma,nb,oc->mno', w.astype(complex), basis(l1).conj(), basis(l2).conj(), basis(l3).conj())
        i = int(np.argmax(np.abs(wr)))
        return np.real(wr / (wr.flat[i] / abs(wr.flat[i])))

    norm0 = sqrt(4 * pi) / sqrt(8 * 1 + 8 * 1)
    norm1 = sqrt(4 * pi) * sqrt(3.0) / sqrt(8 * 1 + 8 * 3)
    y0 = 0.5 / sqrt(pi)
    c1 = sqrt(3.0 / (4.0 * pi))
    c2b, c2c = 0.25 * sqrt(5.0 / pi), 0.25 * sqrt(15.0 / pi)
    y2 = np.array([0, 0, -c2b, 0, -c2c])
    k2 = 0.5 * float(w3j(1, 2, 1)[0, :, 0] @ y2)
    return {
        "s_f0": norm0 * y0 * float(w3j(0, 0, 0)[0, 0, 0]),
        "s_dot": norm0 * c1 * float(w3j(0, 1, 1)[0, 0, 0]),
        "v_f0": norm1 * c1 * float(w3j(1, 1, 0)[0, 0, 0]),
        "v_same": norm1 * y0 * float(w3j(1, 0, 1)[0, 0, 0]),
        "v_cross": norm1 * c1 * float(w3j(1, 1, 1)[0, 1, 2]),
        "v_quad": norm1 * k2,
    }


def resnorm_gnn_kernel(nc, a, out):
    ctx = ExitStack()
    with ctx:
        def sb(name, shape, dt=F32):
            return ctx.enter_context(nc.sbuf_tensor(name, shape, dt))

        def sem(name):
            return ctx.enter_context(nc.semaphore(name))

        def dram(name, shape):
            return nc.dram_tensor(name, shape, F32, kind="Internal").ap()

        edges_src = dram("edges_src", (E, 2))
        edges_dst = dram("edges_dst", (E, 6))
        rows_src = nc.dram_tensor("rows_src", (E, 1), I32, kind="Internal").ap()
        rows_dst = nc.dram_tensor("rows_dst", (E, 1), I32, kind="Internal").ap()
        by_src = dram("by_src", (ROWS, 2))
        by_dst = dram("by_dst", (ROWS, 6))
        staged = dram("staged", (ROWS, C0))
        tab0 = dram("tab0", (NW, C0))
        tab1 = dram("tab1", (NW, C1))
        tab2 = dram("tab2", (NW, F))
        tab3 = dram("tab3", (NW, F))
        tab4 = dram("tab4", (NW, F))
        by_src_v = by_src.rearrange("(p t) c -> p t c", p=P)
        by_dst_v = by_dst.rearrange("(p t) c -> p t c", p=P)
        staged_v = staged.rearrange("(p t) c -> p t c", p=P)

        x = sb("x", [P, W, F])
        tabx = sb("tabx", [P, W, C0])
        acc = sb("acc", [P, W * CM])
        srcs = sb("srcs", [P, TE], I32)
        dsts = sb("dsts", [P, TE], I32)
        pos = sb("pos", [P, TE])
        hot = sb("hot", [P, 2, TPS, P])
        winb = acc[:, 0:TE]
        eqm = acc[:, TE:TE + (TE + 3) // 4 + 1].bitcast(U8)[:, 0:TE]
        cum = acc[:, 4096:4096 + TE]
        fill = acc[:, 8192:8192 + 416 * 6].rearrange("p (t c) -> p t c", c=6)
        fill2 = hot[:, 0, :, :].rearrange("p t n -> p (t n)")[:, 0:416 * 2].rearrange("p (t c) -> p t c", c=2)
        FILL_T = 416
        assert NT % FILL_T == 0

        iota = sb("iota", [P, P])
        iotaw = iota[:, 0:W]
        iotap = sb("iotap", [P, 1])
        ident = sb("ident", [P, P])
        identb = sb("identb", [P, P], BF16)
        ones = sb("ones", [P, P])
        before = sb("before", [P, P])
        far = sb("far", [P, P], BF16)
        pick = sb("pick", [96, 32, P], BF16)
        hist = sb("hist", [P, W])
        start_ = sb("start_", [P, W])
        ends = sb("ends", [P, W])
        gcnt = sb("gcnt", [P, W], I32)
        endT = sb("endT", [P, 1])
        giota = acc[:, 10752:10752 + NG]
        gge = cum[:, 0:NG]
        CHUNK = TE // PARTS
        ch_attr = acc[:, 0:3 * CHUNK].rearrange("p (t c) -> p t c", c=3)
        ch_w = acc[:, 1875:1875 + CHUNK]
        ch_len = acc[:, 2500:2500 + CHUNK]
        ch_sq = acc[:, 3125:3125 + CHUNK]
        ch_pay = acc[:, 3750:3750 + 6 * CHUNK].rearrange("p (t c) -> p t c", c=6)
        pair = acc[:, 0:2 * TE].rearrange("p (t c) -> p t c", c=2)
        whb = tabx[:, :, :].rearrange("p w c -> p (w c)")
        win_src = sb("win_src", [1, NG], I32)
        win_dst = sb("win_dst", [1, NG], I32)
        posr = sb("posr", [P, RSLOTS, RING], I32)
        payr = sb("payr", [P, RSLOTS, RING, 6])

        pay = sb("pay", [P, SLOTS, TPS, 6])
        gat = sb("gat", [P, SLOTS, TPS, C0])
        keyi = sb("keyi", [P, TPS], I32)
        keyf = sb("keyf", [P, TPS])
        hotb = [hot[:, b, :, :].rearrange("p t n -> p (t n)").bitcast(BF16)[:, 0:TPS * P]
                .rearrange("p (t n) -> p t n", n=P) for b in range(2)]
        hotT = sb("hotT", [P, 2, TPS, P], BF16)
        mmax = sb("mmax", [P, W, HEADS])
        asrc = sb("asrc", [P, W, HEADS])
        nodeam = sb("nodeam", [P, W, 2 * HEADS])
        nodesp = sb("nodesp", [P, W, 3, 2 * HEADS], BF16)
        padf = sb("padf", [P, TPS])
        adm = sb("adm", [P, TPS, HEADS])
        adsp = sb("adsp", [P, 2, 3, TPS * HEADS], BF16)
        adT = sb("adT", [96, 2, P], BF16)
        red = sb("red", [P, 2, TPS, C2])
        am = sb("am", [P, TPS, 2 * HEADS])
        logit = sb("logit", [P, TPS, HEADS])
        prob = sb("prob", [P, TPS, HEADS])
        msg = sb("msg", [P, TPS, CM])
        fT = sb("fT", [P, 2, TPS, 5, 8])
        g_s = sb("g_s", [P, 2, TPS, 16])
        g_v = sb("g_v", [P, 2, TPS, 3, 16])
        rx = sb("rx", [P, 2, TPS, 5])
        tmpA = sb("tmpA", [P, TPS, 24])
        tmpB = sb("tmpB", [P, TPS, 24])
        prod = srcs[:, 0:4 * 640].bitcast(F32).rearrange("p (b t r k) -> p b t r k", b=2, t=2, k=16)
        hid = dsts[0:HID + 1, 0:2 * TPS * P].bitcast(F32).rearrange("p (b t n) -> p b t n", b=2, t=TPS)
        keyn = sb("keyn", [P, TPS])
        dT = sb("dT", [TPS, P])
        w1row = sb("w1row", [TPS, HID + 1])
        w1sel = sb("w1sel", [TPS, TPS, HID + 1])
        b1col = sb("b1col", [HID + 1, 1])
        w2raw = sb("w2raw", [HID + 1, 384])
        w2p = sb("w2p", [HID + 1, 384])
        w2t = sb("w2t", [HID + 1, 64])
        wh = sb("wh", [P, F])
        whr = tabx[:, :, :].rearrange("p w c -> p (w c)")[:, 0:F * F].rearrange("p (f o) -> p f o", o=F)
        vtmp = tabx[:, :, :].rearrange("p w c -> p (w c)")[:, F * F:2 * F * F].rearrange("p (f o) -> p f o", o=F)
        fcw = sb("fcw", [P, 2 * F])
        vrow = sb("vrow", [P, 2, HEADS, F])
        gm = sb("gm", [P, GPS, HEADS])
        fcb = sb("fcb", [P, 1])
        bias0 = sb("bias0", [P, F])
        w1T = sb("w1T", [F, F])
        bias1 = sb("bias1", [P, F])
        g3w1 = sb("g3w1", [F, H2])
        g3b1 = sb("g3b1", [P, H2])
        g3w2 = sb("g3w2", [H2, F])
        g3b2 = sb("g3b2", [P, F])
        mask = sb("mask", [P, W])
        st1 = sb("st1", [P, W])
        st2 = sb("st2", [P, W])
        dis = sb("dis", [P, W])
        dinv = sb("dinv", [P, W])
        yb = sb("yb", [P, 2, P])
        yT = sb("yT", [P, 2, P])
        hb = sb("hb", [P, 2, H2])
        hT = sb("hT", [H2, 2, P])

        banks = ctx.enter_context(nc.psum_tensor("banks", [P, 8, 512], F32))
        bank = [banks[:, b, :] for b in range(8)]

        keys_in = sem("keys_in")
        loaded = sem("loaded")
        consts = sem("consts")
        vready = sem("vready")
        histed = sem("histed")
        hsum = sem("hsum")
        ended = sem("ended")
        endedT = sem("endedT")
        bucketed = sem("bucketed")
        compared = sem("compared")
        counted = sem("counted")
        filled = sem("filled")
        fill_set = sem("fill_set")
        ranked = sem("ranked")
        normed = sem("normed")
        sq_in = sem("sq_in")
        sq_out = sem("sq_out")
        ring_full = [sem(f"ring_full{s}") for s in range(RSLOTS)]
        whr_in = sem("whr_in")
        whr_used = sem("whr_used")
        pairs_made = sem("pairs_made")
        pairs_sent = sem("pairs_sent")
        chunk_in = sem("chunk_in")
        chunk_made = sem("chunk_made")
        chunk_sent = sem("chunk_sent")
        rows_sent = [sem(f"rows_sent{p_}") for p_ in range(PARTS)]
        ring_sent = [sem(f"ring_sent{s}") for s in range(RSLOTS)]
        tab_ready = sem("tab_ready")
        tab_sent = sem("tab_sent")
        pay_in = [sem(f"pay_in{s}") for s in range(SLOTS)]
        gat_in = {p_: [sem(f"gat_in{p_}_{s}") for s in range(SLOTS)] for p_ in (0, 2, 3, 4, 5)}
        att_in = [sem(f"att_in{s}") for s in range(SLOTS)]
        staged_out = [sem(f"staged_out{s}") for s in range(SLOTS)]
        step_done = sem("step_done")
        hot_ready = sem("hot_ready")
        sums_ready = sem("sums_ready")
        tp_done = sem("tp_done")
        hotT_ready = sem("hotT_ready")
        split_ready = sem("split_ready")
        mask_ready = sem("mask_ready")
        mask_used = sem("mask_used")
        am_ready = sem("am_ready")
        logit_ready = sem("logit_ready")
        prob_ready = sem("prob_ready")
        msg_ready = sem("msg_ready")
        dT_raw = sem("dT_raw")
        dT_ready = sem("dT_ready")
        hid_raw = sem("hid_raw")
        hid_ready = sem("hid_ready")
        key_ready = sem("key_ready")
        key_used = sem("key_used")
        geo_ready = sem("geo_ready")
        r_ready = sem("r_ready")
        r_used = sem("r_used")
        y_ready = sem("y_ready")
        yT_raw = sem("yT_raw")
        yT_ready = sem("yT_ready")
        z_ready = sem("z_ready")
        z_used = sem("z_used")
        h_ready = sem("h_ready")
        hT_raw = sem("hT_raw")
        hT_ready = sem("hT_ready")
        written = sem("written")

        block = ctx.enter_context(nc.Block())

        def node_rows(t):
            return t.rearrange("(w p) c -> p w c", p=P)

        def window_tail(name):
            return a[name][(W - 1) * P:N, :]

        PASS_MAX, PASS_ATT, PASS_L1, PASS_L2, PASS_L3A, PASS_L3B = range(6)
        KC = {PASS_MAX: 2, PASS_ATT: 2, PASS_L1: 2, PASS_L2: 6, PASS_L3A: 6, PASS_L3B: 6}
        GC = {PASS_MAX: C0, PASS_L1: C1, PASS_L2: F, PASS_L3A: F, PASS_L3B: F}
        TAB = {PASS_MAX: tab0, PASS_L1: tab1, PASS_L2: tab2, PASS_L3A: tab3, PASS_L3B: tab4}
        LIST = {PASS_MAX: by_src_v, PASS_ATT: by_src_v, PASS_L1: by_src_v,
                PASS_L2: by_dst_v, PASS_L3A: by_dst_v, PASS_L3B: by_dst_v}
        GATHERS = [PASS_MAX, PASS_L1, PASS_L2, PASS_L3A, PASS_L3B]

        def payv(s, pas):
            return pay[:, s, :, :].rearrange("p t c -> p (t c)")[:, 0:TPS * KC[pas]].rearrange(
                "p (t c) -> p t c", c=KC[pas])

        def gatv(s, c):
            return gat[:, s, :, :].rearrange("p t c -> p (t c)")[:, 0:TPS * c].rearrange("p (t c) -> p t c", c=c)

        def pay_count(pas, i):
            return (i + (pas * ITERS + 1)) * 16

        def gat_count(pas, i):
            return i * (16 * TPS) + 16 * TPS

        PE_ENGINE, DVE_ENGINE = mybir.EngineType.PE, mybir.EngineType.DVE

        def group_windows(eng, which, win_tab, n):
            _, vals = nc.values_load_multi_w_load_instructions(
                win_tab[0:1, bass.ds(n * GPS, GPS)], engines=(which,), min_val=0, max_val=W - 1,
                skip_runtime_bounds_check_because="the table is clamped to W - 1 where it is made")
            return vals

        FILL_DMAS = 2 * (NT // FILL_T)
        sorted_dmas = 16 * RING

        @block.sync
        def _(sp):
            def load(dst, src):
                sp.dma_start(dst, src).then_inc(loaded, 16)

            sp.dma_start(srcs[:, :], a["src"].rearrange("(p t) -> p t", p=P)).then_inc(keys_in, 16)
            sp.dma_start(dsts[:, :], a["dst"].rearrange("(p t) -> p t", p=P)).then_inc(keys_in, 16)
            load(wh[:, :], a["L0_gnn_w"].rearrange("h f o -> (h f) o"))
            load(fcw[:, :], a["L0_gnn_fc_w"].to_broadcast([P, 2 * F]))
            load(fcb[:, :], a["L0_gnn_fc_b"].rearrange("(a b) -> a b", a=1).to_broadcast([P, 1]))
            load(bias0[:, :], a["L0_gnn_bias"].rearrange("(a b) -> a b", a=1).to_broadcast([P, F]))
            load(w1T[:, :], a["L1_WT"])
            load(bias1[:, :], a["L1_gnn_b"].rearrange("(a b) -> a b", a=1).to_broadcast([P, F]))
            load(g3w1[:, :], a["L3_gnn_W1"])
            load(g3b1[:, :], a["L3_gnn_b1"].rearrange("(a b) -> a b", a=1).to_broadcast([P, H2]))
            load(g3w2[:, :], a["L3_gnn_W2"])
            load(g3b2[:, :], a["L3_gnn_b2"].rearrange("(a b) -> a b", a=1).to_broadcast([P, F]))
            load(w1row[:, 0:HID], a["L2_gnn_w1"].to_broadcast([TPS, HID]))
            load(w2raw[0:HID, :], a["L2_gnn_w2"])
            load(w2raw[HID:HID + 1, :], a["L2_gnn_b2"].rearrange("(a b) -> a b", a=1))
            sp.wait_ge(fill_set, 1)
            load(x[:, 0:W - 1, :], a["x"][0:(W - 1) * P, :].rearrange("(w p) c -> p w c", p=P))
            load(x[0:LAST, W - 1, :], a["x"][(W - 1) * P:N, :])
            with nc.allow_non_contiguous_dma(reason="one value per node"):
                load(mask[:, 0:W - 1], a["node_vec1"][0:(W - 1) * P, :].rearrange("(w p) c -> p (w c)", p=P))
                load(mask[0:LAST, W - 1:W], a["node_vec1"][(W - 1) * P:N, :])
                load(b1col[0:HID, 0:1], a["L2_gnn_b1"].rearrange("(h c) -> h c", c=1))
            for f in range(NT // FILL_T):
                sp.dma_start(by_dst_v[:, f * FILL_T:(f + 1) * FILL_T, :], fill[:, :, :]).then_inc(filled, 16)
            for f in range(NT // FILL_T):
                sp.dma_start(by_src_v[:, f * FILL_T:(f + 1) * FILL_T, :], fill2[:, :, :]).then_inc(filled, 16)
            sp.wait_ge(pairs_made, 1)
            sp.dma_start(edges_src.rearrange("(p t) c -> p t c", p=P), pair).then_inc(pairs_sent, 16)
            def ring_loads(k):
                rows, edges, c = ((rows_src, edges_src, 2), (rows_dst, edges_dst, 6))[k]
                rows_v = rows.rearrange("(p t) c -> p (t c)", p=P)

                def ring_step(i, first):
                    for s in range(RSLOTS):
                        cols = bass.ds(i * (RSLOTS * RING) + s * RING, RING)
                        if not first:
                            sp.wait_ge(ring_sent[s], i * sorted_dmas + sorted_dmas * RITERS * k)
                        sp.dma_start(posr[:, s, :], rows_v[:, cols]).then_inc(ring_full[s], 16)
                        sp.dma_start(payr[:, s, :, :].rearrange("p t c -> p (t c)")[:, 0:RING * c].rearrange("p (t c) -> p t c", c=c),
                                     edges.rearrange("(p t) c -> p t c", p=P)[:, cols, :]).then_inc(ring_full[s], 16)

                if k:
                    sp.wait_ge(chunk_sent, 16 * PARTS)
                    for s in range(RSLOTS):
                        sp.wait_ge(ring_sent[s], sorted_dmas * RITERS * k)
                else:
                    sp.wait_ge(pairs_sent, 16)
                for part in range(PARTS):
                    sp.wait_ge(rows_sent[part], 16 * (k + 1))
                    if part == 0:
                        ring_step(0, True)
                    with sp.Fori(part * PIT + (part == 0), (part + 1) * PIT) as i:
                        ring_step(i, False)

            def send_table(k, dst, c):
                sp.wait_ge(tab_ready, k + 1)
                view = tabx[:, :, :].rearrange("p w c -> p (w c)")[:, 0:W * c].rearrange("p (w c) -> p w c", c=c)
                sp.dma_start(node_rows(dst), view).then_inc(tab_sent, 16)

            def edge_loads(pas):
                with sp.Fori(0, ITERS) as i:
                    for s in range(SLOTS):
                        tiles = bass.ds(i * (SLOTS * TPS) + s * TPS, TPS)
                        sp.wait_ge(step_done, i * SLOTS + (pas * STEPS + s + 1))
                        sp.dma_start(payv(s, pas), LIST[pas][:, tiles, :]).then_inc(pay_in[s], 16)

            ring_loads(0)
            send_table(0, tab0, C0)
            sp.wait_ge(bucketed, 1)
            edge_loads(PASS_MAX)
            ring_loads(1)
            send_table(1, tab1, C1)
            edge_loads(PASS_L1)
            send_table(2, tab2, F)
            sp.wait_ge(bucketed, 2)
            edge_loads(PASS_L2)
            send_table(3, tab3, F)
            edge_loads(PASS_L3A)
            send_table(4, tab4, F)
            edge_loads(PASS_L3B)
            sp.wait_ge(tab_ready, 6)
            sp.dma_start(out[0:(W - 1) * P, :].rearrange("(w p) c -> p w c", p=P), x[:, 0:W - 1, :]).then_inc(written, 16)
            sp.dma_start(out[(W - 1) * P:N, :], x[0:LAST, W - 1, :]).then_inc(written, 16)
            sp.wait_ge(written, 32)
            sp.wait_ge(tab_sent, 16 * 5)
            sp.wait_ge(filled, 16 * FILL_DMAS)
            for s in range(SLOTS):
                sp.wait_ge(staged_out[s], 16 * ITERS)

        N_LOADS = 18

        @block.gpsimd
        def _(pool):
            g = nc.gpsimd
            g.iota(iota[:, :], pattern=[[1, P]], base=0, channel_multiplier=0,
                   allow_small_or_imprecise_dtypes=True)
            g.iota(giota, pattern=[[1, NG]], base=0, channel_multiplier=0,
                   allow_small_or_imprecise_dtypes=True)
            g.memset(ones[:, :], 1.0)
            g.memset(ident[:, :], 0.0)
            g.memset(before[:, :], 0.0)
            g.memset(far[:, :], -BIG)
            g.memset(pick[:, :, :], 0.0)
            pool.drain()
            g.affine_select(out=ident[:, :], in_=ident[:, :], compare_op=ALU.not_equal, fill=1.0,
                            base=0, pattern=[[-1, P]], channel_multiplier=1)
            g.affine_select(out=before[:, :], in_=before[:, :], compare_op=ALU.is_ge, fill=1.0,
                            base=0, pattern=[[-1, P]], channel_multiplier=1)
            g.affine_select(out=far[:, :], in_=far[:, :], compare_op=ALU.not_equal, fill=0.0,
                            base=0, pattern=[[-1, P]], channel_multiplier=1)
            for k in range(3):
                g.affine_select(out=pick[:, :, :], in_=pick[:, :, :], compare_op=ALU.not_equal, fill=1.0,
                                base=-32 * k, pattern=[[-1, 32], [0, P]], channel_multiplier=1)
                pool.drain()
            g.tensor_copy(identb[:, :], ident[:, :]).then_inc(consts, 1)
            pool.wait_ge(loaded, 16 * N_LOADS)
            g.memset(w1row[:, HID:HID + 1], 0.0)
            pool.drain()
            for t in range(TPS):
                g.tensor_copy(w1sel[:, t, :], w1row[:, :])
            pool.drain()
            g.affine_select(out=w1sel[:, :, :], in_=w1sel[:, :, :], compare_op=ALU.is_equal, fill=0.0,
                            base=0, pattern=[[-1, TPS], [0, HID + 1]], channel_multiplier=1).then_inc(consts, 1)

            def bucket(k, dst, c):
                pool.wait_ge(filled, 16 * FILL_DMAS)
                with pool.Fori(0, RITERS) as i:
                    for s in range(RSLOTS):
                        pool.wait_ge(ring_full[s], i * 32 + (32 * RITERS * k + 32))
                        pool.nop(nofuse=True)
                        pr = payr[:, s, :, :].rearrange("p t c -> p (t c)")
                        for j in range(RING):
                            pool.indirect_dma_start(
                                out=dst, out_offset=bass.IndirectOffsetOnAxis(ap=posr[:, s, j:j + 1], axis=0),
                                in_=pr[:, j * c:(j + 1) * c], in_offset=None).then_inc(ring_sent[s], 16)
                for s in range(RSLOTS):
                    pool.wait_ge(ring_sent[s], sorted_dmas * RITERS * (k + 1))
                pool.sem_inc(bucketed, 1)

            def gather(pas):
                def gather_step(i, first):
                    for s in range(SLOTS):
                        pool.wait_ge(pay_in[s], pay_count(pas, i))
                        if pas == PASS_MAX and not first:
                            pool.wait_ge(staged_out[s], i * 16)
                        pool.nop(nofuse=True)
                        for t in range(TPS):
                            pool.indirect_dma_start(
                                out=gatv(s, GC[pas])[:, t, :], out_offset=None, in_=TAB[pas],
                                in_offset=bass.IndirectOffsetOnAxis(ap=payv(s, pas)[:, t, 1:2].bitcast(I32), axis=0),
                            ).then_inc(gat_in[pas][s], 16)

                gather_step(0, True)
                with pool.Fori(1, ITERS) as i:
                    gather_step(i, False)

            bucket(0, by_src, 2)
            pool.wait_ge(tab_sent, 16)
            gather(PASS_MAX)
            bucket(1, by_dst, 6)
            for k, pas in enumerate(GATHERS[1:]):
                pool.wait_ge(tab_sent, 16 * (k + 2))
                gather(pas)

        @block.scalar
        def _(act):
            s_ = nc.scalar
            roots = [0]

            def root(dst, src):
                roots[0] += 1
                act.wait_ge(sq_in, roots[0])
                s_.activation(dst, src, ACT.Sqrt).then_inc(sq_out, 1)

            act.sem_inc(step_done, SLOTS)

            def send_rows(k, rows):
                for part in range(PARTS):
                    cols = slice(part * CHUNK, (part + 1) * CHUNK)
                    act.wait_ge(ranked, PARTS * k + part + 1)
                    act.dma_start(rows.rearrange("(p t) c -> p (t c)", p=P)[:, cols],
                                  pos[:, cols].bitcast(I32)).then_inc(rows_sent[part], 16)

            send_rows(0, rows_src)
            for h in range(HEADS):
                act.wait_ge(whr_used, h + 1)
                act.dma_start(whr, a["L0_gnn_w"][h:h + 1, :, :].to_broadcast([P, F, F])).then_inc(whr_in, 16)
            attr_v = a["edge_attr_3"].rearrange("(p t) c -> p t c", p=P)
            w_v = a["edge_weight"].rearrange("(p t) -> p t", p=P)
            for k in range(PARTS):
                cols = slice(k * CHUNK, (k + 1) * CHUNK)
                if k:
                    act.wait_ge(chunk_made, k)
                act.dma_start(ch_attr, attr_v[:, cols, :]).then_inc(chunk_in, 16)
                act.dma_start(ch_w, w_v[:, cols]).then_inc(chunk_in, 16)
                root(ch_len, ch_sq)
                act.wait_ge(chunk_made, k + 1)
                act.dma_start(edges_dst.rearrange("(p t) c -> p t c", p=P)[:, cols, :], ch_pay).then_inc(chunk_sent, 16)

            send_rows(1, rows_dst)
            with act.Fori(0, ITERS) as i:
                for s in range(SLOTS):
                    n = i * SLOTS + s
                    act.wait_ge(gat_in[PASS_MAX][s], gat_count(PASS_MAX, i))
                    act.dma_start(staged_v[:, bass.ds(i * (SLOTS * TPS) + s * TPS, TPS), :],
                                  gat[:, s, :, :]).then_inc(staged_out[s], 16)
                    act.wait_ge(step_done, n + (PASS_MAX * STEPS + SLOTS - 1))
                    act.wait_ge(tp_done, n + 1)
                    s_.copy(adT[:, s % 2, :], bank[6][0:96, 0:64].bitcast(BF16))
                    s_.copy(hotT[:, s % 2, :, :].rearrange("p t n -> p (t n)"),
                            bank[4].bitcast(BF16)).then_inc(hotT_ready, 1)
            for s in range(SLOTS):
                act.wait_ge(staged_out[s], 16 * ITERS)

            def attention_loads(i, s):
                tiles = bass.ds(i * (SLOTS * TPS) + s * TPS, TPS)
                act.wait_ge(step_done, i * SLOTS + (PASS_ATT * STEPS + s + 1))
                act.dma_start(payv(s, PASS_ATT), by_src_v[:, tiles, :]).then_inc(pay_in[s], 16)
                act.dma_start(gat[:, s, :, :], staged_v[:, tiles, :]).then_inc(att_in[s], 16)

            def attention_transposes(n, s):
                act.wait_ge(tp_done, n + (STEPS + 1))
                for b in range(2):
                    last = s_.copy(hotT[:, s % 2, 4 * b:4 * b + 4, :].rearrange("p t n -> p (t n)"), bank[4 + b])
                last.then_inc(hotT_ready, 1)

            def attention_step(i, s, final):
                n = i * SLOTS + s
                if not (final and s >= 2):
                    attention_loads(i + (s + 2) // SLOTS, (s + 2) % SLOTS)
                act.wait_ge(logit_ready, n + 1)
                s_.activation(prob[:, :, :], logit[:, :, :], ACT.Exp).then_inc(prob_ready, 1)
                if not (final and s == SLOTS - 1):
                    act.wait_ge(am_ready, n + 1)
                    attention_transposes(n + 1, s + 1)

            attention_loads(0, 0)
            attention_loads(0, 1)
            attention_transposes(0, 0)
            with act.Fori(0, ITERS - 1) as i:
                for s in range(SLOTS):
                    attention_step(i, s, False)
            for s in range(SLOTS):
                attention_step(ITERS - 1, s, True)

            def project(k, m, second):
                with act.Fori(0, W // 2) as j:
                    for b in range(2):
                        act.wait_ge(yT_raw, j * 2 + (k * W + b + 1))
                        s_.copy(yT[0:m, b, :], bank[b][0:m, 0:P]).then_inc(yT_ready, 1)
                        if second:
                            act.wait_ge(hT_raw, j * 2 + (b + 1))
                            s_.copy(hT[:, b, :], bank[4 + b][0:H2, 0:P]).then_inc(hT_ready, 1)

            project(0, P, False)
            root(st2[:, :], st2[:, :])
            root(st1[:, :], st1[:, :])
            project(1, F, False)
            root(st2[:, :], st2[:, :])
            def radial_round(i, first):
                for s in range(SLOTS):
                    n = i * SLOTS + s
                    b = s % 2
                    act.wait_ge(dT_raw, n + 1)
                    s_.copy(dT[:, :], bank[7][0:TPS, 0:P]).then_inc(dT_ready, 1)
                    if not first or s >= 2:
                        act.wait_ge(msg_ready, n + (STEPS - 1))
                    act.wait_ge(gat_in[PASS_L2][s], gat_count(PASS_L2, i))
                    fv = gatv(s, F)
                    fv1 = fv[:, :, 8:32].rearrange("p t (v i) -> p t i v", i=3)
                    s_.copy(fT[:, b, :, 0:3, :], fv1)
                    s_.copy(fT[:, b, :, 3:5, :], fv1[:, :, 0:2, :])
                    s_.copy(g_v[:, b, :, :, 0:8], fv1)
                    s_.copy(g_s[:, b, :, 0:8], fv[:, :, 0:8])
                    s_.copy(rx[:, b, :, 0:3], payv(s, PASS_L2)[:, :, 3:6])
                    s_.copy(rx[:, b, :, 3:5], payv(s, PASS_L2)[:, :, 3:5]).then_inc(geo_ready, 1)
                    act.wait_ge(step_done, n + (PASS_L2 * STEPS + SLOTS - 1))
                    act.wait_ge(key_ready, n + 1)
                    for t in range(TPS):
                        last = s_.activation(hot[:, b, t, :], iota[:, :], ACT.Abs, bias=keyn[:, t:t + 1])
                    last.then_inc(key_used, 1)
                    act.wait_ge(key_used, n + 2)
                    s_.activation(hot[:, b, :, :], hot[:, b, :, :], ACT.Relu, bias=ones[:, 0:1], scale=-1.0).then_inc(hot_ready, 1)
                    act.wait_ge(hid_raw, n + 1)
                    for c in range(2):
                        last = s_.activation(hid[:, b, 4 * c:4 * c + 4, :].rearrange("p t n -> p (t n)"),
                                             bank[5 + c][0:HID + 1, :], ACT.Relu, bias=b1col[:, :])
                    last.then_inc(hid_ready, 1)

            radial_round(0, True)
            with act.Fori(1, ITERS) as i:
                radial_round(i, False)
            root(st2[:, :], st2[:, :])
            root(st1[:, :], st1[:, :])
            project(2, F, True)
            root(st2[:, :], st2[:, :])

        @block.tensor
        def _(pe):
            t_ = nc.tensor
            pe.wait_ge(consts, 2)

            def bucket_sums(k):
                pe.wait_ge(histed, k + 1)
                t_.matmul(bank[0][:, 0:W], before[:, :], hist[:, :], start=True, stop=True)
                t_.matmul(bank[0][:, P:P + W], ones[:, :], hist[:, :], start=True, stop=True).then_inc(hsum, 1)
                pe.wait_ge(ended, k + 1)
                t_.transpose(bank[1][0:W, 0:P], ends[:, :], ident[:, :]).then_inc(endedT, 1)
                pe.wait_ge(compared, k + 1)
                q = NG // 4
                for b in range(4):
                    last = t_.matmul(bank[2 + b][0:1, 0:q], ones[0:W, 0:1], gge[0:W, b * q:(b + 1) * q],
                                     start=True, stop=True)
                last.then_inc(counted, 1)

            bucket_sums(0)
            bucket_sums(1)

            def group_sums(hb_, rows, c, where):
                for q in range(GPS):
                    for h in range(TILES_PER_GROUP):
                        t = q * TILES_PER_GROUP + h
                        last = t_.matmul(where(q), hot[:, hb_, t, :], rows(t), start=(h == 0), stop=(h == TILES_PER_GROUP - 1))
                last.then_inc(sums_ready, 1)

            def max_transposes(n, s):
                pe.wait_ge(split_ready, n + 1)
                pe.nop(nofuse=True)
                t_.transpose(bank[6][0:96, 0:64].bitcast(BF16), adsp[:, s % 2, :, :].rearrange("p k c -> p (k c)"), identb[:, :])
                for t in range(TPS):
                    last = t_.transpose(bank[4][:, 64 * t:64 * t + 64].bitcast(BF16), hotb[s % 2][:, t, :], identb[:, :])
                last.then_inc(tp_done, 1)

            def max_step(i, s, final):
                n = i * SLOTS + s
                pe.wait_ge(hotT_ready, n + 1)
                for q in range(GPS):
                    if q == 2 and not (final and s == SLOTS - 1):
                        max_transposes(n + 1, s + 1)
                    pe.wait_ge(mask_used, n * GPS + (q + 1))
                    for h in range(TILES_PER_GROUP):
                        t = q * TILES_PER_GROUP + h
                        dst = bank[2 * (q % 2) + h]
                        hT_b = hotT[:, s % 2, t:t + 1, :].to_broadcast([P, HEADS, P])
                        t_.matmul(dst.rearrange("p (h e) -> p h e", h=HEADS), far[:, :], hT_b,
                                  start=True, stop=False, skip_group_check=True)
                        for hd in range(HEADS):
                            last = t_.matmul(dst[:, hd * P:(hd + 1) * P], pick[:, t * HEADS + hd, :], adT[:, s % 2, :],
                                             start=False, stop=(hd == HEADS - 1), skip_group_check=True)
                    last.then_inc(mask_ready, 1)

            max_transposes(0, 0)
            with pe.Fori(0, ITERS - 1) as i:
                for s in range(SLOTS):
                    max_step(i, s, False)
            for s in range(SLOTS):
                max_step(ITERS - 1, s, True)

            def att_transposes(n, s):
                pe.wait_ge(hot_ready, n + 1)
                for t in range(TPS):
                    last = t_.transpose(bank[4 + t // 4][:, (t % 4) * P:(t % 4 + 1) * P], hot[:, s % 2, t, :], ident[:, :])
                last.then_inc(tp_done, 1)

            def att_step(i, s, final):
                n = i * SLOTS + s
                wins = group_windows(pe, PE_ENGINE, win_src, n)
                pe.wait_ge(hotT_ready, n + (STEPS + 1))
                flat = nodesp[:, :, :, :].rearrange("p w k c -> p (w k c)")
                for t in range(TPS):
                    last = t_.matmul(bank[6][:, 24 * t:24 * t + 24], hotT[:, s % 2, t, :],
                                     flat[:, bass.ds(wins[t // TILES_PER_GROUP] * 24, 24)], start=True, stop=True)
                last.then_inc(am_ready, 1)
                if not (final and s == SLOTS - 1):
                    att_transposes(n + 1, s + 1)
                pe.wait_ge(msg_ready, n + 1)
                group_sums(s % 2, lambda t: msg[:, t, :], CM, lambda q: bank[q // 2][:, (q % 2) * CM:(q % 2 + 1) * CM])

            att_transposes(0, 0)
            with pe.Fori(0, ITERS - 1) as i:
                for s in range(SLOTS):
                    att_step(i, s, False)
            for s in range(SLOTS):
                att_step(ITERS - 1, s, True)

            def project(k, m, w_, mo, second):
                with pe.Fori(0, W // 2) as j:
                    for b in range(2):
                        n = j * 2 + b
                        pe.wait_ge(y_ready, n + (k * W + 1))
                        t_.transpose(bank[b][0:m, 0:P], yb[:, b, 0:m], ident[:, :]).then_inc(yT_raw, 1)
                        pe.wait_ge(yT_ready, n + (k * W + 1))
                        t_.matmul(bank[2 + b][:, 0:mo], yT[0:m, b, :], w_, start=True, stop=True).then_inc(z_ready, 1)
                        if second is not None:
                            pe.wait_ge(h_ready, n + 1)
                            pe.nop(nofuse=True)
                            t_.transpose(bank[4 + b][0:H2, 0:P], hb[:, b, :], ident[:, :]).then_inc(hT_raw, 1)
                            pe.wait_ge(hT_ready, n + 1)
                            t_.matmul(bank[6 + b][:, 0:F], hT[:, b, :], second, start=True, stop=True).then_inc(z_ready, 1)

            def spmm(pas, c, hot_base):
                with pe.Fori(0, ITERS) as i:
                    for s in range(SLOTS):
                        pe.wait_ge(hot_ready, i * SLOTS + (hot_base * STEPS + s + 1))
                        pe.wait_ge(gat_in[pas][s], gat_count(pas, i))
                        group_sums(s % 2, lambda t: gatv(s, c)[:, t, :], c, lambda q: bank[s % 2][:, q * c:(q + 1) * c])

            project(0, P, wh[:, :], F, None)
            spmm(PASS_L1, C1, 1)
            project(1, F, w1T[:, :], F, None)
            def weight_rows(n, i, s):
                pe.wait_ge(pay_in[s], pay_count(PASS_L2, i))
                pe.nop(nofuse=True)
                t_.transpose(bank[7][0:TPS, 0:P], payv(s, PASS_L2)[:, :, 2], ident[:, :]).then_inc(dT_raw, 1)

            def hidden(n, half):
                pe.wait_ge(dT_ready, n + 1)
                for t in range(4 * half, 4 * half + 4):
                    last = t_.matmul(bank[5 + t // 4][0:HID + 1, (t % 4) * P:(t % 4 + 1) * P],
                                     w1sel[:, t, :], dT[:, :], start=True, stop=True)
                if half:
                    last.then_inc(hid_raw, 1)

            def radial_sums(n, s):
                pe.wait_ge(hot_ready, n + (2 * STEPS + 1))
                pe.wait_ge(msg_ready, n + (STEPS + 1))
                group_sums(s % 2, lambda t: red[:, s % 2, t, :], C2, lambda q: bank[0][:, q * C2:(q + 1) * C2])

            def radial_step(i, s, first, more):
                n = i * SLOTS + s
                for p in range(TPS // 2):
                    if p == 0:
                        pe.wait_ge(hid_ready, n + 1)
                    pe.wait_ge(r_used, n * (TPS // 2) + (p + 1))
                    for h in range(2):
                        last = t_.matmul(bank[1 + 2 * (p % 2) + h][:, 0:384], hid[:, s % 2, 2 * p + h, :], w2p[:, :],
                                         start=True, stop=True)
                    last.then_inc(r_ready, 1)
                    if more and p == 0:
                        weight_rows(n + 1, i + (s + 1) // SLOTS, (s + 1) % SLOTS)
                    if p == 1 and not first:
                        radial_sums(n - 1, (s - 1) % SLOTS)
                    if more and p >= 2:
                        hidden(n + 1, p - 2)

            weight_rows(0, 0, 0)
            hidden(0, 0)
            hidden(0, 1)
            for s in range(SLOTS):
                radial_step(0, s, s == 0, True)
            with pe.Fori(1, ITERS - 1) as i:
                for s in range(SLOTS):
                    radial_step(i, s, False, True)
            for s in range(SLOTS):
                radial_step(ITERS - 1, s, False, s < SLOTS - 1)
            radial_sums(STEPS - 1, SLOTS - 1)
            spmm(PASS_L3A, F, 3)
            project(2, F, g3w1[:, :], H2, g3w2[:, :])
            spmm(PASS_L3B, F, 4)

        @block.vector
        def _(dve):
            v = nc.vector
            tabf = tabx[:, :, :].rearrange("p w c -> p (w c)")

            def tab(c):
                return tabf[:, 0:W * c].rearrange("p (w c) -> p w c", c=c)

            def accv(c):
                return acc[:, 0:W * c].rearrange("p (w c) -> p w c", c=c)

            def each(col, c):
                return col.rearrange("p (w a) -> p w a", a=1).to_broadcast([P, W, c])

            def row(vec, c=F):
                return vec.rearrange("p (a c) -> p a c", a=1).to_broadcast([P, W, c])

            dve.sem_inc(mask_used, 2)
            dve.sem_inc(r_used, 2)
            v.memset(fill[:, :, 0:1].bitcast(I32), PAD_KEY)
            v.memset(fill[:, :, 1:3], 0.0)
            v.memset(fill[:, :, 3:6], 1.0)
            v.memset(fill2[:, :, 0:1].bitcast(I32), PAD_KEY)
            v.memset(fill2[:, :, 1:2], 0.0)
            v.memset(x[:, W - 1, :], 0.0)
            v.memset(mask[:, :], 0.0)
            v.memset(b1col[:, :], 1.0)
            v.memset(mmax[:, :, :], -BIG)
            v.memset(red[:, :, :, :], 1.0)
            v.memset(msg[:, :, CM - 1:CM], 1.0).then_inc(fill_set, 1)
            dve.wait_ge(keys_in, 32)
            v.tensor_copy(pair[:, :, 0].bitcast(I32), srcs[:, :])
            v.tensor_copy(pair[:, :, 1].bitcast(I32), dsts[:, :]).then_inc(pairs_made, 1)
            dve.wait_ge(pairs_sent, 16)
            dve.wait_ge(consts, 1)

            def rank(k, key, win_tab):
                v.tensor_scalar(cum.bitcast(I32), key[:, :], 7, None, ALU.logical_shift_right)
                dve.drain()
                v.tensor_copy(winb, cum.bitcast(I32))
                dve.drain()
                with dve.Fori(0, W) as w:
                    v.tensor_scalar(cum, winb, iota[:, bass.ds(w, 1)], None, ALU.is_equal, ALU.add,
                                    accum_out=hist[:, bass.ds(w, 1)])
                    dve.drain()
                v.tensor_copy(start_[:, :], hist[:, :]).then_inc(histed, 1)
                dve.wait_ge(hsum, k + 1)
                v.tensor_scalar(gcnt[:, :], bank[0][:, P:P + W], float(GROUP - 1), None, ALU.add)
                dve.drain()
                v.tensor_scalar(gcnt[:, :], gcnt[:, :], GROUP.bit_length() - 1, None, ALU.logical_shift_right)
                dve.drain()
                v.tensor_copy(hist[:, :], gcnt[:, :])
                dve.drain()
                v.tensor_tensor_scan(ends[:, :], ones[:, 0:W], hist[:, :], 0.0, ALU.mult, ALU.add)
                dve.drain()
                v.tensor_tensor(start_[:, :], ends[:, :], hist[:, :], ALU.subtract).then_inc(ended, 1)
                dve.drain()
                v.tensor_scalar(start_[:, :], start_[:, :], float(GROUP), None, ALU.mult)
                dve.drain()
                v.tensor_tensor(start_[:, :], start_[:, :], bank[0][:, 0:W], ALU.add)
                dve.wait_ge(endedT, k + 1)
                v.tensor_copy(endT[0:W, :], bank[1][0:W, 0:1])
                dve.drain()
                v.tensor_scalar(gge[0:W, :], giota[0:W, :], endT[0:W, :], None, ALU.is_ge).then_inc(compared, 1)
                dve.wait_ge(counted, k + 1)
                q = NG // 4
                for b in range(4):
                    v.tensor_scalar(win_tab[:, b * q:(b + 1) * q], bank[2 + b][0:1, 0:q], float(W - 1), None, ALU.min)
                for part in range(PARTS):
                    cols = slice(part * CHUNK, (part + 1) * CHUNK)
                    win_, eq_, cum_, pos_ = winb[:, cols], eqm[:, 0:CHUNK], cum[:, 0:CHUNK], pos[:, cols]
                    tmp_ = cum[:, CHUNK:2 * CHUNK]
                    with dve.Fori(0, W) as w:
                        v.tensor_scalar(eq_, win_, iota[:, bass.ds(w, 1)], None, ALU.is_equal)
                        dve.drain()
                        v.tensor_tensor_scan(cum_, eq_, eq_, start_[:, bass.ds(w, 1)], ALU.add, ALU.max)
                        dve.drain()
                        v.copy_predicated(pos_, eq_, cum_)
                        v.tensor_copy(start_[:, bass.ds(w, 1)], cum_[:, CHUNK - 1:CHUNK])
                        dve.drain()
                    v.tensor_scalar(cum_.bitcast(I32), pos_, -1.0, None, ALU.add)
                    dve.drain()
                    v.tensor_scalar(tmp_.bitcast(I32), cum_.bitcast(I32), 7, None, ALU.logical_shift_right)
                    v.tensor_scalar(pos_.bitcast(I32), cum_.bitcast(I32), P - 1, None, ALU.bitwise_and)
                    dve.drain()
                    v.tensor_copy(cum_, pos_.bitcast(I32))
                    dve.drain()
                    v.scalar_tensor_tensor(pos_.bitcast(I32), cum_, float(NT), tmp_.bitcast(I32),
                                           ALU.mult, ALU.add).then_inc(ranked, 1)
                    dve.drain()

            rank(0, srcs, win_src)

            dve.wait_ge(loaded, 16 * N_LOADS)

            dve.sem_inc(whr_used, 1)
            for h in range(HEADS):
                dve.wait_ge(whr_in, 16 * (h + 1))
                for k in range(2):
                    v.tensor_tensor(vtmp, whr, fcw[:, k * F:(k + 1) * F].rearrange("p (a c) -> p a c", a=1)
                                    .to_broadcast([P, F, F]), ALU.mult)
                    dve.drain()
                    last = v.tensor_reduce(vrow[:, k, h, :], vtmp, AX.X, ALU.add)
                    dve.drain()
                v.tensor_copy(gm[:, 0, 0:1], iota[:, 0:1]).then_inc(whr_used, 1)

            for k in range(PARTS):
                cols = slice(k * CHUNK, (k + 1) * CHUNK)
                dve.wait_ge(chunk_in, 32 * (k + 1))
                if k:
                    dve.wait_ge(chunk_sent, 16 * k)
                v.tensor_copy(ch_pay[:, :, 0].bitcast(I32), dsts[:, cols])
                v.tensor_copy(ch_pay[:, :, 1].bitcast(I32), srcs[:, cols])
                v.tensor_copy(ch_pay[:, :, 2], ch_w)
                v.tensor_tensor(ch_pay[:, :, 3:6], ch_attr, ch_attr, ALU.mult)
                dve.drain()
                v.tensor_reduce(ch_sq, ch_pay[:, :, 3:6], AX.X, ALU.add).then_inc(sq_in, 1)
                dve.wait_ge(sq_out, k + 1)
                v.reciprocal(ch_sq, ch_len)
                dve.drain()
                for c in range(3):
                    v.tensor_tensor(ch_pay[:, :, 3 + c], ch_attr[:, :, (c + 1) % 3], ch_sq, ALU.mult)
                dve.drain()
                v.tensor_copy(gm[:, 0, 0:1], iota[:, 0:1]).then_inc(chunk_made, 1)
            dve.wait_ge(chunk_sent, 16 * PARTS)

            cp = _coupling()
            q_ = w2p[:, 0:256].rearrange("p (u k) -> p u k", k=16)
            ab = w2p[:, 256:384].rearrange("p (u k) -> p u k", k=16)
            blk = [w2raw[:, 64 * b:64 * b + 64].rearrange("p (u v) -> p u v", v=8) for b in range(3)]
            vec = w2raw[:, 192:384].rearrange("p (u v k) -> p u v k", v=8, k=3)
            w2tv = w2t[:, :].rearrange("p (u v) -> p u v", v=8)
            v.tensor_scalar(q_[:, 0:8, 0:8], blk[0], cp["s_f0"], None, ALU.mult)
            v.tensor_scalar(q_[:, 0:8, 8:16], blk[1], cp["s_dot"], None, ALU.mult)
            v.tensor_scalar(q_[:, 8:16, 0:8], blk[2], cp["v_f0"], None, ALU.mult)
            v.tensor_scalar(q_[:, 8:16, 8:16], vec[:, :, :, 2], 3.0 * cp["v_quad"], None, ALU.mult)
            v.tensor_scalar(ab[:, :, 8:16], vec[:, :, :, 1], cp["v_cross"], None, ALU.mult)
            v.tensor_scalar(w2tv, vec[:, :, :, 2], -cp["v_quad"], None, ALU.mult)
            v.tensor_scalar(ab[:, :, 0:8], vec[:, :, :, 0], cp["v_same"], None, ALU.mult)
            dve.drain()
            v.tensor_tensor(ab[:, :, 0:8], ab[:, :, 0:8], w2tv, ALU.add)
            dve.drain()

            t0 = tab(C0)
            sq = acc[:, 0:W * F].rearrange("p (w c) -> p w c", c=F)
            for k in range(2):
                for h in range(HEADS):
                    v.tensor_tensor(sq, x[:, :, :], row(vrow[:, k, h, :]), ALU.mult)
                    dve.drain()
                    dst = asrc[:, :, h] if k == 0 else t0[:, :, F + 1 + h]
                    v.tensor_reduce(dst, sq, AX.X, ALU.add)
                    dve.drain()
            v.tensor_copy(t0[:, :, 0:F], x[:, :, :])
            v.memset(t0[:, :, F:F + 1], 1.0).then_inc(tab_ready, 1)

            for part in range(PARTS):
                dve.wait_ge(rows_sent[part], 16)
            rank(1, dsts, win_dst)

            def windows(win_tab, n):
                return group_windows(dve, DVE_ENGINE, win_tab, n)

            def steps(step):
                with dve.Fori(0, ITERS - 1) as i:
                    for s in range(SLOTS):
                        step(i, s, True)
                for s in range(SLOTS):
                    step(ITERS - 1, s, s < SLOTS - 1)

            def after(i, s):
                return i + (s + 1) // SLOTS, (s + 1) % SLOTS

            def one_hot(s, pas, i, dst, pads=False):
                dve.wait_ge(pay_in[s], pay_count(pas, i))
                key = payv(s, pas)[:, :, 0].bitcast(I32)
                v.tensor_scalar(keyi[:, :], key, KEY_MASK, None, ALU.bitwise_and)
                if pads:
                    v.tensor_scalar(padf[:, :], key, float(PAD_KEY), -BIG, ALU.is_ge, ALU.mult)
                dve.drain()
                v.tensor_copy(keyf[:, :], keyi[:, :])
                dve.drain()
                return v.tensor_tensor(dst, iota[:, :].rearrange("p (a n) -> p a n", a=1).to_broadcast([P, TPS, P]),
                                       keyf[:, :].rearrange("p (t a) -> p t a", a=1).to_broadcast([P, TPS, P]),
                                       ALU.is_equal)

            def add_sums(wins, c, where, order, n, pas):
                dve.drain()
                dve.wait_ge(sums_ready, n + (order * STEPS + 1))
                for q in range(GPS):
                    if q:
                        dve.drain()
                    dst = acc[:, bass.ds(wins[q] * c, c)]
                    last = v.tensor_tensor(dst, dst, where(q), ALU.add)
                last.then_inc(step_done, 1)

            def max_prepare(i, s):
                b = s % 2
                one_hot(s, PASS_MAX, i, hotb[b], pads=True)
                dve.wait_ge(gat_in[PASS_MAX][s], gat_count(PASS_MAX, i))
                v.tensor_tensor(adm[:, :, :], gat[:, s, :, F + 1:C0],
                                padf[:, :].rearrange("p (t a) -> p t a", a=1).to_broadcast([P, TPS, HEADS]), ALU.add)
                dve.drain()
                flat = adm[:, :, :].rearrange("p t h -> p (t h)")
                v.tensor_copy(adsp[:, b, 0, :], flat)
                dve.drain()
                v.tensor_tensor(flat, flat, adsp[:, b, 0, :], ALU.subtract)
                dve.drain()
                v.tensor_copy(adsp[:, b, 1, :], flat)
                dve.drain()
                v.tensor_tensor(adsp[:, b, 2, :], flat, adsp[:, b, 1, :], ALU.subtract).then_inc(split_ready, 1)

            def max_step(i, s, more):
                n = i * SLOTS + s
                wins = windows(win_src, n)
                if more:
                    max_prepare(*after(i, s))
                for q in range(GPS):
                    dve.wait_ge(mask_ready, n * GPS + (q + 1))
                    v.tensor_reduce(gm[:, q, :], banks[:, 2 * (q % 2):2 * (q % 2) + 2, :].rearrange(
                        "p t (h e) -> p h t e", h=HEADS), AX.XY, ALU.max).then_inc(mask_used, 1)
                for q in range(GPS):
                    dve.drain()
                    dst = mmax[:, :, :].rearrange("p w h -> p (w h)")[:, bass.ds(wins[q] * HEADS, HEADS)]
                    last = v.tensor_tensor(dst, dst, gm[:, q, :], ALU.max)
                last.then_inc(step_done, 1)

            max_prepare(0, 0)
            steps(max_step)
            dve.drain()
            v.tensor_scalar(nodeam[:, :, 0:HEADS], asrc[:, :, :], fcb[:, :], None, ALU.add)
            dve.drain()
            v.tensor_tensor(mmax[:, :, :], mmax[:, :, :], nodeam[:, :, 0:HEADS], ALU.add)
            dve.drain()
            v.scalar_tensor_tensor(nodeam[:, :, HEADS:2 * HEADS], mmax[:, :, :], 0.2, mmax[:, :, :], ALU.mult, ALU.max)
            dve.drain()
            v.tensor_copy(nodesp[:, :, 0, :], nodeam[:, :, :])
            dve.drain()
            v.tensor_tensor(nodeam[:, :, :], nodeam[:, :, :], nodesp[:, :, 0, :], ALU.subtract)
            dve.drain()
            v.tensor_copy(nodesp[:, :, 1, :], nodeam[:, :, :])
            dve.drain()
            v.tensor_tensor(nodesp[:, :, 2, :], nodeam[:, :, :], nodesp[:, :, 1, :], ALU.subtract)
            dve.wait_ge(filled, 16 * FILL_DMAS)
            v.memset(acc[:, :], 0.0)
            dve.drain()

            def att_step(i, s, more):
                n = i * SLOTS + s
                wins = windows(win_src, n)
                dve.wait_ge(am_ready, n + 1)
                v.tensor_reduce(am[:, :, :], bank[6][:, 0:24 * TPS].rearrange("p (t k c) -> p t c k", k=3, c=2 * HEADS),
                                AX.X, ALU.add)
                dve.drain()
                dve.wait_ge(att_in[s], i * 16 + 16)
                v.tensor_tensor(logit[:, :, :], am[:, :, 0:HEADS], gat[:, s, :, F + 1:C0], ALU.add)
                dve.drain()
                v.scalar_tensor_tensor(logit[:, :, :], logit[:, :, :], 0.2, logit[:, :, :], ALU.mult, ALU.max)
                dve.drain()
                v.tensor_tensor(logit[:, :, :], logit[:, :, :], am[:, :, HEADS:2 * HEADS], ALU.subtract)
                dve.drain()
                v.tensor_scalar(logit[:, :, :], logit[:, :, :], 0.0, None, ALU.min).then_inc(logit_ready, 1)
                if more:
                    i1, s1 = after(i, s)
                    one_hot(s1, PASS_ATT, i1, hot[:, s1 % 2, :, :]).then_inc(hot_ready, 1)
                dve.wait_ge(prob_ready, n + 1)
                v.tensor_tensor(msg[:, :, 0:CM - 1].rearrange("p t (h c) -> p t h c", h=HEADS),
                                gat[:, s, :, 0:F + 1].rearrange("p t (a c) -> p t a c", a=1).to_broadcast([P, TPS, HEADS, F + 1]),
                                prob[:, :, :].rearrange("p t (h a) -> p t h a", a=1).to_broadcast([P, TPS, HEADS, F + 1]),
                                ALU.mult).then_inc(msg_ready, 1)
                add_sums(wins, CM, lambda q: bank[q // 2][:, (q % 2) * CM:(q % 2 + 1) * CM], 0, n, PASS_ATT)

            one_hot(0, PASS_ATT, 0, hot[:, 0, :, :]).then_inc(hot_ready, 1)
            steps(att_step)
            dve.drain()

            def spmm(pas, c, order, win_tab):
                def step(i, s, more):
                    n = i * SLOTS + s
                    wins = windows(win_tab, n)
                    if more:
                        i1, s1 = after(i, s)
                        one_hot(s1, pas, i1, hot[:, s1 % 2, :, :]).then_inc(hot_ready, 1)
                    add_sums(wins, c, lambda q: bank[s % 2][:, q * c:(q + 1) * c], order, n, pas)

                one_hot(0, pas, 0, hot[:, 0, :, :]).then_inc(hot_ready, 1)
                steps(step)
                dve.drain()

            def project(k, make_y, take_z, take_h=None):
                zs = W * k
                per = 2 if take_h else 1
                with dve.Fori(0, W // 2) as j:
                    for b in range(2):
                        make_y(j * 2 + b, b).then_inc(y_ready, 1)
                    for b in range(2):
                        if take_h:
                            dve.wait_ge(z_ready, j * 4 + (zs + 2 * b + 1))
                            take_h(b).then_inc(h_ready, 1)
                        dve.wait_ge(z_ready, j * (2 * per) + (zs + per * b + per))
                        take_z(j * 2 + b, b)
                dve.drain()

            roots = [PARTS]

            def root_of(last):
                last.then_inc(sq_in, 1)
                roots[0] += 1
                dve.wait_ge(sq_out, roots[0])

            def layernorm():
                t = tab(F)
                v.tensor_reduce(st1[:, :], x[:, :, :], AX.X, ALU.add)
                dve.drain()
                v.tensor_scalar(st1[:, :], st1[:, :], 1.0 / F, None, ALU.mult)
                dve.drain()
                v.tensor_tensor(x[:, :, :], x[:, :, :], each(st1[:, :], F), ALU.subtract)
                dve.drain()
                v.tensor_tensor(t, x[:, :, :], x[:, :, :], ALU.mult)
                dve.drain()
                v.tensor_reduce(st2[:, :], t, AX.X, ALU.add)
                dve.drain()
                root_of(v.tensor_scalar(st2[:, :], st2[:, :], 1.0 / F, EPS, ALU.mult, ALU.add))
                v.reciprocal(st2[:, :], st2[:, :])
                dve.drain()
                v.tensor_tensor(x[:, :, :], x[:, :, :], each(st2[:, :], F), ALU.mult)
                dve.drain()

            a0 = accv(CM)
            sums = a0[:, :, 0:CM - 1].rearrange("p w (h c) -> p w h c", h=HEADS)[:, :, :, F]
            v.tensor_scalar(asrc[:, :, :], sums, 0.0, None, ALU.is_equal)
            dve.drain()
            v.tensor_tensor(asrc[:, :, :], asrc[:, :, :], sums, ALU.add)
            dve.drain()
            v.reciprocal(asrc[:, :, :], asrc[:, :, :])
            v.tensor_copy(dis[:, :], a0[:, :, CM - 1])
            dve.drain()

            def y0(w, b):
                return v.tensor_tensor(
                    yb[:, b, :].rearrange("p (h c) -> p h c", h=HEADS),
                    acc[:, bass.ds(w * CM, CM)][:, 0:CM - 1].rearrange("p (h c) -> p h c", h=HEADS)[:, :, 0:F],
                    asrc[:, :, :].rearrange("p w h -> p (w h)")[:, bass.ds(w * HEADS, HEADS)]
                    .rearrange("p (h a) -> p h a", a=1).to_broadcast([P, HEADS, F]), ALU.mult)

            def xw(w):
                return x[:, :, :].rearrange("p w c -> p (w c)")[:, bass.ds(w * F, F)]

            def z0(w, b):
                return v.scalar_tensor_tensor(xw(w), bank[2 + b][:, 0:F], 1.0 / HEADS, xw(w), ALU.mult, ALU.add)

            project(0, y0, z0)
            v.tensor_tensor(x[:, :, :], x[:, :, :], row(bias0[:, :]), ALU.add)
            dve.wait_ge(tab_sent, 16)
            dve.drain()
            layernorm()

            v.tensor_scalar(dinv[:, :], dis[:, :], 0.0, None, ALU.is_gt)
            root_of(v.tensor_scalar(st1[:, :], dis[:, :], 1.0, None, ALU.max))
            v.reciprocal(st1[:, :], st1[:, :])
            dve.drain()
            v.tensor_tensor(dis[:, :], st1[:, :], dinv[:, :], ALU.mult)
            dve.drain()
            t1 = tab(C1)
            v.tensor_tensor(t1[:, :, F + 1], dis[:, :], mask[:, :], ALU.mult)
            v.tensor_copy(t1[:, :, F], dis[:, :])
            ok = acc[:, 0:W * F // 4].bitcast(U8).rearrange("p (w c) -> p w c", c=F)
            v.tensor_tensor(ok, x[:, :, :], x[:, :, :], ALU.is_equal)
            v.memset(t1[:, :, 0:F], 0.0)
            dve.drain()
            v.copy_predicated(t1[:, :, 0:F], ok, x[:, :, :])
            dve.drain()
            v.tensor_scalar(t1[:, :, 0:F], t1[:, :, 0:F], FMAX, -FMAX, ALU.min, ALU.max)
            dve.drain()
            v.tensor_tensor(t1[:, :, 0:F], t1[:, :, 0:F], t1[:, :, F + 1:F + 2].to_broadcast([P, W, F]),
                            ALU.mult).then_inc(tab_ready, 1)
            dve.drain()
            v.memset(acc[:, 0:W * C1], 0.0)
            dve.drain()
            spmm(PASS_L1, C1, 1, win_src)
            a1 = accv(C1)
            v.tensor_tensor(st2[:, :], dis[:, :], a1[:, :, F + 1], ALU.mult)
            v.tensor_tensor(st1[:, :], dis[:, :], a1[:, :, F], ALU.mult)
            dve.drain()
            v.tensor_scalar(dinv[:, :], st2[:, :], 0.0, None, ALU.is_equal)
            v.tensor_tensor(st1[:, :], st1[:, :], dis[:, :], ALU.mult)
            dve.drain()
            v.tensor_tensor(st2[:, :], st2[:, :], dinv[:, :], ALU.add)
            dve.drain()
            v.reciprocal(st2[:, :], st2[:, :])
            v.tensor_scalar(dinv[:, :], dinv[:, :], -1.0, 1.0, ALU.mult, ALU.add)
            dve.drain()
            v.tensor_tensor(st1[:, :], st1[:, :], st2[:, :], ALU.mult)
            dve.drain()
            v.tensor_tensor(st1[:, :], st1[:, :], dinv[:, :], ALU.mult)
            dve.drain()

            def y1(w, b):
                return v.tensor_scalar(yb[:, b, 0:F], acc[:, bass.ds(w * C1, C1)][:, 0:F], st1[:, bass.ds(w, 1)],
                                       None, ALU.mult)

            def z1(w, b):
                return v.tensor_tensor(xw(w), bank[2 + b][:, 0:F], xw(w), ALU.add)

            project(1, y1, z1)
            v.tensor_tensor(x[:, :, :], x[:, :, :], row(bias1[:, :]), ALU.add)
            dve.wait_ge(tab_sent, 32)
            dve.drain()
            layernorm()

            v.tensor_copy(tab(F), x[:, :, :]).then_inc(tab_ready, 1)
            v.memset(acc[:, 0:W * C2], 0.0)
            dve.drain()

            def r_(b, lo):
                return rx[:, b, :, lo:lo + 3].rearrange("p t (o a) -> p t o a", a=1).to_broadcast([P, TPS, 3, 8])

            tA = tmpA[:, :, :].rearrange("p t (o v) -> p t o v", o=3)
            tB = tmpB[:, :, :].rearrange("p t (o v) -> p t o v", o=3)

            def minus_keys(i, s):
                dve.wait_ge(pay_in[s], pay_count(PASS_L2, i))
                v.tensor_scalar(keyi[:, :], payv(s, PASS_L2)[:, :, 0].bitcast(I32), KEY_MASK, None, ALU.bitwise_and)
                dve.drain()
                dve.wait_ge(key_used, i * SLOTS + (s + 1))
                v.tensor_scalar(keyn[:, :], keyi[:, :], -1.0, None, ALU.mult).then_inc(key_ready, 1)

            def geometry(i, s):
                b = s % 2
                dve.wait_ge(geo_ready, i * SLOTS + (s + 1))
                v.tensor_tensor(tA, fT[:, b, :, 2:5, :], r_(b, 1), ALU.mult)
                v.tensor_tensor(tB, fT[:, b, :, 1:4, :], r_(b, 2), ALU.mult)
                dve.drain()
                v.tensor_tensor(g_v[:, b, :, :, 8:16], tA, tB, ALU.subtract)
                dve.drain()
                v.tensor_tensor(tA, fT[:, b, :, 0:3, :], r_(b, 0), ALU.mult)
                dve.drain()
                v.tensor_reduce(g_s[:, b, :, 8:16], tmpA[:, :, :].rearrange("p t (o v) -> p t v o", o=3), AX.X, ALU.add)

            def radial_sums(n, wins):
                add_sums(wins, C2, lambda q: bank[0][:, q * C2:(q + 1) * C2], 2, n, PASS_L2)

            def radial_step(i, s, first, more):
                n = i * SLOTS + s
                b = s % 2
                if not first:
                    wins = windows(win_dst, n - 1)
                if more:
                    minus_keys(*after(i, s))
                dve.drain()
                for p in range(TPS // 2):
                    t0, pb, lo = 2 * p, p % 2, 1 + 2 * (p % 2)
                    dve.wait_ge(r_ready, n * (TPS // 2) + (p + 1))
                    v.tensor_tensor(prod[:, pb, :, 0:16, :],
                                    banks[:, lo:lo + 2, 0:256].rearrange("p t (u k) -> p t u k", k=16),
                                    g_s[:, b, t0:t0 + 2, :].rearrange("p t (a k) -> p t a k", a=1).to_broadcast([P, 2, 16, 16]),
                                    ALU.mult)
                    for h in range(2):
                        last = v.tensor_tensor(
                            prod[:, pb, h, 16:40, :].rearrange("p (u o) k -> p u o k", o=3),
                            bank[lo + h][:, 256:384].rearrange("p (u a k) -> p u a k", a=1, k=16).to_broadcast([P, 8, 3, 16]),
                            g_v[:, b, t0 + h:t0 + h + 1, :, :].to_broadcast([P, 8, 3, 16]), ALU.mult)
                    last.then_inc(r_used, 1)
                    dve.drain()
                    v.tensor_reduce(red[:, b, t0:t0 + 2, 0:40], prod[:, pb, :, :, :], AX.X, ALU.add)
                    if p == 1 and not first:
                        radial_sums(n - 1, wins)
                dve.drain()
                v.tensor_tensor(tmpA[:, :, :].rearrange("p t (u o) -> p t u o", o=3),
                                rx[:, b, :, 0:3].rearrange("p t (a o) -> p t a o", a=1).to_broadcast([P, TPS, 8, 3]),
                                red[:, b, :, 8:16].rearrange("p t (u a) -> p t u a", a=1).to_broadcast([P, TPS, 8, 3]), ALU.mult)
                dve.drain()
                v.tensor_tensor(red[:, b, :, 16:40], red[:, b, :, 16:40], tmpA[:, :, :], ALU.add).then_inc(msg_ready, 1)
                if more:
                    dve.drain()
                    geometry(*after(i, s))

            dve.sem_inc(key_used, 1)
            minus_keys(0, 0)
            geometry(0, 0)
            for s in range(SLOTS):
                radial_step(0, s, s == 0, True)
            with dve.Fori(1, ITERS - 1) as i:
                for s in range(SLOTS):
                    radial_step(i, s, False, True)
            for s in range(SLOTS):
                radial_step(ITERS - 1, s, False, s < SLOTS - 1)
            radial_sums(STEPS - 1, windows(win_dst, STEPS - 1))
            dve.drain()
            a2 = accv(C2)
            v.tensor_tensor(x[:, :, 0:8], x[:, :, 0:8], a2[:, :, 0:8], ALU.add)
            v.tensor_tensor(x[:, :, 8:F], x[:, :, 8:F], a2[:, :, 16:40], ALU.add)
            v.tensor_copy(dinv[:, :], a2[:, :, 40])
            dve.wait_ge(tab_sent, 48)
            dve.drain()
            layernorm()
            root_of(v.tensor_scalar(st1[:, :], dinv[:, :], 1.0, None, ALU.add))
            v.reciprocal(dinv[:, :], st1[:, :])
            dve.drain()
            v.tensor_tensor(tab(F), x[:, :, :], each(dinv[:, :], F), ALU.mult).then_inc(tab_ready, 1)
            v.memset(acc[:, 0:W * F], 0.0)
            dve.drain()
            spmm(PASS_L3A, F, 3, win_dst)

            def tw(w):
                return tabf[:, bass.ds(w * F, F)]

            v.tensor_tensor(acc[:, 0:W * F], acc[:, 0:W * F], tabf[:, 0:W * F], ALU.add)
            dve.wait_ge(tab_sent, 64)
            dve.drain()

            def y2(w, b):
                return v.tensor_scalar(yb[:, b, 0:F], acc[:, bass.ds(w * F, F)], dinv[:, bass.ds(w, 1)], None, ALU.mult)

            def h2(b):
                v.tensor_tensor(hb[:, b, :], bank[2 + b][:, 0:H2], g3b1[:, :], ALU.add)
                dve.drain()
                return v.tensor_scalar(hb[:, b, :], hb[:, b, :], 0.0, None, ALU.max)

            def z2(w, b):
                return v.tensor_scalar(tw(w), bank[6 + b][:, 0:F], dinv[:, bass.ds(w, 1)], None, ALU.mult)

            project(2, y2, z2, h2)
            v.memset(acc[:, 0:W * F], 0.0).then_inc(tab_ready, 1)
            dve.drain()
            spmm(PASS_L3B, F, 4, win_dst)
            v.tensor_tensor(acc[:, 0:W * F], acc[:, 0:W * F], tabf[:, 0:W * F], ALU.add)
            dve.drain()
            a3 = accv(F)
            v.tensor_tensor(a3, a3, each(dinv[:, :], F), ALU.mult)
            dve.drain()
            v.tensor_tensor(a3, a3, row(g3b2[:, :]), ALU.add)
            dve.drain()
            v.scalar_tensor_tensor(x[:, :, :], a3, 0.0, x[:, :, :], ALU.max, ALU.add)
            dve.wait_ge(tab_sent, 80)
            dve.drain()
            layernorm()
            v.tensor_copy(gm[:, 0, 0:1], iota[:, 0:1]).then_inc(tab_ready, 1)


_INS = ['x', 'src', 'dst', 'edge_attr_3', 'edge_weight', 'node_vec1', 'L0_gnn_w', 'L0_gnn_fc_w', 'L0_gnn_fc_b',
        'L0_gnn_bias', 'L1_gnn_W', 'L1_gnn_b', 'L2_gnn_w1', 'L2_gnn_b1', 'L2_gnn_w2', 'L2_gnn_b2',
        'L3_gnn_W1', 'L3_gnn_b1', 'L3_gnn_W2', 'L3_gnn_b2']


def kernel(**inputs):
    import numpy as _np
    import concourse.bacc as _bacc
    from concourse import mybir as _mybir
    from concourse.bass_utils import run_bass_kernel_spmd as _run

    nc = _bacc.Bacc("TRN2", target_bir_lowering=False, num_devices=1)
    arrays, args = {}, {}
    for name in _INS:
        arr = _np.asarray(inputs[name])
        key = name
        if name == 'L1_gnn_W':
            arr, key = arr.T, 'L1_WT'
        arr = _np.ascontiguousarray(arr)
        arrays[f"in_{key}"] = arr
        args[key] = nc.dram_tensor(f"in_{key}", arr.shape, _mybir.dt.from_np(arr.dtype), kind="ExternalInput").ap()
    out = nc.dram_tensor("out", (N, F), _mybir.dt.float32, kind="ExternalOutput").ap()
    resnorm_gnn_kernel(nc, args, out)
    r = _run(nc, [arrays], core_ids=[0])
    return r.results[0]["out"]
```

```python
import concourse.bass as bass
import concourse.mybir as mybir
import numpy as np
from contextlib import ExitStack
from math import factorial, pi, sqrt

F32 = mybir.dt.float32
BF16 = mybir.dt.bfloat16
I32 = mybir.dt.int32
U8 = mybir.dt.uint8
ALU = mybir.AluOpType
ACT = mybir.ActivationFunctionType
AX = mybir.AxisListType

P = 128
N = 12500
F = 32
W = -(-N // P)
NW = W * P
LAST = N - (W - 1) * P
PW = 7
BATCHES = W // PW
assert BATCHES * PW == W and BATCHES % 2 == 0
E = 400000
TE = E // P
HEADS = 4
HID = 64
H2 = 64

TILES_PER_GROUP = 2
GROUP = TILES_PER_GROUP * P
SLOTS = 4
GPS = 4
TPS = GPS * TILES_PER_GROUP
MAX_GROUPS = (E + W * (GROUP - 1)) // GROUP
ITERS = -(-MAX_GROUPS // (SLOTS * GPS))
STEPS = ITERS * SLOTS
NG = STEPS * GPS
NT = NG * TILES_PER_GROUP
ROWS = P * NT

RING = 5
RSLOTS = 5
RITERS = TE // (RING * RSLOTS)
PARTS = 5
ROW_PARTS = ((0, 2), (2, 5), (5, 10), (10, 15), (15, 20), (20, 25))
RP = len(ROW_PARTS)
LATE = 1
assert TE % 25 == 0

PAD_KEY = 1 << 20
KEY_MASK = PAD_KEY | (P - 1)
BIG = float(2.0 ** 100)
FMAX = 3.4028234663852886e38
EPS = 1e-05

C0 = F + 1 + HEADS
CM = HEADS * (F + 1) + 1
C1 = F + 2
C2 = 41
CF = F


def _coupling():
    def cg(j1, j2, j3, m1, m2, m3):
        if m1 + m2 != m3:
            return 0.0
        f = factorial
        pre = sqrt((2 * j3 + 1) * f(j3 + j1 - j2) * f(j3 - j1 + j2) * f(j1 + j2 - j3) / f(j1 + j2 + j3 + 1))
        pre *= sqrt(f(j3 + m3) * f(j3 - m3) * f(j1 - m1) * f(j1 + m1) * f(j2 - m2) * f(j2 + m2))
        s = 0.0
        for k in range(max(0, j2 - j3 - m1, j1 - j3 + m2), min(j1 + j2 - j3, j1 - m1, j2 + m2) + 1):
            s += (-1) ** k / (f(k) * f(j1 + j2 - j3 - k) * f(j1 - m1 - k) * f(j2 + m2 - k)
                              * f(j3 - j2 + m1 + k) * f(j3 - j1 - m2 + k))
        return pre * s

    def basis(l):
        a = np.zeros((2 * l + 1, 2 * l + 1), dtype=complex)
        a[l, l] = 1.0
        for m in range(1, l + 1):
            a[l + m, l + m] = (-1) ** m / sqrt(2)
            a[l + m, l - m] = 1.0 / sqrt(2)
            a[l - m, l - m] = 1j / sqrt(2)
            a[l - m, l + m] = -1j * (-1) ** m / sqrt(2)
        return a

    def w3j(l1, l2, l3):
        w = np.zeros((2 * l1 + 1, 2 * l2 + 1, 2 * l3 + 1))
        for m1 in range(-l1, l1 + 1):
            for m2 in range(-l2, l2 + 1):
                m3 = -(m1 + m2)
                if abs(m3) <= l3:
                    w[m1 + l1, m2 + l2, m3 + l3] = (-1) ** (l1 - l2 - m3) / sqrt(2 * l3 + 1) * cg(l1, l2, l3, m1, m2, -m3)
        wr = np.einsum('abc,ma,nb,oc->mno', w.astype(complex), basis(l1).conj(), basis(l2).conj(), basis(l3).conj())
        i = int(np.argmax(np.abs(wr)))
        return np.real(wr / (wr.flat[i] / abs(wr.flat[i])))

    norm0 = sqrt(4 * pi) / sqrt(8 * 1 + 8 * 1)
    norm1 = sqrt(4 * pi) * sqrt(3.0) / sqrt(8 * 1 + 8 * 3)
    y0 = 0.5 / sqrt(pi)
    c1 = sqrt(3.0 / (4.0 * pi))
    c2b, c2c = 0.25 * sqrt(5.0 / pi), 0.25 * sqrt(15.0 / pi)
    y2 = np.array([0, 0, -c2b, 0, -c2c])
    k2 = 0.5 * float(w3j(1, 2, 1)[0, :, 0] @ y2)
    return {
        "s_f0": norm0 * y0 * float(w3j(0, 0, 0)[0, 0, 0]),
        "s_dot": norm0 * c1 * float(w3j(0, 1, 1)[0, 0, 0]),
        "v_f0": norm1 * c1 * float(w3j(1, 1, 0)[0, 0, 0]),
        "v_same": norm1 * y0 * float(w3j(1, 0, 1)[0, 0, 0]),
        "v_cross": norm1 * c1 * float(w3j(1, 1, 1)[0, 1, 2]),
        "v_quad": norm1 * k2,
    }


def resnorm_gnn_kernel(nc, a, out):
    ctx = ExitStack()
    with ctx:
        def sb(name, shape, dt=F32):
            return ctx.enter_context(nc.sbuf_tensor(name, shape, dt))

        def sem(name):
            return ctx.enter_context(nc.semaphore(name))

        def dram(name, shape):
            return nc.dram_tensor(name, shape, F32, kind="Internal").ap()

        edges_src = dram("edges_src", (E, 2))
        edges_dst = dram("edges_dst", (E, 6))
        rows_src = nc.dram_tensor("rows_src", (E, 1), I32, kind="Internal").ap()
        rows_dst = nc.dram_tensor("rows_dst", (E, 1), I32, kind="Internal").ap()
        by_src = dram("by_src", (ROWS, 2))
        by_dst = dram("by_dst", (ROWS, 6))
        staged = dram("staged", (ROWS, C0))
        tab0 = dram("tab0", (NW, C0))
        tab1 = dram("tab1", (NW, C1))
        tab2 = dram("tab2", (NW, F))
        tab3 = dram("tab3", (NW, F))
        tab4 = dram("tab4", (NW, F))
        by_src_v = by_src.rearrange("(p t) c -> p t c", p=P)
        by_dst_v = by_dst.rearrange("(p t) c -> p t c", p=P)
        staged_v = staged.rearrange("(p t) c -> p t c", p=P)

        x = sb("x", [P, W, F])
        tabx = sb("tabx", [P, W, C0])
        acc = sb("acc", [P, W * CM])
        srcs = sb("srcs", [P, TE], I32)
        dsts = sb("dsts", [P, TE], I32)
        pos = sb("pos", [P, TE])
        hot = sb("hot", [P, 2, TPS, P])
        winb = acc[:, 0:TE].bitcast(BF16)[:, 0:TE]
        eqm = acc[:, TE:TE + (TE + 3) // 4 + 1].bitcast(U8)[:, 0:TE]
        cum = acc[:, 4096:4096 + TE]
        fill = acc[:, 8192:8192 + 416 * 6].rearrange("p (t c) -> p t c", c=6)
        fill2 = hot[:, 0, :, :].rearrange("p t n -> p (t n)")[:, 0:416 * 2].rearrange("p (t c) -> p t c", c=2)
        FILL_T = 416
        assert NT % FILL_T == 0

        iota = sb("iota", [P, P])
        iotaw = iota[:, 0:W]
        ident = sb("ident", [P, P])
        identb = sb("identb", [P, P], BF16)
        ones = sb("ones", [P, P])
        before = sb("before", [P, P])
        far = sb("far", [P, P], BF16)
        pick = sb("pick", [96, 32, P], BF16)
        hist = sb("hist", [P, W])
        start_ = sb("start_", [P, W])
        ends = sb("ends", [P, W])
        gcnt = sb("gcnt", [P, W], I32)
        endT = sb("endT", [P, 1])
        giota = acc[:, 10752:10752 + NG]
        gge = cum[:, 0:NG]
        CHUNK = TE // PARTS
        ch_attr = acc[:, 0:3 * CHUNK].rearrange("p (t c) -> p t c", c=3)
        ch_w = acc[:, 1875:1875 + CHUNK]
        ch_len = acc[:, 2500:2500 + CHUNK]
        ch_sq = acc[:, 3125:3125 + CHUNK]
        ch_pay = acc[:, 3750:3750 + 6 * CHUNK].rearrange("p (t c) -> p t c", c=6)
        pair = acc[:, 0:2 * TE].rearrange("p (t c) -> p t c", c=2)
        whb = tabx[:, :, :].rearrange("p w c -> p (w c)")
        win_src = sb("win_src", [1, NG], I32)
        win_dst = sb("win_dst", [1, NG], I32)
        posr = sb("posr", [P, RSLOTS, RING], I32)
        payr = sb("payr", [P, RSLOTS, RING, 6])

        pay = sb("pay", [P, SLOTS, TPS, 6])
        gat = sb("gat", [P, SLOTS, TPS, C0])
        keyi = sb("keyi", [P, TPS], I32)
        keyf = sb("keyf", [P, TPS])
        hotb = [hot[:, b, :, :].rearrange("p t n -> p (t n)").bitcast(BF16)[:, 0:TPS * P]
                .rearrange("p (t n) -> p t n", n=P) for b in range(2)]
        hotT = sb("hotT", [P, 2, TPS, P], BF16)
        mmax = sb("mmax", [P, W, HEADS])
        asrc = sb("asrc", [P, W, HEADS])
        nodeam = sb("nodeam", [P, W, 2 * HEADS])
        nodesp = sb("nodesp", [P, W, 3, 2 * HEADS], BF16)
        padf = sb("padf", [P, TPS])
        adm = sb("adm", [P, TPS, HEADS])
        adsp = sb("adsp", [P, 2, 3, TPS * HEADS], BF16)
        adT = sb("adT", [96, 2, P], BF16)
        red = sb("red", [P, 2, TPS, C2])
        am = sb("am", [P, TPS, 2 * HEADS])
        logit = sb("logit", [P, TPS, HEADS])
        prob = sb("prob", [P, TPS, HEADS])
        msg = sb("msg", [P, TPS, CM])
        fT = sb("fT", [P, 2, TPS, 5, 8])
        g_s = sb("g_s", [P, 2, TPS, 16])
        g_v = sb("g_v", [P, 2, TPS, 3, 16])
        rx = sb("rx", [P, 2, TPS, 5])
        tmpA = sb("tmpA", [P, TPS, 24])
        tmpB = sb("tmpB", [P, TPS, 24])
        prod = srcs[:, 0:4 * 640].bitcast(F32).rearrange("p (b t r k) -> p b t r k", b=2, t=2, k=16)
        hid = dsts[0:HID + 1, 0:2 * TPS * P].bitcast(F32).rearrange("p (b t n) -> p b t n", b=2, t=TPS)
        radial = sb("radial", [P, TPS, 24])
        tmpC = sb("tmpC", [P, TPS, 24])
        wrest = sb("wrest", [P, TPS])
        wparts = sb("wparts", [P, 2, 9, TPS], BF16)
        dT = sb("dT", [9 * TPS, P], BF16)
        w1row = sb("w1row", [9 * TPS, HID + 1])
        w1parts = sb("w1parts", [9 * TPS, 3, HID + 1], BF16)
        row_of = sb("row_of", [9 * TPS, 3, TPS])
        w1sel = sb("w1sel", [9 * TPS, TPS, HID + 1], BF16)
        w1tmp = hotT[0:9 * TPS, :, :, :].rearrange("p b t n -> p (b t n)").bitcast(F32)[:, 0:TPS * (HID + 1)] \
            .rearrange("p (t h) -> p t h", t=TPS)
        b1col = sb("b1col", [HID + 1, 1])
        w2raw = sb("w2raw", [HID + 1, 384])
        w2p = sb("w2p", [HID + 1, 384])
        w2t = sb("w2t", [HID + 1, 64])
        hot4 = [hot[:, b, :, :] for b in range(2)] + [
            srcs[:, b * TPS * P:(b + 1) * TPS * P].bitcast(F32).rearrange("p (t n) -> p t n", n=P) for b in range(2)]
        wh = sb("wh", [P, F])
        whr = tabx[:, :, :].rearrange("p w c -> p (w c)")[:, 0:F * F].rearrange("p (f o) -> p f o", o=F)
        vtmp = tabx[:, :, :].rearrange("p w c -> p (w c)")[:, F * F:2 * F * F].rearrange("p (f o) -> p f o", o=F)
        fcw = sb("fcw", [P, 2 * F])
        vrow = sb("vrow", [P, 2, HEADS, F])
        gm = sb("gm", [P, GPS, HEADS])
        fcb = sb("fcb", [P, 1])
        bias0 = sb("bias0", [P, F])
        w1T = sb("w1T", [F, F])
        bias1 = sb("bias1", [P, F])
        g3w1 = sb("g3w1", [F, H2])
        g3b1 = sb("g3b1", [P, H2])
        g3w2 = sb("g3w2", [H2, F])
        g3b2 = sb("g3b2", [P, F])
        mask = sb("mask", [P, W])
        st1 = sb("st1", [P, W])
        st2 = sb("st2", [P, W])
        dis = sb("dis", [P, W])
        dinv = sb("dinv", [P, W])
        yb = hot[:, :, :, :].rearrange("p b t n -> p (b t n)")[:, 0:2 * PW * P].rearrange("p (b w n) -> p b w n", b=2, w=PW)
        yT = srcs[:, 0:2 * PW * P].bitcast(F32).rearrange("p (b w n) -> p b w n", b=2, w=PW)
        hb = msg[:, :, :].rearrange("p t c -> p (t c)")[:, 0:2 * PW * H2].rearrange("p (b w c) -> p b w c", b=2, w=PW)
        hT = dsts[0:H2, 0:2 * PW * P].bitcast(F32).rearrange("p (b w n) -> p b w n", b=2, w=PW)

        banks = ctx.enter_context(nc.psum_tensor("banks", [P, 8, 512], F32))
        bank = [banks[:, b, :] for b in range(8)]
        turned = [banks[:, 2 * b:2 * b + 2, :].rearrange("p k n -> p (k n)")[:, 0:PW * P] for b in range(2)]

        keys_in = sem("keys_in")
        loaded = sem("loaded")
        consts = sem("consts")
        histed = sem("histed")
        hsum = sem("hsum")
        ended = sem("ended")
        endedT = sem("endedT")
        bucketed = sem("bucketed")
        compared = sem("compared")
        counted = sem("counted")
        filled = sem("filled")
        fill_set = sem("fill_set")
        ranked = sem("ranked")
        sq_in = sem("sq_in")
        sq_out = sem("sq_out")
        ring_full = [sem(f"ring_full{s}") for s in range(RSLOTS)]
        whr_in = sem("whr_in")
        whr_used = sem("whr_used")
        pairs_made = sem("pairs_made")
        pairs_sent = sem("pairs_sent")
        chunk_in = sem("chunk_in")
        chunk_made = sem("chunk_made")
        chunk_sent = sem("chunk_sent")
        rows_sent = [sem(f"rows_sent{p_}") for p_ in range(RP)]
        ring_sent = [sem(f"ring_sent{s}") for s in range(RSLOTS)]
        tab_ready = sem("tab_ready")
        tab_sent = sem("tab_sent")
        pay_in = [sem(f"pay_in{s}") for s in range(SLOTS)]
        gat_in = {p_: [sem(f"gat_in{p_}_{s}") for s in range(SLOTS)] for p_ in (0, 2, 3, 4, 5)}
        att_in = [sem(f"att_in{s}") for s in range(SLOTS)]
        staged_out = [sem(f"staged_out{s}") for s in range(SLOTS)]
        step_done = sem("step_done")
        hot_ready = sem("hot_ready")
        sums_ready = sem("sums_ready")
        tp_done = sem("tp_done")
        hotT_ready = sem("hotT_ready")
        split_ready = sem("split_ready")
        mask_ready = sem("mask_ready")
        mask_used = sem("mask_used")
        am_ready = sem("am_ready")
        logit_ready = sem("logit_ready")
        prob_ready = sem("prob_ready")
        msg_ready = sem("msg_ready")
        dT_raw = sem("dT_raw")
        dT_ready = sem("dT_ready")
        hid_raw = sem("hid_raw")
        hid_ready = sem("hid_ready")
        key_ready = sem("key_ready")
        key_read = sem("key_read")
        key_used = sem("key_used")
        geo_ready = sem("geo_ready")
        geo_ops = sem("geo_ops")
        split_ops = sem("split_ops")
        r_ready = sem("r_ready")
        r_used = sem("r_used")
        y_ready = sem("y_ready")
        yT_raw = sem("yT_raw")
        yT_ready = sem("yT_ready")
        z_ready = sem("z_ready")
        h_ready = sem("h_ready")
        hT_raw = sem("hT_raw")
        hT_ready = sem("hT_ready")
        written = sem("written")

        block = ctx.enter_context(nc.Block())

        def node_rows(t):
            return t.rearrange("(w p) c -> p w c", p=P)

        def window_tail(name):
            return a[name][(W - 1) * P:N, :]

        PASS_MAX, PASS_ATT, PASS_L1, PASS_L2, PASS_L3A, PASS_L3B = range(6)
        KC = {PASS_MAX: 2, PASS_ATT: 2, PASS_L1: 2, PASS_L2: 6, PASS_L3A: 6, PASS_L3B: 6}
        GC = {PASS_MAX: C0, PASS_L1: C1, PASS_L2: F, PASS_L3A: F, PASS_L3B: F}
        TAB = {PASS_MAX: tab0, PASS_L1: tab1, PASS_L2: tab2, PASS_L3A: tab3, PASS_L3B: tab4}
        LIST = {PASS_MAX: by_src_v, PASS_ATT: by_src_v, PASS_L1: by_src_v,
                PASS_L2: by_dst_v, PASS_L3A: by_dst_v, PASS_L3B: by_dst_v}
        GATHERS = [PASS_MAX, PASS_L1, PASS_L2, PASS_L3A, PASS_L3B]

        def payv(s, pas):
            return pay[:, s, :, :].rearrange("p t c -> p (t c)")[:, 0:TPS * KC[pas]].rearrange(
                "p (t c) -> p t c", c=KC[pas])

        def gatv(s, c):
            return gat[:, s, :, :].rearrange("p t c -> p (t c)")[:, 0:TPS * c].rearrange("p (t c) -> p t c", c=c)

        def pay_count(pas, i):
            return (i + (pas * ITERS + 1)) * 16

        def gat_count(pas, i):
            return i * (16 * TPS) + 16 * TPS

        PE_ENGINE, DVE_ENGINE = mybir.EngineType.PE, mybir.EngineType.DVE

        def group_windows(eng, which, win_tab, n):
            _, vals = nc.values_load_multi_w_load_instructions(
                win_tab[0:1, bass.ds(n * GPS, GPS)], engines=(which,), min_val=0, max_val=W - 1,
                skip_runtime_bounds_check_because="the table is clamped to W - 1 where it is made")
            return vals

        GEO_OPS, SPLIT_OPS = 6, 4
        FILL_DMAS = 2 * (NT // FILL_T)
        sorted_dmas = 16 * RING

        @block.sync
        def _(sp):
            def load(dst, src):
                sp.dma_start(dst, src).then_inc(loaded, 16)

            sp.dma_start(srcs[:, :], a["src"].rearrange("(p t) -> p t", p=P)).then_inc(keys_in, 16)
            sp.dma_start(dsts[:, :], a["dst"].rearrange("(p t) -> p t", p=P)).then_inc(keys_in, 16)
            load(wh[:, :], a["L0_gnn_w"].rearrange("h f o -> (h f) o"))
            load(fcw[:, :], a["L0_gnn_fc_w"].to_broadcast([P, 2 * F]))
            load(fcb[:, :], a["L0_gnn_fc_b"].rearrange("(a b) -> a b", a=1).to_broadcast([P, 1]))
            load(bias0[:, :], a["L0_gnn_bias"].rearrange("(a b) -> a b", a=1).to_broadcast([P, F]))
            load(w1T[:, :], a["L1_WT"])
            load(bias1[:, :], a["L1_gnn_b"].rearrange("(a b) -> a b", a=1).to_broadcast([P, F]))
            load(g3w1[:, :], a["L3_gnn_W1"])
            load(g3b1[:, :], a["L3_gnn_b1"].rearrange("(a b) -> a b", a=1).to_broadcast([P, H2]))
            load(g3w2[:, :], a["L3_gnn_W2"])
            load(g3b2[:, :], a["L3_gnn_b2"].rearrange("(a b) -> a b", a=1).to_broadcast([P, F]))
            load(w1row[:, 0:HID], a["L2_gnn_w1"].to_broadcast([9 * TPS, HID]))
            load(w2raw[0:HID, :], a["L2_gnn_w2"])
            load(w2raw[HID:HID + 1, :], a["L2_gnn_b2"].rearrange("(a b) -> a b", a=1))
            sp.wait_ge(fill_set, 1)
            load(x[:, 0:W - 1, :], a["x"][0:(W - 1) * P, :].rearrange("(w p) c -> p w c", p=P))
            load(x[0:LAST, W - 1, :], a["x"][(W - 1) * P:N, :])
            with nc.allow_non_contiguous_dma(reason="one value per node"):
                load(mask[:, 0:W - 1], a["node_vec1"][0:(W - 1) * P, :].rearrange("(w p) c -> p (w c)", p=P))
                load(mask[0:LAST, W - 1:W], a["node_vec1"][(W - 1) * P:N, :])
                load(b1col[0:HID, 0:1], a["L2_gnn_b1"].rearrange("(h c) -> h c", c=1))
            for f in range(NT // FILL_T):
                sp.dma_start(by_dst_v[:, f * FILL_T:(f + 1) * FILL_T, :], fill[:, :, :]).then_inc(filled, 16)
            for f in range(NT // FILL_T):
                sp.dma_start(by_src_v[:, f * FILL_T:(f + 1) * FILL_T, :], fill2[:, :, :]).then_inc(filled, 16)
            sp.wait_ge(pairs_made, 1)
            sp.dma_start(edges_src.rearrange("(p t) c -> p t c", p=P), pair).then_inc(pairs_sent, 16)
            def ring_loads(k):
                rows, edges, c = ((rows_src, edges_src, 2), (rows_dst, edges_dst, 6))[k]
                rows_v = rows.rearrange("(p t) c -> p (t c)", p=P)

                def ring_step(i, first):
                    for s in range(RSLOTS):
                        cols = bass.ds(i * (RSLOTS * RING) + s * RING, RING)
                        if not first:
                            sp.wait_ge(ring_sent[s], i * sorted_dmas + sorted_dmas * RITERS * k)
                        sp.dma_start(posr[:, s, :], rows_v[:, cols]).then_inc(ring_full[s], 16)
                        sp.dma_start(payr[:, s, :, :].rearrange("p t c -> p (t c)")[:, 0:RING * c].rearrange("p (t c) -> p t c", c=c),
                                     edges.rearrange("(p t) c -> p t c", p=P)[:, cols, :]).then_inc(ring_full[s], 16)

                if k:
                    sp.wait_ge(chunk_sent, 16 * PARTS)
                    for s in range(RSLOTS):
                        sp.wait_ge(ring_sent[s], sorted_dmas * RITERS * k)
                else:
                    sp.wait_ge(pairs_sent, 16)
                for part, (lo, hi) in enumerate(ROW_PARTS):
                    sp.wait_ge(rows_sent[part], 16 * (k + 1))
                    if part == 0:
                        ring_step(0, True)
                    with sp.Fori(RITERS * lo // 25 + (part == 0), RITERS * hi // 25) as i:
                        ring_step(i, False)

            def send_table(k, dst, c):
                sp.wait_ge(tab_ready, k + 1)
                view = tabx[:, :, :].rearrange("p w c -> p (w c)")[:, 0:W * c].rearrange("p (w c) -> p w c", c=c)
                sp.dma_start(node_rows(dst), view).then_inc(tab_sent, 16)

            def edge_loads(pas):
                with sp.Fori(0, ITERS) as i:
                    for s in range(SLOTS):
                        tiles = bass.ds(i * (SLOTS * TPS) + s * TPS, TPS)
                        sp.wait_ge(step_done, i * SLOTS + (pas * STEPS + s + 1))
                        sp.dma_start(payv(s, pas), LIST[pas][:, tiles, :]).then_inc(pay_in[s], 16)

            ring_loads(0)
            send_table(0, tab0, C0)
            sp.wait_ge(bucketed, 1)
            edge_loads(PASS_MAX)
            ring_loads(1)
            send_table(1, tab1, C1)
            edge_loads(PASS_L1)
            send_table(2, tab2, F)
            sp.wait_ge(bucketed, 2)
            edge_loads(PASS_L2)
            send_table(3, tab3, F)
            edge_loads(PASS_L3A)
            send_table(4, tab4, F)
            edge_loads(PASS_L3B)
            sp.wait_ge(tab_ready, 6)
            sp.dma_start(out[0:(W - 1) * P, :].rearrange("(w p) c -> p w c", p=P), x[:, 0:W - 1, :]).then_inc(written, 16)
            sp.dma_start(out[(W - 1) * P:N, :], x[0:LAST, W - 1, :]).then_inc(written, 16)
            sp.wait_ge(written, 32)
            sp.wait_ge(tab_sent, 16 * 5)
            sp.wait_ge(filled, 16 * FILL_DMAS)
            for s in range(SLOTS):
                sp.wait_ge(staged_out[s], 16 * ITERS)

        N_LOADS = 18

        @block.gpsimd
        def _(pool):
            g = nc.gpsimd
            g.iota(iota[:, :], pattern=[[1, P]], base=0, channel_multiplier=0,
                   allow_small_or_imprecise_dtypes=True)
            g.iota(giota, pattern=[[1, NG]], base=0, channel_multiplier=0,
                   allow_small_or_imprecise_dtypes=True)
            g.memset(ones[:, :], 1.0)
            g.memset(ident[:, :], 0.0)
            g.memset(before[:, :], 0.0)
            g.memset(far[:, :], -BIG)
            g.memset(pick[:, :, :], 0.0)
            pool.drain()
            g.affine_select(out=ident[:, :], in_=ident[:, :], compare_op=ALU.not_equal, fill=1.0,
                            base=0, pattern=[[-1, P]], channel_multiplier=1)
            g.affine_select(out=before[:, :], in_=before[:, :], compare_op=ALU.is_ge, fill=1.0,
                            base=0, pattern=[[-1, P]], channel_multiplier=1)
            g.affine_select(out=far[:, :], in_=far[:, :], compare_op=ALU.not_equal, fill=0.0,
                            base=0, pattern=[[-1, P]], channel_multiplier=1)
            for k in range(3):
                g.affine_select(out=pick[:, :, :], in_=pick[:, :, :], compare_op=ALU.not_equal, fill=1.0,
                                base=-32 * k, pattern=[[-1, 32], [0, P]], channel_multiplier=1)
                pool.drain()
            g.tensor_copy(identb[:, :], ident[:, :]).then_inc(consts, 1)
            pool.wait_ge(loaded, 16 * N_LOADS)
            g.memset(w1row[:, HID:HID + 1], 0.0)
            heads = [ident[0:9 * TPS, k * 3 * TPS:(k + 1) * 3 * TPS] for k in range(3)]
            flat = row_of[:, :, :].rearrange("p j t -> p (j t)")
            g.tensor_tensor(flat, heads[0], heads[1], ALU.add)
            pool.drain()
            g.tensor_tensor(flat, flat, heads[2], ALU.add)
            for j in range(3):
                g.tensor_copy(w1parts[:, j, :], w1row[:, :])
                pool.drain()
                if j < 2:
                    g.tensor_tensor(w1row[:, :], w1row[:, :], w1parts[:, j, :], ALU.subtract)
                    pool.drain()
            for j in range(3):
                last = g.tensor_tensor(w1tmp if j else w1sel[:, :, :],
                                       w1parts[:, j:j + 1, :].to_broadcast([9 * TPS, TPS, HID + 1]),
                                       row_of[:, j, :].rearrange("p (t a) -> p t a", a=1).to_broadcast([9 * TPS, TPS, HID + 1]),
                                       ALU.mult)
                pool.drain()
                if j:
                    last = g.tensor_tensor(w1sel[:, :, :], w1sel[:, :, :], w1tmp, ALU.add)
                    if j < 2:
                        pool.drain()
            last.then_inc(consts, 1)

            def bucket(k, dst, c):
                pool.wait_ge(filled, 16 * FILL_DMAS)
                with pool.Fori(0, RITERS) as i:
                    for s in range(RSLOTS):
                        pool.wait_ge(ring_full[s], i * 32 + (32 * RITERS * k + 32))
                        pool.nop(nofuse=True)
                        pr = payr[:, s, :, :].rearrange("p t c -> p (t c)")
                        for j in range(RING):
                            pool.indirect_dma_start(
                                out=dst, out_offset=bass.IndirectOffsetOnAxis(ap=posr[:, s, j:j + 1], axis=0),
                                in_=pr[:, j * c:(j + 1) * c], in_offset=None).then_inc(ring_sent[s], 16)
                for s in range(RSLOTS):
                    pool.wait_ge(ring_sent[s], sorted_dmas * RITERS * (k + 1))
                pool.sem_inc(bucketed, 1)

            def gather_step(pas, i, s, first):
                pool.wait_ge(pay_in[s], pay_count(pas, i))
                if pas == PASS_MAX and not first:
                    pool.wait_ge(staged_out[s], i * 16)
                pool.nop(nofuse=True)
                for t in range(TPS):
                    pool.indirect_dma_start(
                        out=gatv(s, GC[pas])[:, t, :], out_offset=None, in_=TAB[pas],
                        in_offset=bass.IndirectOffsetOnAxis(ap=payv(s, pas)[:, t, 1:2].bitcast(I32), axis=0),
                    ).then_inc(gat_in[pas][s], 16)

            def gather(pas):
                for s in range(SLOTS):
                    gather_step(pas, 0, s, True)
                with pool.Fori(1, ITERS) as i:
                    for s in range(SLOTS):
                        gather_step(pas, i, s, False)

            def r_(b, lo):
                return rx[:, b, :, lo:lo + 3].rearrange("p t (o a) -> p t o a", a=1).to_broadcast([P, TPS, 3, 8])

            tA, tB, tC = [t[:, :, :].rearrange("p t (o v) -> p t o v", o=3) for t in (tmpA, tmpB, tmpC)]

            def geometry(n, s, stage, first=False):
                b = s % 2
                if stage == 0:
                    if not first:
                        pool.wait_ge(geo_ops, n * GEO_OPS)
                    pool.wait_ge(geo_ready, n + 1)
                    pool.nop(nofuse=True)
                    g.tensor_tensor(tA, fT[:, b, :, 2:5, :], r_(b, 1), ALU.mult).then_inc(geo_ops, 1)
                    g.tensor_tensor(tB, fT[:, b, :, 1:4, :], r_(b, 2), ALU.mult).then_inc(geo_ops, 1)
                    g.tensor_tensor(tC, fT[:, b, :, 0:3, :], r_(b, 0), ALU.mult).then_inc(geo_ops, 1)
                elif stage == 1:
                    pool.wait_ge(geo_ops, n * GEO_OPS + 3)
                    pool.nop(nofuse=True)
                    g.tensor_tensor(g_v[:, b, :, :, 8:16], tA, tB, ALU.subtract).then_inc(geo_ops, 1)
                    g.tensor_tensor(g_s[:, b, :, 8:16], tC[:, :, 0, :], tC[:, :, 1, :], ALU.add).then_inc(geo_ops, 1)
                elif stage == 2:
                    pool.wait_ge(geo_ops, n * GEO_OPS + 5)
                    pool.nop(nofuse=True)
                    g.tensor_tensor(g_s[:, b, :, 8:16], g_s[:, b, :, 8:16], tC[:, :, 2, :], ALU.add).then_inc(geo_ops, 1)

            def split(n, s, stage, first=False):
                b = s % 2
                ew = payv(s, PASS_L2)[:, :, 2]
                part = [wparts[:, b, 3 * k:3 * k + 3, :] for k in range(3)]

                def thrice(t):
                    return t.rearrange("p (a t) -> p a t", a=1).to_broadcast([P, 3, TPS])

                if stage == 0:
                    if not first:
                        pool.wait_ge(dT_raw, n - 1)
                    pool.nop(nofuse=True)
                    g.tensor_copy(part[0], thrice(ew)).then_inc(split_ops, 1)
                else:
                    pool.wait_ge(split_ops, n * SPLIT_OPS + stage)
                    pool.nop(nofuse=True)
                    if stage == 1:
                        last = g.tensor_tensor(wrest[:, :], ew, wparts[:, b, 0, :], ALU.subtract)
                    elif stage == 2:
                        last = g.tensor_copy(part[1], thrice(wrest[:, :]))
                    else:
                        last = g.tensor_tensor(part[2], thrice(wrest[:, :]), wparts[:, b, 3:6, :], ALU.subtract)
                    last.then_inc(split_ops, 1)

            def radial_gather():
                def step(i, s, gathers, geo):
                    n = i * SLOTS + s
                    s1, s2 = (s + 1) % SLOTS, (s + 2) % SLOTS
                    if gathers:
                        gather_step(PASS_L2, i + (s + 2) // SLOTS, s2, False)
                    for stage in range(4):
                        if geo:
                            geometry(n + 1, s1, stage)
                        if gathers:
                            split(n + 2, s2, stage)

                for s in range(2):
                    gather_step(PASS_L2, 0, s, True)
                    for stage in range(4):
                        split(s, s, stage, first=True)
                for stage in range(3):
                    geometry(0, 0, stage, first=True)
                with pool.Fori(0, ITERS - 1) as i:
                    for s in range(SLOTS):
                        step(i, s, True, True)
                for s in range(SLOTS):
                    step(ITERS - 1, s, s < SLOTS - 2, s < SLOTS - 1)

            bucket(0, by_src, 2)
            pool.wait_ge(tab_sent, 16)
            gather(PASS_MAX)
            bucket(1, by_dst, 6)
            for k, pas in enumerate(GATHERS[1:]):
                pool.wait_ge(tab_sent, 16 * (k + 2))
                if pas == PASS_L2:
                    radial_gather()
                else:
                    gather(pas)

        @block.scalar
        def _(act):
            s_ = nc.scalar
            roots = [0]

            def root(dst, src):
                roots[0] += 1
                act.wait_ge(sq_in, roots[0])
                s_.activation(dst, src, ACT.Sqrt).then_inc(sq_out, 1)

            act.sem_inc(step_done, SLOTS)

            def send_rows(k, rows, parts):
                for part in parts:
                    lo, hi = ROW_PARTS[part]
                    cols = slice(TE * lo // 25, TE * hi // 25)
                    act.wait_ge(ranked, RP * k + part + 1)
                    act.dma_start(rows.rearrange("(p t) c -> p (t c)", p=P)[:, cols],
                                  pos[:, cols].bitcast(I32)).then_inc(rows_sent[part], 16)

            send_rows(0, rows_src, range(RP))
            for h in range(HEADS):
                act.wait_ge(whr_used, h + 1)
                act.dma_start(whr, a["L0_gnn_w"][h:h + 1, :, :].to_broadcast([P, F, F])).then_inc(whr_in, 16)
            attr_v = a["edge_attr_3"].rearrange("(p t) c -> p t c", p=P)
            w_v = a["edge_weight"].rearrange("(p t) -> p t", p=P)
            for k in range(PARTS):
                cols = slice(k * CHUNK, (k + 1) * CHUNK)
                if k:
                    act.wait_ge(chunk_made, k)
                act.dma_start(ch_attr, attr_v[:, cols, :]).then_inc(chunk_in, 16)
                act.dma_start(ch_w, w_v[:, cols]).then_inc(chunk_in, 16)
                root(ch_len, ch_sq)
                act.wait_ge(chunk_made, k + 1)
                act.dma_start(edges_dst.rearrange("(p t) c -> p t c", p=P)[:, cols, :], ch_pay).then_inc(chunk_sent, 16)

            send_rows(1, rows_dst, range(RP - LATE))
            with act.Fori(0, ITERS) as i:
                for s in range(SLOTS):
                    n = i * SLOTS + s
                    act.wait_ge(gat_in[PASS_MAX][s], gat_count(PASS_MAX, i))
                    act.dma_start(staged_v[:, bass.ds(i * (SLOTS * TPS) + s * TPS, TPS), :],
                                  gat[:, s, :, :]).then_inc(staged_out[s], 16)
                    act.wait_ge(step_done, n + (PASS_MAX * STEPS + SLOTS - 1))
                    act.wait_ge(tp_done, n + 1)
                    s_.copy(adT[:, s % 2, :], bank[6][0:96, 0:64].bitcast(BF16))
                    s_.copy(hotT[:, s % 2, :, :].rearrange("p t n -> p (t n)"),
                            bank[4].bitcast(BF16)).then_inc(hotT_ready, 1)
            for s in range(SLOTS):
                act.wait_ge(staged_out[s], 16 * ITERS)

            send_rows(1, rows_dst, range(RP - LATE, RP))

            def attention_loads(i, s):
                tiles = bass.ds(i * (SLOTS * TPS) + s * TPS, TPS)
                act.wait_ge(step_done, i * SLOTS + (PASS_ATT * STEPS + s + 1))
                act.dma_start(payv(s, PASS_ATT), by_src_v[:, tiles, :]).then_inc(pay_in[s], 16)
                act.dma_start(gat[:, s, :, :], staged_v[:, tiles, :]).then_inc(att_in[s], 16)

            def attention_transposes(n, s):
                act.wait_ge(tp_done, n + (STEPS + 1))
                for b in range(2):
                    last = s_.copy(hotT[:, s % 2, 4 * b:4 * b + 4, :].rearrange("p t n -> p (t n)"), bank[4 + b])
                last.then_inc(hotT_ready, 1)

            def attention_step(i, s, final):
                n = i * SLOTS + s
                if not (final and s >= 2):
                    attention_loads(i + (s + 2) // SLOTS, (s + 2) % SLOTS)
                act.wait_ge(logit_ready, n + 1)
                s_.activation(prob[:, :, :], logit[:, :, :], ACT.Exp).then_inc(prob_ready, 1)
                if not (final and s == SLOTS - 1):
                    act.wait_ge(am_ready, n + 1)
                    attention_transposes(n + 1, s + 1)

            attention_loads(0, 0)
            attention_loads(0, 1)
            attention_transposes(0, 0)
            with act.Fori(0, ITERS - 1) as i:
                for s in range(SLOTS):
                    attention_step(i, s, False)
            for s in range(SLOTS):
                attention_step(ITERS - 1, s, True)

            def project(k, m, second):
                with act.Fori(0, BATCHES // 2) as j:
                    for b in range(2):
                        act.wait_ge(yT_raw, j * 2 + (k * BATCHES + b + 1))
                        s_.copy(yT[0:m, b, :, :].rearrange("p w n -> p (w n)"), turned[b][0:m, :]).then_inc(yT_ready, 1)
                    if second:
                        for b in range(2):
                            act.wait_ge(hT_raw, j * 2 + (b + 1))
                            s_.copy(hT[:, b, :, :].rearrange("p w n -> p (w n)"), turned[b][0:H2, :]).then_inc(hT_ready, 1)

            project(0, P, False)
            root(st2[:, :], st2[:, :])
            root(st1[:, :], st1[:, :])
            project(1, F, False)
            root(st2[:, :], st2[:, :])
            def radial_round(i, first):
                for s in range(SLOTS):
                    n = i * SLOTS + s
                    b = s % 2
                    act.wait_ge(dT_raw, n + 1)
                    s_.copy(dT[:, :], bank[7][0:9 * TPS, 0:P // 2].bitcast(BF16)).then_inc(dT_ready, 1)
                    if not first or s >= 2:
                        act.wait_ge(msg_ready, n + (STEPS - 1))
                    act.wait_ge(gat_in[PASS_L2][s], gat_count(PASS_L2, i))
                    fv = gatv(s, F)
                    fv1 = fv[:, :, 8:32].rearrange("p t (v i) -> p t i v", i=3)
                    s_.copy(fT[:, b, :, 0:3, :], fv1)
                    s_.copy(fT[:, b, :, 3:5, :], fv1[:, :, 0:2, :])
                    s_.copy(g_v[:, b, :, :, 0:8], fv1)
                    s_.copy(g_s[:, b, :, 0:8], fv[:, :, 0:8])
                    s_.copy(rx[:, b, :, 0:3], payv(s, PASS_L2)[:, :, 3:6])
                    s_.copy(rx[:, b, :, 3:5], payv(s, PASS_L2)[:, :, 3:5]).then_inc(geo_ready, 1)
                    act.wait_ge(step_done, n + (PASS_L2 * STEPS + SLOTS - 1))
                    act.wait_ge(key_ready, n + 1)
                    s_.copy(keyf[:, :], keyi[:, :]).then_inc(key_read, 1)
                    act.wait_ge(key_read, n + 2)
                    for t in range(TPS):
                        last = s_.activation(hot[:, b, t, :], iota[:, :], ACT.Abs, bias=keyf[:, t:t + 1], scale=-1.0)
                    last.then_inc(key_used, 1)
                    act.wait_ge(key_used, n + 1)
                    s_.activation(hot[:, b, :, :], hot[:, b, :, :], ACT.Relu, bias=ones[:, 0:1], scale=-1.0).then_inc(hot_ready, 1)
                    act.wait_ge(hid_raw, n + 1)
                    for c in range(2):
                        last = s_.activation(hid[:, b, 4 * c:4 * c + 4, :].rearrange("p t n -> p (t n)"),
                                             bank[5 + c][0:HID + 1, :], ACT.Relu, bias=b1col[:, :])
                    last.then_inc(hid_ready, 1)

            radial_round(0, True)
            with act.Fori(1, ITERS) as i:
                radial_round(i, False)
            root(st2[:, :], st2[:, :])
            root(st1[:, :], st1[:, :])
            project(2, F, True)
            root(st2[:, :], st2[:, :])

        @block.tensor
        def _(pe):
            t_ = nc.tensor
            pe.wait_ge(consts, 2)

            def bucket_sums(k):
                pe.wait_ge(histed, k + 1)
                t_.matmul(bank[0][:, 0:W], before[:, :], hist[:, :], start=True, stop=True)
                t_.matmul(bank[0][:, P:P + W], ones[:, :], hist[:, :], start=True, stop=True).then_inc(hsum, 1)
                pe.wait_ge(ended, k + 1)
                t_.transpose(bank[1][0:W, 0:P], ends[:, :], ident[:, :]).then_inc(endedT, 1)
                pe.wait_ge(compared, k + 1)
                q = NG // 4
                for b in range(4):
                    last = t_.matmul(bank[2 + b][0:1, 0:q], ones[0:W, 0:1], gge[0:W, b * q:(b + 1) * q],
                                     start=True, stop=True)
                last.then_inc(counted, 1)

            bucket_sums(0)
            bucket_sums(1)

            def group_sums(hots, rows, c, where):
                for q in range(GPS):
                    for h in range(TILES_PER_GROUP):
                        t = q * TILES_PER_GROUP + h
                        last = t_.matmul(where(q), hots[:, t, :], rows(t), start=(h == 0), stop=(h == TILES_PER_GROUP - 1))
                last.then_inc(sums_ready, 1)

            def max_transposes(n, s):
                pe.wait_ge(split_ready, n + 1)
                pe.nop(nofuse=True)
                t_.transpose(bank[6][0:96, 0:64].bitcast(BF16), adsp[:, s % 2, :, :].rearrange("p k c -> p (k c)"), identb[:, :])
                for t in range(TPS):
                    last = t_.transpose(bank[4][:, 64 * t:64 * t + 64].bitcast(BF16), hotb[s % 2][:, t, :], identb[:, :])
                last.then_inc(tp_done, 1)

            def max_step(i, s, final):
                n = i * SLOTS + s
                pe.wait_ge(hotT_ready, n + 1)
                for q in range(GPS):
                    if q == 2 and not (final and s == SLOTS - 1):
                        max_transposes(n + 1, s + 1)
                    pe.wait_ge(mask_used, n * GPS + (q + 1))
                    for h in range(TILES_PER_GROUP):
                        t = q * TILES_PER_GROUP + h
                        dst = bank[2 * (q % 2) + h]
                        hT_b = hotT[:, s % 2, t:t + 1, :].to_broadcast([P, HEADS, P])
                        t_.matmul(dst.rearrange("p (h e) -> p h e", h=HEADS), far[:, :], hT_b,
                                  start=True, stop=False, skip_group_check=True)
                        for hd in range(HEADS):
                            last = t_.matmul(dst[:, hd * P:(hd + 1) * P], pick[:, t * HEADS + hd, :], adT[:, s % 2, :],
                                             start=False, stop=(hd == HEADS - 1), skip_group_check=True)
                    last.then_inc(mask_ready, 1)

            max_transposes(0, 0)
            with pe.Fori(0, ITERS - 1) as i:
                for s in range(SLOTS):
                    max_step(i, s, False)
            for s in range(SLOTS):
                max_step(ITERS - 1, s, True)

            def att_transposes(n, s):
                pe.wait_ge(hot_ready, n + 1)
                for t in range(TPS):
                    last = t_.transpose(bank[4 + t // 4][:, (t % 4) * P:(t % 4 + 1) * P], hot4[s][:, t, :], ident[:, :])
                last.then_inc(tp_done, 1)

            def att_nodes(n, s):
                wins = group_windows(pe, PE_ENGINE, win_src, n)
                pe.wait_ge(hotT_ready, n + (STEPS + 1))
                flat = nodesp[:, :, :, :].rearrange("p w k c -> p (w k c)")
                for t in range(TPS):
                    last = t_.matmul(bank[6][:, 24 * t:24 * t + 24], hotT[:, s % 2, t, :],
                                     flat[:, bass.ds(wins[t // TILES_PER_GROUP] * 24, 24)], start=True, stop=True)
                last.then_inc(am_ready, 1)

            def att_sums(n, s):
                pe.wait_ge(msg_ready, n + 1)
                group_sums(hot4[s], lambda t: msg[:, t, :], CM, lambda q: bank[q // 2][:, (q % 2) * CM:(q % 2 + 1) * CM])

            def att_step(i, s, first, more):
                n = i * SLOTS + s
                if not first:
                    att_sums(n - 1, (s - 1) % SLOTS)
                if more:
                    att_transposes(n + 1, (s + 1) % SLOTS)
                    att_nodes(n + 1, (s + 1) % SLOTS)

            att_transposes(0, 0)
            att_nodes(0, 0)
            for s in range(SLOTS):
                att_step(0, s, s == 0, True)
            with pe.Fori(1, ITERS - 1) as i:
                for s in range(SLOTS):
                    att_step(i, s, False, True)
            for s in range(SLOTS):
                att_step(ITERS - 1, s, False, s < SLOTS - 1)
            att_sums(STEPS - 1, SLOTS - 1)

            def project(k, m, w_, mo, second):
                with pe.Fori(0, BATCHES // 2) as j:
                    for b in range(2):
                        pe.wait_ge(y_ready, j * 2 + (k * BATCHES + b + 1))
                        pe.nop(nofuse=True)
                        for w in range(PW):
                            last = t_.transpose(turned[b][0:m, w * P:(w + 1) * P], yb[:, b, w, 0:m], ident[:, :])
                        last.then_inc(yT_raw, 1)
                    for b in range(2):
                        pe.wait_ge(yT_ready, j * 2 + (k * BATCHES + b + 1))
                        for w in range(PW):
                            last = t_.matmul(bank[4 + b][:, w * mo:(w + 1) * mo], yT[0:m, b, w, :], w_, start=True, stop=True)
                        last.then_inc(z_ready, 1)
                    if second is not None:
                        for b in range(2):
                            pe.wait_ge(h_ready, j * 2 + (b + 1))
                            pe.nop(nofuse=True)
                            for w in range(PW):
                                last = t_.transpose(turned[b][0:H2, w * P:(w + 1) * P], hb[:, b, w, :], ident[:, :])
                            last.then_inc(hT_raw, 1)
                        for b in range(2):
                            pe.wait_ge(hT_ready, j * 2 + (b + 1))
                            for w in range(PW):
                                last = t_.matmul(bank[6 + b][:, w * F:(w + 1) * F], hT[:, b, w, :], second, start=True, stop=True)
                            last.then_inc(z_ready, 1)

            def spmm(pas, c, hot_base):
                with pe.Fori(0, ITERS) as i:
                    for s in range(SLOTS):
                        pe.wait_ge(hot_ready, i * SLOTS + (hot_base * STEPS + s + 1))
                        pe.wait_ge(gat_in[pas][s], gat_count(pas, i))
                        group_sums(hot[:, s % 2, :, :], lambda t: gatv(s, c)[:, t, :], c, lambda q: bank[s % 2][:, q * c:(q + 1) * c])

            project(0, P, wh[:, :], F, None)
            spmm(PASS_L1, C1, 1)
            project(1, F, w1T[:, :], F, None)
            def weight_rows(n, s):
                pe.wait_ge(split_ops, (n + 1) * SPLIT_OPS)
                pe.nop(nofuse=True)
                t_.transpose(bank[7][0:9 * TPS, 0:P // 2].bitcast(BF16),
                             wparts[:, s % 2, :, :].rearrange("p k t -> p (k t)"), identb[:, :]).then_inc(dT_raw, 1)

            def hidden(n, half):
                pe.wait_ge(dT_ready, n + 1)
                for t in range(4 * half, 4 * half + 4):
                    last = t_.matmul(bank[5 + t // 4][0:HID + 1, (t % 4) * P:(t % 4 + 1) * P],
                                     w1sel[:, t, :], dT[:, :], start=True, stop=True)
                if half:
                    last.then_inc(hid_raw, 1)

            def radial_sums(n, s):
                pe.wait_ge(hot_ready, n + (2 * STEPS + 1))
                pe.wait_ge(msg_ready, n + (STEPS + 1))
                group_sums(hot[:, s % 2, :, :], lambda t: red[:, s % 2, t, :], C2, lambda q: bank[0][:, q * C2:(q + 1) * C2])

            def radial_step(i, s, first, more):
                n = i * SLOTS + s
                for p in range(TPS // 2):
                    if p == 0:
                        pe.wait_ge(hid_ready, n + 1)
                    pe.wait_ge(r_used, n * (TPS // 2) + (p + 1))
                    for h in range(2):
                        last = t_.matmul(bank[1 + 2 * (p % 2) + h][:, 0:384], hid[:, s % 2, 2 * p + h, :], w2p[:, :],
                                         start=True, stop=True)
                    last.then_inc(r_ready, 1)
                    if more and p == 0:
                        weight_rows(n + 1, (s + 1) % SLOTS)
                    if p == 1 and not first:
                        radial_sums(n - 1, (s - 1) % SLOTS)
                    if more and p >= 2:
                        hidden(n + 1, p - 2)

            weight_rows(0, 0)
            hidden(0, 0)
            hidden(0, 1)
            for s in range(SLOTS):
                radial_step(0, s, s == 0, True)
            with pe.Fori(1, ITERS - 1) as i:
                for s in range(SLOTS):
                    radial_step(i, s, False, True)
            for s in range(SLOTS):
                radial_step(ITERS - 1, s, False, s < SLOTS - 1)
            radial_sums(STEPS - 1, SLOTS - 1)
            spmm(PASS_L3A, F, 3)
            project(2, F, g3w1[:, :], H2, g3w2[:, :])
            spmm(PASS_L3B, F, 4)

        @block.vector
        def _(dve):
            v = nc.vector
            tabf = tabx[:, :, :].rearrange("p w c -> p (w c)")

            def tab(c):
                return tabf[:, 0:W * c].rearrange("p (w c) -> p w c", c=c)

            def accv(c):
                return acc[:, 0:W * c].rearrange("p (w c) -> p w c", c=c)

            def each(col, c):
                return col.rearrange("p (w a) -> p w a", a=1).to_broadcast([P, W, c])

            def row(vec, c=F):
                return vec.rearrange("p (a c) -> p a c", a=1).to_broadcast([P, W, c])

            dve.sem_inc(mask_used, 2)
            dve.sem_inc(r_used, 2)
            v.memset(fill[:, :, 0:1].bitcast(I32), PAD_KEY)
            v.memset(fill[:, :, 1:3], 0.0)
            v.memset(fill[:, :, 3:6], 1.0)
            v.memset(fill2[:, :, 0:1].bitcast(I32), PAD_KEY)
            v.memset(fill2[:, :, 1:2], 0.0)
            v.memset(x[:, W - 1, :], 0.0)
            v.memset(mask[:, :], 0.0)
            v.memset(b1col[:, :], 1.0)
            v.memset(mmax[:, :, :], -BIG)
            v.memset(red[:, :, :, :], 1.0)
            v.memset(msg[:, :, CM - 1:CM], 1.0).then_inc(fill_set, 1)
            dve.wait_ge(keys_in, 32)
            v.tensor_copy(pair[:, :, 0].bitcast(I32), srcs[:, :])
            v.tensor_copy(pair[:, :, 1].bitcast(I32), dsts[:, :]).then_inc(pairs_made, 1)
            dve.wait_ge(pairs_sent, 16)
            dve.wait_ge(consts, 1)

            def rank(k, key, win_tab):
                v.tensor_scalar(cum.bitcast(I32), key[:, :], 7, None, ALU.logical_shift_right)
                dve.drain()
                v.tensor_copy(winb, cum.bitcast(I32))
                dve.drain()
                with dve.Fori(0, W) as w:
                    v.tensor_scalar(cum.bitcast(BF16)[:, 0:TE], winb, iota[:, bass.ds(w, 1)], None, ALU.is_equal, ALU.add,
                                    accum_out=hist[:, bass.ds(w, 1)])
                    dve.drain()
                v.tensor_copy(start_[:, :], hist[:, :]).then_inc(histed, 1)
                dve.wait_ge(hsum, k + 1)
                v.tensor_scalar(gcnt[:, :], bank[0][:, P:P + W], float(GROUP - 1), None, ALU.add)
                dve.drain()
                v.tensor_scalar(gcnt[:, :], gcnt[:, :], GROUP.bit_length() - 1, None, ALU.logical_shift_right)
                dve.drain()
                v.tensor_copy(hist[:, :], gcnt[:, :])
                dve.drain()
                v.tensor_tensor_scan(ends[:, :], ones[:, 0:W], hist[:, :], 0.0, ALU.mult, ALU.add)
                dve.drain()
                v.tensor_tensor(start_[:, :], ends[:, :], hist[:, :], ALU.subtract).then_inc(ended, 1)
                dve.drain()
                v.tensor_scalar(start_[:, :], start_[:, :], float(GROUP), None, ALU.mult)
                dve.drain()
                v.tensor_tensor(start_[:, :], start_[:, :], bank[0][:, 0:W], ALU.add)
                dve.wait_ge(endedT, k + 1)
                v.tensor_copy(endT[0:W, :], bank[1][0:W, 0:1])
                dve.drain()
                v.tensor_scalar(gge[0:W, :], giota[0:W, :], endT[0:W, :], None, ALU.is_ge).then_inc(compared, 1)
                dve.wait_ge(counted, k + 1)
                q = NG // 4
                for b in range(4):
                    v.tensor_scalar(win_tab[:, b * q:(b + 1) * q], bank[2 + b][0:1, 0:q], float(W - 1), None, ALU.min)

            def rank_parts(parts):
                for lo, hi in (ROW_PARTS[part] for part in parts):
                    cols = slice(TE * lo // 25, TE * hi // 25)
                    m = TE * (hi - lo) // 25
                    win_, eq_, cum_, pos_ = winb[:, cols], eqm[:, 0:m], cum[:, 0:m], pos[:, cols]
                    tmp_ = cum[:, m:2 * m]
                    with dve.Fori(0, W) as w:
                        v.tensor_scalar(eq_, win_, iota[:, bass.ds(w, 1)], None, ALU.is_equal)
                        dve.drain()
                        v.tensor_tensor_scan(cum_, eq_, eq_, start_[:, bass.ds(w, 1)], ALU.add, ALU.max)
                        dve.drain()
                        v.copy_predicated(pos_, eq_, cum_)
                        v.tensor_copy(start_[:, bass.ds(w, 1)], cum_[:, m - 1:m])
                        dve.drain()
                    v.tensor_scalar(cum_.bitcast(I32), pos_, -1.0, None, ALU.add)
                    dve.drain()
                    v.tensor_scalar(tmp_.bitcast(I32), cum_.bitcast(I32), 7, None, ALU.logical_shift_right)
                    v.tensor_scalar(pos_.bitcast(I32), cum_.bitcast(I32), P - 1, None, ALU.bitwise_and)
                    dve.drain()
                    v.tensor_copy(cum_, pos_.bitcast(I32))
                    dve.drain()
                    v.scalar_tensor_tensor(pos_.bitcast(I32), cum_, float(NT), tmp_.bitcast(I32),
                                           ALU.mult, ALU.add).then_inc(ranked, 1)
                    dve.drain()

            rank(0, srcs, win_src)
            rank_parts(range(RP))

            dve.wait_ge(loaded, 16 * N_LOADS)

            dve.sem_inc(whr_used, 1)
            for h in range(HEADS):
                dve.wait_ge(whr_in, 16 * (h + 1))
                for k in range(2):
                    v.tensor_tensor(vtmp, whr, fcw[:, k * F:(k + 1) * F].rearrange("p (a c) -> p a c", a=1)
                                    .to_broadcast([P, F, F]), ALU.mult)
                    dve.drain()
                    last = v.tensor_reduce(vrow[:, k, h, :], vtmp, AX.X, ALU.add)
                    dve.drain()
                v.tensor_copy(gm[:, 0, 0:1], iota[:, 0:1]).then_inc(whr_used, 1)

            for k in range(PARTS):
                cols = slice(k * CHUNK, (k + 1) * CHUNK)
                dve.wait_ge(chunk_in, 32 * (k + 1))
                if k:
                    dve.wait_ge(chunk_sent, 16 * k)
                v.tensor_copy(ch_pay[:, :, 0].bitcast(I32), dsts[:, cols])
                v.tensor_copy(ch_pay[:, :, 1].bitcast(I32), srcs[:, cols])
                v.tensor_copy(ch_pay[:, :, 2], ch_w)
                v.tensor_tensor(ch_pay[:, :, 3:6], ch_attr, ch_attr, ALU.mult)
                dve.drain()
                v.tensor_reduce(ch_sq, ch_pay[:, :, 3:6], AX.X, ALU.add).then_inc(sq_in, 1)
                dve.wait_ge(sq_out, k + 1)
                v.reciprocal(ch_sq, ch_len)
                dve.drain()
                for c in range(3):
                    v.tensor_tensor(ch_pay[:, :, 3 + c], ch_attr[:, :, (c + 1) % 3], ch_sq, ALU.mult)
                dve.drain()
                v.tensor_copy(gm[:, 0, 0:1], iota[:, 0:1]).then_inc(chunk_made, 1)
            dve.wait_ge(chunk_sent, 16 * PARTS)

            cp = _coupling()
            q_ = w2p[:, 0:256].rearrange("p (u k) -> p u k", k=16)
            ab = w2p[:, 256:384].rearrange("p (u k) -> p u k", k=16)
            blk = [w2raw[:, 64 * b:64 * b + 64].rearrange("p (u v) -> p u v", v=8) for b in range(3)]
            vec = w2raw[:, 192:384].rearrange("p (u v k) -> p u v k", v=8, k=3)
            w2tv = w2t[:, :].rearrange("p (u v) -> p u v", v=8)
            v.tensor_scalar(q_[:, 0:8, 0:8], blk[0], cp["s_f0"], None, ALU.mult)
            v.tensor_scalar(q_[:, 0:8, 8:16], blk[1], cp["s_dot"], None, ALU.mult)
            v.tensor_scalar(q_[:, 8:16, 0:8], blk[2], cp["v_f0"], None, ALU.mult)
            v.tensor_scalar(q_[:, 8:16, 8:16], vec[:, :, :, 2], 3.0 * cp["v_quad"], None, ALU.mult)
            v.tensor_scalar(ab[:, :, 8:16], vec[:, :, :, 1], cp["v_cross"], None, ALU.mult)
            v.tensor_scalar(w2tv, vec[:, :, :, 2], -cp["v_quad"], None, ALU.mult)
            v.tensor_scalar(ab[:, :, 0:8], vec[:, :, :, 0], cp["v_same"], None, ALU.mult)
            dve.drain()
            v.tensor_tensor(ab[:, :, 0:8], ab[:, :, 0:8], w2tv, ALU.add)
            dve.drain()

            t0 = tab(C0)
            sq = acc[:, 0:W * F].rearrange("p (w c) -> p w c", c=F)
            for k in range(2):
                for h in range(HEADS):
                    v.tensor_tensor(sq, x[:, :, :], row(vrow[:, k, h, :]), ALU.mult)
                    dve.drain()
                    dst = asrc[:, :, h] if k == 0 else t0[:, :, F + 1 + h]
                    v.tensor_reduce(dst, sq, AX.X, ALU.add)
                    dve.drain()
            v.tensor_copy(t0[:, :, 0:F], x[:, :, :])
            v.memset(t0[:, :, F:F + 1], 1.0).then_inc(tab_ready, 1)

            for part in range(RP):
                dve.wait_ge(rows_sent[part], 16)
            rank(1, dsts, win_dst)
            rank_parts(range(RP - LATE))

            def windows(win_tab, n):
                return group_windows(dve, DVE_ENGINE, win_tab, n)

            def steps(step):
                with dve.Fori(0, ITERS - 1) as i:
                    for s in range(SLOTS):
                        step(i, s, True)
                for s in range(SLOTS):
                    step(ITERS - 1, s, s < SLOTS - 1)

            def after(i, s):
                return i + (s + 1) // SLOTS, (s + 1) % SLOTS

            def one_hot(s, pas, i, dst, pads=False):
                dve.wait_ge(pay_in[s], pay_count(pas, i))
                key = payv(s, pas)[:, :, 0].bitcast(I32)
                v.tensor_scalar(keyi[:, :], key, KEY_MASK, None, ALU.bitwise_and)
                if pads:
                    v.tensor_scalar(padf[:, :], key, float(PAD_KEY), -BIG, ALU.is_ge, ALU.mult)
                dve.drain()
                v.tensor_copy(keyf[:, :], keyi[:, :])
                dve.drain()
                return v.tensor_tensor(dst, iota[:, :].rearrange("p (a n) -> p a n", a=1).to_broadcast([P, TPS, P]),
                                       keyf[:, :].rearrange("p (t a) -> p t a", a=1).to_broadcast([P, TPS, P]),
                                       ALU.is_equal)

            def add_sums(wins, c, where, order, n, pas):
                dve.drain()
                dve.wait_ge(sums_ready, n + (order * STEPS + 1))
                for q in range(GPS):
                    if q:
                        dve.drain()
                    dst = acc[:, bass.ds(wins[q] * c, c)]
                    last = v.tensor_tensor(dst, dst, where(q), ALU.add)
                last.then_inc(step_done, 1)

            def max_prepare(i, s):
                b = s % 2
                one_hot(s, PASS_MAX, i, hotb[b], pads=True)
                dve.wait_ge(gat_in[PASS_MAX][s], gat_count(PASS_MAX, i))
                v.tensor_tensor(adm[:, :, :], gat[:, s, :, F + 1:C0],
                                padf[:, :].rearrange("p (t a) -> p t a", a=1).to_broadcast([P, TPS, HEADS]), ALU.add)
                dve.drain()
                flat = adm[:, :, :].rearrange("p t h -> p (t h)")
                v.tensor_copy(adsp[:, b, 0, :], flat)
                dve.drain()
                v.tensor_tensor(flat, flat, adsp[:, b, 0, :], ALU.subtract)
                dve.drain()
                v.tensor_copy(adsp[:, b, 1, :], flat)
                dve.drain()
                v.tensor_tensor(adsp[:, b, 2, :], flat, adsp[:, b, 1, :], ALU.subtract).then_inc(split_ready, 1)

            def max_step(i, s, more):
                n = i * SLOTS + s
                wins = windows(win_src, n)
                for q in range(GPS):
                    dve.wait_ge(mask_ready, n * GPS + (q + 1))
                    v.tensor_reduce(gm[:, q, :], banks[:, 2 * (q % 2):2 * (q % 2) + 2, :].rearrange(
                        "p t (h e) -> p h t e", h=HEADS), AX.XY, ALU.max).then_inc(mask_used, 1)
                for q in range(GPS):
                    dve.drain()
                    dst = mmax[:, :, :].rearrange("p w h -> p (w h)")[:, bass.ds(wins[q] * HEADS, HEADS)]
                    last = v.tensor_tensor(dst, dst, gm[:, q, :], ALU.max)
                last.then_inc(step_done, 1)
                if more:
                    max_prepare(i + (s + 2) // SLOTS, (s + 2) % SLOTS)

            max_prepare(0, 0)
            dve.drain()
            max_prepare(0, 1)
            with dve.Fori(0, ITERS - 1) as i:
                for s in range(SLOTS):
                    max_step(i, s, True)
            for s in range(SLOTS):
                max_step(ITERS - 1, s, s < SLOTS - 2)
            dve.drain()
            rank_parts(range(RP - LATE, RP))
            v.tensor_scalar(nodeam[:, :, 0:HEADS], asrc[:, :, :], fcb[:, :], None, ALU.add)
            dve.drain()
            v.tensor_tensor(mmax[:, :, :], mmax[:, :, :], nodeam[:, :, 0:HEADS], ALU.add)
            dve.drain()
            v.scalar_tensor_tensor(nodeam[:, :, HEADS:2 * HEADS], mmax[:, :, :], 0.2, mmax[:, :, :], ALU.mult, ALU.max)
            dve.drain()
            v.tensor_copy(nodesp[:, :, 0, :], nodeam[:, :, :])
            dve.drain()
            v.tensor_tensor(nodeam[:, :, :], nodeam[:, :, :], nodesp[:, :, 0, :], ALU.subtract)
            dve.drain()
            v.tensor_copy(nodesp[:, :, 1, :], nodeam[:, :, :])
            dve.drain()
            v.tensor_tensor(nodesp[:, :, 2, :], nodeam[:, :, :], nodesp[:, :, 1, :], ALU.subtract)
            dve.wait_ge(filled, 16 * FILL_DMAS)
            v.memset(acc[:, :], 0.0)
            dve.drain()

            def att_sums(n, wins):
                add_sums(wins, CM, lambda q: bank[q // 2][:, (q % 2) * CM:(q % 2 + 1) * CM], 0, n, PASS_ATT)

            def att_step(i, s, first, more):
                n = i * SLOTS + s
                if not first:
                    wins = windows(win_src, n - 1)
                dve.wait_ge(am_ready, n + 1)
                v.tensor_reduce(am[:, :, :], bank[6][:, 0:24 * TPS].rearrange("p (t k c) -> p t c k", k=3, c=2 * HEADS),
                                AX.X, ALU.add)
                dve.drain()
                dve.wait_ge(att_in[s], i * 16 + 16)
                v.tensor_tensor(logit[:, :, :], am[:, :, 0:HEADS], gat[:, s, :, F + 1:C0], ALU.add)
                dve.drain()
                v.scalar_tensor_tensor(logit[:, :, :], logit[:, :, :], 0.2, logit[:, :, :], ALU.mult, ALU.max)
                dve.drain()
                v.tensor_tensor(logit[:, :, :], logit[:, :, :], am[:, :, HEADS:2 * HEADS], ALU.subtract)
                dve.drain()
                v.tensor_scalar(logit[:, :, :], logit[:, :, :], 0.0, None, ALU.min).then_inc(logit_ready, 1)
                if more:
                    i1, s1 = after(i, s)
                    one_hot(s1, PASS_ATT, i1, hot4[s1]).then_inc(hot_ready, 1)
                if not first:
                    att_sums(n - 1, wins)
                dve.wait_ge(prob_ready, n + 1)
                v.tensor_tensor(msg[:, :, 0:CM - 1].rearrange("p t (h c) -> p t h c", h=HEADS),
                                gat[:, s, :, 0:F + 1].rearrange("p t (a c) -> p t a c", a=1).to_broadcast([P, TPS, HEADS, F + 1]),
                                prob[:, :, :].rearrange("p t (h a) -> p t h a", a=1).to_broadcast([P, TPS, HEADS, F + 1]),
                                ALU.mult).then_inc(msg_ready, 1)

            one_hot(0, PASS_ATT, 0, hot4[0]).then_inc(hot_ready, 1)
            for s in range(SLOTS):
                att_step(0, s, s == 0, True)
            with dve.Fori(1, ITERS - 1) as i:
                for s in range(SLOTS):
                    att_step(i, s, False, True)
            for s in range(SLOTS):
                att_step(ITERS - 1, s, False, s < SLOTS - 1)
            att_sums(STEPS - 1, windows(win_src, STEPS - 1))
            dve.drain()

            def spmm(pas, c, order, win_tab):
                def step(i, s, more):
                    n = i * SLOTS + s
                    wins = windows(win_tab, n)
                    if more:
                        i1, s1 = after(i, s)
                        one_hot(s1, pas, i1, hot[:, s1 % 2, :, :]).then_inc(hot_ready, 1)
                    add_sums(wins, c, lambda q: bank[s % 2][:, q * c:(q + 1) * c], order, n, pas)

                one_hot(0, pas, 0, hot[:, 0, :, :]).then_inc(hot_ready, 1)
                steps(step)
                dve.drain()

            def project(k, make_y, take_z, take_h=None):
                zs = BATCHES * k
                with dve.Fori(0, BATCHES // 2) as j:
                    for b in range(2):
                        make_y(j * (2 * PW) + b * PW, b).then_inc(y_ready, 1)
                    if take_h:
                        for b in range(2):
                            dve.wait_ge(z_ready, j * 4 + (zs + b + 1))
                            take_h(b).then_inc(h_ready, 1)
                        for b in range(2):
                            dve.wait_ge(z_ready, j * 4 + (zs + b + 3))
                            take_z(j * (2 * PW) + b * PW, b)
                    else:
                        for b in range(2):
                            dve.wait_ge(z_ready, j * 2 + (zs + b + 1))
                            take_z(j * (2 * PW) + b * PW, b)
                dve.drain()

            def batch(flat, w, c):
                return flat[:, bass.ds(w * c, PW * c)]

            def per_window(col, w):
                return batch(col, w, 1).rearrange("p (w a) -> p w a", a=1).to_broadcast([P, PW, F])

            roots = [PARTS]

            def root_of(last):
                last.then_inc(sq_in, 1)
                roots[0] += 1
                dve.wait_ge(sq_out, roots[0])

            def layernorm():
                t = tab(F)
                v.tensor_reduce(st1[:, :], x[:, :, :], AX.X, ALU.add)
                dve.drain()
                v.tensor_scalar(st1[:, :], st1[:, :], 1.0 / F, None, ALU.mult)
                dve.drain()
                v.tensor_tensor(x[:, :, :], x[:, :, :], each(st1[:, :], F), ALU.subtract)
                dve.drain()
                v.tensor_tensor(t, x[:, :, :], x[:, :, :], ALU.mult)
                dve.drain()
                v.tensor_reduce(st2[:, :], t, AX.X, ALU.add)
                dve.drain()
                root_of(v.tensor_scalar(st2[:, :], st2[:, :], 1.0 / F, EPS, ALU.mult, ALU.add))
                v.reciprocal(st2[:, :], st2[:, :])
                dve.drain()
                v.tensor_tensor(x[:, :, :], x[:, :, :], each(st2[:, :], F), ALU.mult)
                dve.drain()

            a0 = accv(CM)
            sums = a0[:, :, 0:CM - 1].rearrange("p w (h c) -> p w h c", h=HEADS)[:, :, :, F]
            v.tensor_scalar(asrc[:, :, :], sums, 0.0, None, ALU.is_equal)
            dve.drain()
            v.tensor_tensor(asrc[:, :, :], asrc[:, :, :], sums, ALU.add)
            dve.drain()
            v.reciprocal(asrc[:, :, :], asrc[:, :, :])
            v.tensor_copy(dis[:, :], a0[:, :, CM - 1])
            dve.drain()

            def y0(w, b):
                return v.tensor_tensor(
                    yb[:, b, :, :].rearrange("p w (h c) -> p w h c", h=HEADS),
                    batch(acc, w, CM).rearrange("p (w c) -> p w c", c=CM)[:, :, 0:CM - 1]
                    .rearrange("p w (h c) -> p w h c", h=HEADS)[:, :, :, 0:F],
                    batch(asrc[:, :, :].rearrange("p w h -> p (w h)"), w, HEADS)
                    .rearrange("p (w h a) -> p w h a", h=HEADS, a=1).to_broadcast([P, PW, HEADS, F]), ALU.mult)

            def xw(w):
                return batch(x[:, :, :].rearrange("p w c -> p (w c)"), w, F)

            def z0(w, b):
                return v.scalar_tensor_tensor(xw(w), bank[4 + b][:, 0:PW * F], 1.0 / HEADS, xw(w), ALU.mult, ALU.add)

            project(0, y0, z0)
            v.tensor_tensor(x[:, :, :], x[:, :, :], row(bias0[:, :]), ALU.add)
            dve.wait_ge(tab_sent, 16)
            dve.drain()
            layernorm()

            v.tensor_scalar(dinv[:, :], dis[:, :], 0.0, None, ALU.is_gt)
            root_of(v.tensor_scalar(st1[:, :], dis[:, :], 1.0, None, ALU.max))
            v.reciprocal(st1[:, :], st1[:, :])
            dve.drain()
            v.tensor_tensor(dis[:, :], st1[:, :], dinv[:, :], ALU.mult)
            dve.drain()
            t1 = tab(C1)
            v.tensor_tensor(t1[:, :, F + 1], dis[:, :], mask[:, :], ALU.mult)
            v.tensor_copy(t1[:, :, F], dis[:, :])
            ok = acc[:, 0:W * F // 4].bitcast(U8).rearrange("p (w c) -> p w c", c=F)
            v.tensor_tensor(ok, x[:, :, :], x[:, :, :], ALU.is_equal)
            v.memset(t1[:, :, 0:F], 0.0)
            dve.drain()
            v.copy_predicated(t1[:, :, 0:F], ok, x[:, :, :])
            dve.drain()
            v.tensor_scalar(t1[:, :, 0:F], t1[:, :, 0:F], FMAX, -FMAX, ALU.min, ALU.max)
            dve.drain()
            v.tensor_tensor(t1[:, :, 0:F], t1[:, :, 0:F], t1[:, :, F + 1:F + 2].to_broadcast([P, W, F]),
                            ALU.mult).then_inc(tab_ready, 1)
            dve.drain()
            v.memset(acc[:, 0:W * C1], 0.0)
            dve.drain()
            spmm(PASS_L1, C1, 1, win_src)
            a1 = accv(C1)
            v.tensor_tensor(st2[:, :], dis[:, :], a1[:, :, F + 1], ALU.mult)
            v.tensor_tensor(st1[:, :], dis[:, :], a1[:, :, F], ALU.mult)
            dve.drain()
            v.tensor_scalar(dinv[:, :], st2[:, :], 0.0, None, ALU.is_equal)
            v.tensor_tensor(st1[:, :], st1[:, :], dis[:, :], ALU.mult)
            dve.drain()
            v.tensor_tensor(st2[:, :], st2[:, :], dinv[:, :], ALU.add)
            dve.drain()
            v.reciprocal(st2[:, :], st2[:, :])
            v.tensor_scalar(dinv[:, :], dinv[:, :], -1.0, 1.0, ALU.mult, ALU.add)
            dve.drain()
            v.tensor_tensor(st1[:, :], st1[:, :], st2[:, :], ALU.mult)
            dve.drain()
            v.tensor_tensor(st1[:, :], st1[:, :], dinv[:, :], ALU.mult)
            dve.drain()

            def y1(w, b):
                return v.tensor_tensor(yb[:, b, :, 0:F], batch(acc, w, C1).rearrange("p (w c) -> p w c", c=C1)[:, :, 0:F],
                                       per_window(st1, w), ALU.mult)

            def z1(w, b):
                return v.tensor_tensor(xw(w), bank[4 + b][:, 0:PW * F], xw(w), ALU.add)

            project(1, y1, z1)
            v.tensor_tensor(x[:, :, :], x[:, :, :], row(bias1[:, :]), ALU.add)
            dve.wait_ge(tab_sent, 32)
            dve.drain()
            layernorm()

            v.tensor_copy(tab(F), x[:, :, :]).then_inc(tab_ready, 1)
            v.memset(acc[:, 0:W * C2], 0.0)
            dve.drain()

            def window_keys(i, s):
                dve.wait_ge(key_read, i * SLOTS + (s + 1))
                dve.wait_ge(pay_in[s], pay_count(PASS_L2, i))
                v.tensor_scalar(keyi[:, :], payv(s, PASS_L2)[:, :, 0].bitcast(I32), KEY_MASK, None,
                                ALU.bitwise_and).then_inc(key_ready, 1)

            def radial_sums(n, wins):
                add_sums(wins, C2, lambda q: bank[0][:, q * C2:(q + 1) * C2], 2, n, PASS_L2)

            def radial_step(i, s, first, more):
                n = i * SLOTS + s
                b = s % 2
                if not first:
                    wins = windows(win_dst, n - 1)
                if more:
                    window_keys(*after(i, s))
                dve.wait_ge(geo_ops, (n + 1) * GEO_OPS)
                for p in range(TPS // 2):
                    t0, pb, lo = 2 * p, p % 2, 1 + 2 * (p % 2)
                    dve.wait_ge(r_ready, n * (TPS // 2) + (p + 1))
                    v.tensor_tensor(prod[:, pb, :, 0:16, :],
                                    banks[:, lo:lo + 2, 0:256].rearrange("p t (u k) -> p t u k", k=16),
                                    g_s[:, b, t0:t0 + 2, :].rearrange("p t (a k) -> p t a k", a=1).to_broadcast([P, 2, 16, 16]),
                                    ALU.mult)
                    for h in range(2):
                        last = v.tensor_tensor(
                            prod[:, pb, h, 16:40, :].rearrange("p (u o) k -> p u o k", o=3),
                            bank[lo + h][:, 256:384].rearrange("p (u a k) -> p u a k", a=1, k=16).to_broadcast([P, 8, 3, 16]),
                            g_v[:, b, t0 + h:t0 + h + 1, :, :].to_broadcast([P, 8, 3, 16]), ALU.mult)
                    last.then_inc(r_used, 1)
                    dve.drain()
                    v.tensor_reduce(red[:, b, t0:t0 + 2, 0:40], prod[:, pb, :, :, :], AX.X, ALU.add)
                    if p == 1 and not first:
                        radial_sums(n - 1, wins)
                dve.drain()
                v.tensor_tensor(radial[:, :, :].rearrange("p t (u o) -> p t u o", o=3),
                                rx[:, b, :, 0:3].rearrange("p t (a o) -> p t a o", a=1).to_broadcast([P, TPS, 8, 3]),
                                red[:, b, :, 8:16].rearrange("p t (u a) -> p t u a", a=1).to_broadcast([P, TPS, 8, 3]), ALU.mult)
                dve.drain()
                v.tensor_tensor(red[:, b, :, 16:40], red[:, b, :, 16:40], radial[:, :, :], ALU.add).then_inc(msg_ready, 1)

            dve.sem_inc(key_read, 1)
            window_keys(0, 0)
            for s in range(SLOTS):
                radial_step(0, s, s == 0, True)
            with dve.Fori(1, ITERS - 1) as i:
                for s in range(SLOTS):
                    radial_step(i, s, False, True)
            for s in range(SLOTS):
                radial_step(ITERS - 1, s, False, s < SLOTS - 1)
            radial_sums(STEPS - 1, windows(win_dst, STEPS - 1))
            dve.drain()
            a2 = accv(C2)
            v.tensor_tensor(x[:, :, 0:8], x[:, :, 0:8], a2[:, :, 0:8], ALU.add)
            v.tensor_tensor(x[:, :, 8:F], x[:, :, 8:F], a2[:, :, 16:40], ALU.add)
            v.tensor_copy(dinv[:, :], a2[:, :, 40])
            dve.wait_ge(tab_sent, 48)
            dve.drain()
            layernorm()
            root_of(v.tensor_scalar(st1[:, :], dinv[:, :], 1.0, None, ALU.add))
            v.reciprocal(dinv[:, :], st1[:, :])
            dve.drain()
            v.tensor_tensor(tab(F), x[:, :, :], each(dinv[:, :], F), ALU.mult).then_inc(tab_ready, 1)
            v.memset(acc[:, 0:W * F], 0.0)
            dve.drain()
            spmm(PASS_L3A, F, 3, win_dst)

            v.tensor_tensor(acc[:, 0:W * F], acc[:, 0:W * F], tabf[:, 0:W * F], ALU.add)
            dve.wait_ge(tab_sent, 64)
            dve.drain()

            def y2(w, b):
                return v.tensor_tensor(yb[:, b, :, 0:F], batch(acc, w, F).rearrange("p (w c) -> p w c", c=F),
                                       per_window(dinv, w), ALU.mult)

            def h2(b):
                v.tensor_tensor(hb[:, b, :, :], bank[4 + b][:, 0:PW * H2].rearrange("p (w c) -> p w c", c=H2),
                                g3b1[:, :].rearrange("p (a c) -> p a c", a=1).to_broadcast([P, PW, H2]), ALU.add)
                dve.drain()
                return v.tensor_scalar(hb[:, b, :, :], hb[:, b, :, :], 0.0, None, ALU.max)

            def z2(w, b):
                return v.tensor_tensor(batch(tabf, w, F).rearrange("p (w c) -> p w c", c=F),
                                       bank[6 + b][:, 0:PW * F].rearrange("p (w c) -> p w c", c=F),
                                       per_window(dinv, w), ALU.mult)

            project(2, y2, z2, h2)
            v.memset(acc[:, 0:W * F], 0.0).then_inc(tab_ready, 1)
            dve.drain()
            spmm(PASS_L3B, F, 4, win_dst)
            v.tensor_tensor(acc[:, 0:W * F], acc[:, 0:W * F], tabf[:, 0:W * F], ALU.add)
            dve.drain()
            a3 = accv(F)
            v.tensor_tensor(a3, a3, each(dinv[:, :], F), ALU.mult)
            dve.drain()
            v.tensor_tensor(a3, a3, row(g3b2[:, :]), ALU.add)
            dve.drain()
            v.scalar_tensor_tensor(x[:, :, :], a3, 0.0, x[:, :, :], ALU.max, ALU.add)
            dve.wait_ge(tab_sent, 80)
            dve.drain()
            layernorm()
            v.tensor_copy(gm[:, 0, 0:1], iota[:, 0:1]).then_inc(tab_ready, 1)


_INS = ['x', 'src', 'dst', 'edge_attr_3', 'edge_weight', 'node_vec1', 'L0_gnn_w', 'L0_gnn_fc_w', 'L0_gnn_fc_b',
        'L0_gnn_bias', 'L1_gnn_W', 'L1_gnn_b', 'L2_gnn_w1', 'L2_gnn_b1', 'L2_gnn_w2', 'L2_gnn_b2',
        'L3_gnn_W1', 'L3_gnn_b1', 'L3_gnn_W2', 'L3_gnn_b2']


def kernel(**inputs):
    import numpy as _np
    import concourse.bacc as _bacc
    from concourse import mybir as _mybir
    from concourse.bass_utils import run_bass_kernel_spmd as _run

    nc = _bacc.Bacc("TRN2", target_bir_lowering=False, num_devices=1)
    arrays, args = {}, {}
    for name in _INS:
        arr = _np.asarray(inputs[name])
        key = name
        if name == 'L1_gnn_W':
            arr, key = arr.T, 'L1_WT'
        arr = _np.ascontiguousarray(arr)
        arrays[f"in_{key}"] = arr
        args[key] = nc.dram_tensor(f"in_{key}", arr.shape, _mybir.dt.from_np(arr.dtype), kind="ExternalInput").ap()
    out = nc.dram_tensor("out", (N, F), _mybir.dt.float32, kind="ExternalOutput").ap()
    resnorm_gnn_kernel(nc, args, out)
    r = _run(nc, [arrays], core_ids=[0])
    return r.results[0]["out"]
```
